# Optimizing a Trainium2 kernel written in Bass

```python
import numpy as np
import jax
import jax.numpy as jnp

def _softmax(x, axis=-1):
    return jax.nn.softmax(x, axis=axis)

def _gelu(x):
    return jax.nn.gelu(x, approximate=True)

def _silu(x):
    return jax.nn.silu(x)

def _sigmoid(x):
    return jax.nn.sigmoid(x)

def _layernorm(x, axis=-1, eps=1e-05):
    m = jnp.mean(x, axis=axis, keepdims=True)
    v = jnp.var(x, axis=axis, keepdims=True)
    return (x - m) / jnp.sqrt(v + eps)

def _scatter_add(tgt, idx, src, axis=0):
    return tgt.at[idx].add(src)

def _segment_sum(src, seg, n):
    return jax.ops.segment_sum(src, seg, n)
kernel_name = 'mk_macaron_d4_jaxref_r8_b2e1d4'

def setup_inputs(seed: int=0):
    np.random.seed(seed)
    _w = jnp.asarray

    def _L0_attn_setup():
        import jax, jax.numpy as jnp
        import numpy as np
        D = 128
        H = 16
        KVH = 4
        HD = D // H
        LAT = 32
        WIN = 32
        B, S = (1, 256)
        BASE_G, BASE_L = (1000000.0, 10000.0)
        EPS = 1e-06

        def rmsnorm(x, w):
            return x * jax.lax.rsqrt(jnp.mean(x * x, axis=-1, keepdims=True) + EPS) * w

        def qk_norm(x):
            return x * jax.lax.rsqrt(jnp.mean(x * x, axis=-1, keepdims=True) + EPS)

        def rope(x, base):
            s, hd = (x.shape[-2], x.shape[-1])
            inv_freq = 1.0 / base ** (jnp.arange(0, hd, 2, dtype=jnp.float32) / hd)
            freqs = jnp.arange(s, dtype=jnp.float32)[:, None] * inv_freq[None, :]
            cos, sin = (jnp.cos(freqs), jnp.sin(freqs))
            xe, xo = (x[..., ::2], x[..., 1::2])
            out = jnp.stack([xe * cos - xo * sin, xe * sin + xo * cos], axis=-1)
            return out.reshape(x.shape)

        def split_heads(x, n_heads):
            b, s, _ = x.shape
            return x.reshape(b, s, n_heads, HD).transpose(0, 2, 1, 3)

        def repeat_kv(x):
            return jnp.repeat(x, H // KVH, axis=1)

        def sdpa(q, k, v, mask):
            scores = jnp.einsum('bhqd,bhkd->bhqk', q, k) / np.sqrt(HD).astype(np.float32)
            scores = jnp.where(mask, scores, jnp.float32(-1e+30))
            probs = jax.nn.softmax(scores, axis=-1)
            return jnp.einsum('bhqk,bhkd->bhqd', probs, v)

        def merge_heads(x):
            b, h, s, hd = x.shape
            return x.transpose(0, 2, 1, 3).reshape(b, s, h * hd)

        def global_latent_attn(x, wq, w_kv_down, w_k_up, w_v_up, wo):
            q = split_heads(x @ wq, H)
            latent = x @ w_kv_down
            k = split_heads(latent @ w_k_up, KVH)
            v = split_heads(latent @ w_v_up, KVH)
            q, k = (rope(q, BASE_G), rope(k, BASE_G))
            q, k = (qk_norm(q), qk_norm(k))
            k, v = (repeat_kv(k), repeat_kv(v))
            i = jnp.arange(x.shape[1])
            causal = i[:, None] >= i[None, :]
            return merge_heads(sdpa(q, k, v, causal)) @ wo

        def local_gqa_attn(x, wq, wk, wv, wo):
            q = split_heads(x @ wq, H)
            k = split_heads(x @ wk, KVH)
            v = split_heads(x @ wv, KVH)
            q, k = (rope(q, BASE_L), rope(k, BASE_L))
            q, k = (qk_norm(q), qk_norm(k))
            k, v = (repeat_kv(k), repeat_kv(v))
            i = jnp.arange(x.shape[1])
            diff = i[:, None] - i[None, :]
            mask = (diff >= 0) & (diff < WIN)
            return merge_heads(sdpa(q, k, v, mask)) @ wo
        key = jax.random.key(seed)
        ks = jax.random.split(key, 12)
        std = 0.02
        return {'hidden': jax.random.normal(ks[0], (B, S, D), dtype=jnp.float32), 'norm1_w': jnp.ones((D,), jnp.float32), 'norm2_w': jnp.ones((D,), jnp.float32), 'g_wq': jax.random.normal(ks[1], (D, H * HD), jnp.float32) * std, 'g_kv_down': jax.random.normal(ks[2], (D, LAT), jnp.float32) * std, 'g_k_up': jax.random.normal(ks[3], (LAT, KVH * HD), jnp.float32) * std, 'g_v_up': jax.random.normal(ks[4], (LAT, KVH * HD), jnp.float32) * std, 'g_wo': jax.random.normal(ks[5], (D, D), jnp.float32) * std, 'l_wq': jax.random.normal(ks[6], (D, H * HD), jnp.float32) * std, 'l_wk': jax.random.normal(ks[7], (D, KVH * HD), jnp.float32) * std, 'l_wv': jax.random.normal(ks[8], (D, KVH * HD), jnp.float32) * std, 'l_wo': jax.random.normal(ks[9], (D, D), jnp.float32) * std}
    _L0_attn_in = _L0_attn_setup()

    def _L0_ffn_setup():
        import jax, jax.numpy as jnp
        import numpy as np
        LN_EPS = 1e-05

        def layer_norm(x, g, b):
            mu = jnp.mean(x, axis=-1, keepdims=True)
            var = jnp.mean(jnp.square(x - mu), axis=-1, keepdims=True)
            return (x - mu) * jax.lax.rsqrt(var + LN_EPS) * g + b

        def ternary_quant(w):
            scale = 1.0 / jnp.clip(jnp.mean(jnp.abs(w)), 1e-05)
            wq = jnp.clip(jnp.round(w * scale), -1.0, 1.0) / scale
            return w + jax.lax.stop_gradient(wq - w)
        key = jax.random.key(seed)
        ks = jax.random.split(key, 3)
        dim, hidden = (128, 512)
        B, S = (8, 128)
        x = jax.random.normal(ks[0], (B, S, dim), dtype=jnp.float32)
        w1 = jax.random.normal(ks[1], (hidden, dim), dtype=jnp.float32) * 0.02
        w2 = jax.random.normal(ks[2], (dim, hidden), dtype=jnp.float32) * 0.02
        return {'x': x, 'ln1_g': jnp.ones((dim,), jnp.float32), 'ln1_b': jnp.zeros((dim,), jnp.float32), 'w1': w1, 'b1': jnp.zeros((hidden,), jnp.float32), 'ln2_g': jnp.ones((hidden,), jnp.float32), 'ln2_b': jnp.zeros((hidden,), jnp.float32), 'w2': w2, 'b2': jnp.zeros((dim,), jnp.float32)}
    _L0_ffn_in = _L0_ffn_setup()

    def _L1_attn_setup():
        import jax, jax.numpy as jnp
        import numpy as np
        D_MODEL, D_STATE, D_INNER = (128, 8, int(128 * 1.5))
        LN_EPS = 1e-05

        def layer_norm(x, g, b):
            mu = jnp.mean(x, axis=-1, keepdims=True)
            var = jnp.mean(jnp.square(x - mu), axis=-1, keepdims=True)
            return (x - mu) / jnp.sqrt(var + LN_EPS) * g + b
        key = jax.random.key(seed)
        ks = jax.random.split(key, 8)
        x = jax.random.normal(ks[0], (4, 256, D_MODEL), dtype=jnp.float32)
        W_in = jax.random.normal(ks[1], (2 * D_INNER, D_MODEL), dtype=jnp.float32) * 0.02
        W_out = jax.random.normal(ks[2], (D_MODEL, D_INNER), dtype=jnp.float32) * 0.02
        A_init = jax.random.normal(ks[3], (D_INNER, D_STATE), dtype=jnp.float32) * 0.1
        A_log = jnp.log(jnp.abs(A_init) + 0.1)
        B = jax.random.normal(ks[4], (D_INNER, D_STATE), dtype=jnp.float32) * 0.1
        C = jax.random.normal(ks[5], (D_INNER, D_STATE), dtype=jnp.float32) * 0.01
        ln_in_g = jnp.ones((D_MODEL,), jnp.float32)
        ln_in_b = jnp.zeros((D_MODEL,), jnp.float32)
        ln_out_g = jnp.ones((D_MODEL,), jnp.float32)
        ln_out_b = jnp.zeros((D_MODEL,), jnp.float32)
        return {'x': x, 'W_in': W_in, 'W_out': W_out, 'A_log': A_log, 'B': B, 'C': C, 'ln_in_g': ln_in_g, 'ln_in_b': ln_in_b, 'ln_out_g': ln_out_g, 'ln_out_b': ln_out_b}
    _L1_attn_in = _L1_attn_setup()

    def _L1_ffn_setup():
        import jax, jax.numpy as jnp
        import numpy as np
        HIDDEN_SIZE = 128
        NUM_EXPERTS = 8
        MOE_INTERMEDIATE_SIZE = 176
        NUM_EXPERTS_PER_TOK = 2
        SHARED_EXPERT_INTERMEDIATE_SIZE = 352
        B, T = (2, 128)
        W_SCALE = 0.02
        key = jax.random.key(seed)
        ks = jax.random.split(key, 8)
        H, E, I, SI = (HIDDEN_SIZE, NUM_EXPERTS, MOE_INTERMEDIATE_SIZE, SHARED_EXPERT_INTERMEDIATE_SIZE)
        return {'x': jax.random.normal(ks[0], (B, T, H), jnp.float32), 'gate_w': jax.random.normal(ks[1], (E, H), jnp.float32) * W_SCALE, 'experts_gate_up': jax.random.normal(ks[2], (E, 2 * I, H), jnp.float32) * W_SCALE, 'experts_down': jax.random.normal(ks[3], (E, H, I), jnp.float32) * W_SCALE, 'shared_gate_w': jax.random.normal(ks[4], (SI, H), jnp.float32) * W_SCALE, 'shared_up_w': jax.random.normal(ks[5], (SI, H), jnp.float32) * W_SCALE, 'shared_down_w': jax.random.normal(ks[6], (H, SI), jnp.float32) * W_SCALE, 'shared_expert_gate_w': jax.random.normal(ks[7], (1, H), jnp.float32) * W_SCALE}
    _L1_ffn_in = _L1_ffn_setup()

    def _L2_attn_setup():
        import math
        import jax, jax.numpy as jnp
        import numpy as np
        from jax.scipy.special import xlogy, gammaln

        def get_positional_embed(seq_len, feature_size):
            distances = jnp.arange(-seq_len + 1, seq_len, dtype=jnp.float32)
            n = feature_size // 6
            absd = jnp.abs(distances)[:, None]
            max_range = math.log(seq_len) / math.log(2.0)
            half_life = 2.0 ** jnp.linspace(3.0, max_range, n)
            feat_exp = jnp.exp(-math.log(2.0) / half_life[None, :] * absd)
            center_widths = 2.0 ** jnp.arange(1, n + 1, dtype=jnp.float32) - 1.0
            feat_cm = (center_widths[None, :] > absd).astype(jnp.float32)
            stddev = seq_len / (2.0 * n)
            start_mean = seq_len / n
            mean = jnp.linspace(start_mean, float(seq_len), n)[None, :]
            conc = (mean / stddev) ** 2
            rate = mean / stddev ** 2
            log_unnorm = xlogy(conc - 1.0, absd) - rate * absd
            log_norm = gammaln(conc) - conc * jnp.log(rate)
            probs = jnp.exp(log_unnorm - log_norm) + 1e-08
            feat_gamma = probs / jnp.max(probs, axis=-1, keepdims=True)
            emb = jnp.concatenate([feat_exp, feat_cm, feat_gamma], axis=-1)
            emb = jnp.concatenate([emb, jnp.sign(distances)[:, None] * emb], axis=-1)
            return emb

        def relative_shift(x):
            b, h, t1, t2m1 = x.shape
            x = jnp.pad(x, ((0, 0), (0, 0), (0, 0), (1, 0)))
            t2 = t2m1 + 1
            x = x.reshape(b, h, t2, t1)
            x = x[:, :, 1:, :]
            x = x.reshape(b, h, t1, t2 - 1)
            return x[..., :(t2 + 1) // 2]
        key = jax.random.key(seed)
        ks = jax.random.split(key, 9)
        B, L, D = (2, 128, 128)
        H, Dk, Dv = (8, 128, 128)
        R = 192
        sq = math.sqrt(2.0 / (D + Dk))
        sv = math.sqrt(2.0 / (D + Dv))
        return {'q': jax.random.normal(ks[0], (B, L, D), jnp.float32), 'w_qs': jax.random.normal(ks[1], (D, H * Dk), jnp.float32) * sq, 'w_ks': jax.random.normal(ks[2], (D, H * Dk), jnp.float32) * sq, 'w_vs': jax.random.normal(ks[3], (D, H * Dv), jnp.float32) * sv, 'w_rel_pos_k': jax.random.normal(ks[4], (R, H * Dk), jnp.float32) * 0.05, 'rel_embed_bias': jax.random.normal(ks[5], (1, H, 1, Dk), jnp.float32), 'rel_pos_bias': jax.random.normal(ks[6], (1, H, 1, Dk), jnp.float32), 'w_out': jax.random.normal(ks[7], (H * Dv, D), jnp.float32) * 0.02, 'b_out': jax.random.normal(ks[8], (D,), jnp.float32) * 0.02}
    _L2_attn_in = _L2_attn_setup()

    def _L2_ffn_setup():
        import jax, jax.numpy as jnp
        import numpy as np
        B, T, D, H, E, K = (2, 256, 128, 512, 8, 2)
        EPS = 1e-12

        def moe_forward(x, Wg, bg, W1, b1, W2, b2):
            gates = jax.nn.softmax(x @ Wg + bg, axis=-1)
            _, top_idx = jax.lax.top_k(gates, K)
            mask = jax.nn.one_hot(top_idx, E, dtype=gates.dtype).sum(axis=-2)
            g = gates * mask
            g = g / jnp.maximum(jnp.sum(jnp.abs(g), axis=-1, keepdims=True), EPS)
            h = jnp.einsum('btd,edh->bteh', x, W1) + b1[None, None]
            h = jax.nn.gelu(h, approximate=False)
            eo = jnp.einsum('bteh,ehd->bted', h, W2) + b2[None, None]
            return jnp.einsum('bte,bted->btd', g, eo)
        key = jax.random.key(seed)
        ks = jax.random.split(key, 8)
        s_d = 1.0 / np.sqrt(D)
        s_h = 1.0 / np.sqrt(H)
        return {'x': jax.random.normal(ks[0], (B, T, D), dtype=jnp.float32), 'Wg': jax.random.uniform(ks[1], (D, E), jnp.float32, -s_d, s_d), 'bg': jax.random.uniform(ks[2], (E,), jnp.float32, -s_d, s_d), 'W1': jax.random.uniform(ks[3], (E, D, H), jnp.float32, -s_d, s_d), 'b1': jax.random.uniform(ks[4], (E, H), jnp.float32, -s_d, s_d), 'W2': jax.random.uniform(ks[5], (E, H, D), jnp.float32, -s_h, s_h), 'b2': jax.random.uniform(ks[6], (E, D), jnp.float32, -s_h, s_h)}
    _L2_ffn_in = _L2_ffn_setup()

    def _L3_attn_setup():
        import jax, jax.numpy as jnp
        import numpy as np
        import math
        H = 16
        EPS = 1e-05
        key = jax.random.key(seed)
        ks = jax.random.split(key, 4)
        B, T, D = (2, 256, 128)
        s = 1.0 / math.sqrt(D)
        return {'x': jax.random.normal(ks[0], (B, T, D), dtype=jnp.float32), 'ln_g': jnp.ones((D,), jnp.float32), 'ln_b': jnp.zeros((D,), jnp.float32), 'Wq': jax.random.normal(ks[1], (D, D), jnp.float32) * s, 'bq': jnp.zeros((D,), jnp.float32), 'Wk': jax.random.normal(ks[2], (D, D), jnp.float32) * s, 'bk': jnp.zeros((D,), jnp.float32), 'Wv': jax.random.normal(ks[3], (D, D), jnp.float32) * s, 'bv': jnp.zeros((D,), jnp.float32)}
    _L3_attn_in = _L3_attn_setup()

    def _L3_ffn_setup():
        import jax, jax.numpy as jnp
        import numpy as np
        B, T, C, H, E, K = (4, 128, 128, 128, 8, 2)

        def _swiglu(x):
            a, b = jnp.split(x, 2, axis=-1)
            return jax.nn.silu(a) * b
        key = jax.random.key(seed)
        ks = jax.random.split(key, 6)
        s = 0.02
        x = jax.random.normal(ks[0], (B, T, C), jnp.float32)
        w_shared_in = jax.random.normal(ks[1], (C, 2 * H), jnp.float32) * s
        w_shared_out = jax.random.normal(ks[2], (H, C), jnp.float32) * s
        w1_shared = jax.random.normal(ks[3], (C, 2 * H), jnp.float32) * s
        w2 = jax.random.normal(ks[4], (E, H, C), jnp.float32) * s
        w_gate = jax.random.normal(ks[5], (C, E), jnp.float32) * s
        gate_bias = jnp.zeros((E,), jnp.float32)
        return {'x': x, 'w_shared_in': w_shared_in, 'w_shared_out': w_shared_out, 'w1_shared': w1_shared, 'w2': w2, 'w_gate': w_gate, 'gate_bias': gate_bias}
    _L3_ffn_in = _L3_ffn_setup()
    _d = {'L0_attn_hidden': _L0_attn_in['hidden'], 'L0_attn_norm1_w': _L0_attn_in['norm1_w'], 'L0_attn_norm2_w': _L0_attn_in['norm2_w'], 'L0_attn_g_wq': _L0_attn_in['g_wq'], 'L0_attn_g_kv_down': _L0_attn_in['g_kv_down'], 'L0_attn_g_k_up': _L0_attn_in['g_k_up'], 'L0_attn_g_v_up': _L0_attn_in['g_v_up'], 'L0_attn_g_wo': _L0_attn_in['g_wo'], 'L0_attn_l_wq': _L0_attn_in['l_wq'], 'L0_attn_l_wk': _L0_attn_in['l_wk'], 'L0_attn_l_wv': _L0_attn_in['l_wv'], 'L0_attn_l_wo': _L0_attn_in['l_wo'], 'L0_ffn_ln1_g': _L0_ffn_in['ln1_g'], 'L0_ffn_ln1_b': _L0_ffn_in['ln1_b'], 'L0_ffn_w1': _L0_ffn_in['w1'], 'L0_ffn_b1': _L0_ffn_in['b1'], 'L0_ffn_ln2_g': _L0_ffn_in['ln2_g'], 'L0_ffn_ln2_b': _L0_ffn_in['ln2_b'], 'L0_ffn_w2': _L0_ffn_in['w2'], 'L0_ffn_b2': _L0_ffn_in['b2'], 'L1_attn_W_in': _L1_attn_in['W_in'], 'L1_attn_W_out': _L1_attn_in['W_out'], 'L1_attn_A_log': _L1_attn_in['A_log'], 'L1_attn_B': _L1_attn_in['B'], 'L1_attn_C': _L1_attn_in['C'], 'L1_attn_ln_in_g': _L1_attn_in['ln_in_g'], 'L1_attn_ln_in_b': _L1_attn_in['ln_in_b'], 'L1_attn_ln_out_g': _L1_attn_in['ln_out_g'], 'L1_attn_ln_out_b': _L1_attn_in['ln_out_b'], 'L1_ffn_gate_w': _L1_ffn_in['gate_w'], 'L1_ffn_experts_gate_up': _L1_ffn_in['experts_gate_up'], 'L1_ffn_experts_down': _L1_ffn_in['experts_down'], 'L1_ffn_shared_gate_w': _L1_ffn_in['shared_gate_w'], 'L1_ffn_shared_up_w': _L1_ffn_in['shared_up_w'], 'L1_ffn_shared_down_w': _L1_ffn_in['shared_down_w'], 'L1_ffn_shared_expert_gate_w': _L1_ffn_in['shared_expert_gate_w'], 'L2_attn_w_qs': _L2_attn_in['w_qs'], 'L2_attn_w_ks': _L2_attn_in['w_ks'], 'L2_attn_w_vs': _L2_attn_in['w_vs'], 'L2_attn_w_rel_pos_k': _L2_attn_in['w_rel_pos_k'], 'L2_attn_rel_embed_bias': _L2_attn_in['rel_embed_bias'], 'L2_attn_rel_pos_bias': _L2_attn_in['rel_pos_bias'], 'L2_attn_w_out': _L2_attn_in['w_out'], 'L2_attn_b_out': _L2_attn_in['b_out'], 'L2_ffn_Wg': _L2_ffn_in['Wg'], 'L2_ffn_bg': _L2_ffn_in['bg'], 'L2_ffn_W1': _L2_ffn_in['W1'], 'L2_ffn_b1': _L2_ffn_in['b1'], 'L2_ffn_W2': _L2_ffn_in['W2'], 'L2_ffn_b2': _L2_ffn_in['b2'], 'L3_attn_ln_g': _L3_attn_in['ln_g'], 'L3_attn_ln_b': _L3_attn_in['ln_b'], 'L3_attn_Wq': _L3_attn_in['Wq'], 'L3_attn_bq': _L3_attn_in['bq'], 'L3_attn_Wk': _L3_attn_in['Wk'], 'L3_attn_bk': _L3_attn_in['bk'], 'L3_attn_Wv': _L3_attn_in['Wv'], 'L3_attn_bv': _L3_attn_in['bv'], 'L3_ffn_w_shared_in': _L3_ffn_in['w_shared_in'], 'L3_ffn_w_shared_out': _L3_ffn_in['w_shared_out'], 'L3_ffn_w1_shared': _L3_ffn_in['w1_shared'], 'L3_ffn_w2': _L3_ffn_in['w2'], 'L3_ffn_w_gate': _L3_ffn_in['w_gate'], 'L3_ffn_gate_bias': _L3_ffn_in['gate_bias']}
    _x0 = _d['L0_attn_hidden']
    _d['L0_attn_hidden'] = jax.random.normal(jax.random.fold_in(jax.random.key(seed), 1), (8, 256, 128), dtype=_x0.dtype)
    del _x0
    return _d

def reference(L0_attn_hidden, L0_attn_norm1_w, L0_attn_norm2_w, L0_attn_g_wq, L0_attn_g_kv_down, L0_attn_g_k_up, L0_attn_g_v_up, L0_attn_g_wo, L0_attn_l_wq, L0_attn_l_wk, L0_attn_l_wv, L0_attn_l_wo, L0_ffn_ln1_g, L0_ffn_ln1_b, L0_ffn_w1, L0_ffn_b1, L0_ffn_ln2_g, L0_ffn_ln2_b, L0_ffn_w2, L0_ffn_b2, L1_attn_W_in, L1_attn_W_out, L1_attn_A_log, L1_attn_B, L1_attn_C, L1_attn_ln_in_g, L1_attn_ln_in_b, L1_attn_ln_out_g, L1_attn_ln_out_b, L1_ffn_gate_w, L1_ffn_experts_gate_up, L1_ffn_experts_down, L1_ffn_shared_gate_w, L1_ffn_shared_up_w, L1_ffn_shared_down_w, L1_ffn_shared_expert_gate_w, L2_attn_w_qs, L2_attn_w_ks, L2_attn_w_vs, L2_attn_w_rel_pos_k, L2_attn_rel_embed_bias, L2_attn_rel_pos_bias, L2_attn_w_out, L2_attn_b_out, L2_ffn_Wg, L2_ffn_bg, L2_ffn_W1, L2_ffn_b1, L2_ffn_W2, L2_ffn_b2, L3_attn_ln_g, L3_attn_ln_b, L3_attn_Wq, L3_attn_bq, L3_attn_Wk, L3_attn_bk, L3_attn_Wv, L3_attn_bv, L3_ffn_w_shared_in, L3_ffn_w_shared_out, L3_ffn_w1_shared, L3_ffn_w2, L3_ffn_w_gate, L3_ffn_gate_bias):

    def _L0_attn_ref(hidden, norm1_w, norm2_w, g_wq, g_kv_down, g_k_up, g_v_up, g_wo, l_wq, l_wk, l_wv, l_wo):
        import jax, jax.numpy as jnp
        import numpy as np
        D = 128
        H = 16
        KVH = 4
        HD = D // H
        LAT = 32
        WIN = 32
        B, S = (1, 256)
        BASE_G, BASE_L = (1000000.0, 10000.0)
        EPS = 1e-06

        def rmsnorm(x, w):
            return x * jax.lax.rsqrt(jnp.mean(x * x, axis=-1, keepdims=True) + EPS) * w

        def qk_norm(x):
            return x * jax.lax.rsqrt(jnp.mean(x * x, axis=-1, keepdims=True) + EPS)

        def rope(x, base):
            s, hd = (x.shape[-2], x.shape[-1])
            inv_freq = 1.0 / base ** (jnp.arange(0, hd, 2, dtype=jnp.float32) / hd)
            freqs = jnp.arange(s, dtype=jnp.float32)[:, None] * inv_freq[None, :]
            cos, sin = (jnp.cos(freqs), jnp.sin(freqs))
            xe, xo = (x[..., ::2], x[..., 1::2])
            out = jnp.stack([xe * cos - xo * sin, xe * sin + xo * cos], axis=-1)
            return out.reshape(x.shape)

        def split_heads(x, n_heads):
            b, s, _ = x.shape
            return x.reshape(b, s, n_heads, HD).transpose(0, 2, 1, 3)

        def repeat_kv(x):
            return jnp.repeat(x, H // KVH, axis=1)

        def sdpa(q, k, v, mask):
            scores = jnp.einsum('bhqd,bhkd->bhqk', q, k) / np.sqrt(HD).astype(np.float32)
            scores = jnp.where(mask, scores, jnp.float32(-1e+30))
            probs = jax.nn.softmax(scores, axis=-1)
            return jnp.einsum('bhqk,bhkd->bhqd', probs, v)

        def merge_heads(x):
            b, h, s, hd = x.shape
            return x.transpose(0, 2, 1, 3).reshape(b, s, h * hd)

        def global_latent_attn(x, wq, w_kv_down, w_k_up, w_v_up, wo):
            q = split_heads(x @ wq, H)
            latent = x @ w_kv_down
            k = split_heads(latent @ w_k_up, KVH)
            v = split_heads(latent @ w_v_up, KVH)
            q, k = (rope(q, BASE_G), rope(k, BASE_G))
            q, k = (qk_norm(q), qk_norm(k))
            k, v = (repeat_kv(k), repeat_kv(v))
            i = jnp.arange(x.shape[1])
            causal = i[:, None] >= i[None, :]
            return merge_heads(sdpa(q, k, v, causal)) @ wo

        def local_gqa_attn(x, wq, wk, wv, wo):
            q = split_heads(x @ wq, H)
            k = split_heads(x @ wk, KVH)
            v = split_heads(x @ wv, KVH)
            q, k = (rope(q, BASE_L), rope(k, BASE_L))
            q, k = (qk_norm(q), qk_norm(k))
            k, v = (repeat_kv(k), repeat_kv(v))
            i = jnp.arange(x.shape[1])
            diff = i[:, None] - i[None, :]
            mask = (diff >= 0) & (diff < WIN)
            return merge_heads(sdpa(q, k, v, mask)) @ wo
        x = hidden
        x = x + global_latent_attn(rmsnorm(x, norm1_w), g_wq, g_kv_down, g_k_up, g_v_up, g_wo)
        x = x + local_gqa_attn(rmsnorm(x, norm2_w), l_wq, l_wk, l_wv, l_wo)
        return x

    def _L0_ffn_ref(x, ln1_g, ln1_b, w1, b1, ln2_g, ln2_b, w2, b2):
        import jax, jax.numpy as jnp
        import numpy as np
        LN_EPS = 1e-05

        def layer_norm(x, g, b):
            mu = jnp.mean(x, axis=-1, keepdims=True)
            var = jnp.mean(jnp.square(x - mu), axis=-1, keepdims=True)
            return (x - mu) * jax.lax.rsqrt(var + LN_EPS) * g + b

        def ternary_quant(w):
            scale = 1.0 / jnp.clip(jnp.mean(jnp.abs(w)), 1e-05)
            wq = jnp.clip(jnp.round(w * scale), -1.0, 1.0) / scale
            return w + jax.lax.stop_gradient(wq - w)
        h = layer_norm(x, ln1_g, ln1_b)
        h = jnp.einsum('bsd,hd->bsh', h, ternary_quant(w1)) + b1
        h = jax.nn.gelu(h, approximate=False)
        h = layer_norm(h, ln2_g, ln2_b)
        out = jnp.einsum('bsh,dh->bsd', h, ternary_quant(w2)) + b2
        return out

    def _L1_attn_ref(x, W_in, W_out, A_log, B, C, ln_in_g, ln_in_b, ln_out_g, ln_out_b):
        import jax, jax.numpy as jnp
        import numpy as np
        D_MODEL, D_STATE, D_INNER = (128, 8, int(128 * 1.5))
        LN_EPS = 1e-05

        def layer_norm(x, g, b):
            mu = jnp.mean(x, axis=-1, keepdims=True)
            var = jnp.mean(jnp.square(x - mu), axis=-1, keepdims=True)
            return (x - mu) / jnp.sqrt(var + LN_EPS) * g + b
        Bb, L, D = x.shape
        x_norm = layer_norm(x, ln_in_g, ln_in_b)
        x_proj = jnp.clip(x_norm @ W_in.T, -5.0, 5.0)
        x_ssm, gate = jnp.split(x_proj, 2, axis=-1)
        A = jnp.clip(-jnp.exp(jnp.clip(A_log, -5.0, 0.0)), -2.0, -0.01)
        decay = A * 0.9

        def step(h, x_t):
            h = h * decay + x_t[:, :, None] * B[None] * 0.1
            h = jnp.clip(h, -5.0, 5.0)
            y = jnp.clip(jnp.einsum('bid,id->bi', h, C), -5.0, 5.0)
            return (h, y)
        h0 = jnp.zeros((Bb, D_INNER, D_STATE), x.dtype)
        _, ys = jax.lax.scan(step, h0, jnp.swapaxes(x_ssm, 0, 1))
        out_ssm = jnp.swapaxes(ys, 0, 1)
        out = out_ssm * jnp.tanh(gate) @ W_out.T
        out = jnp.clip(out, -5.0, 5.0)
        return layer_norm(out, ln_out_g, ln_out_b)

    def _L1_ffn_ref(x, gate_w, experts_gate_up, experts_down, shared_gate_w, shared_up_w, shared_down_w, shared_expert_gate_w):
        import jax, jax.numpy as jnp
        import numpy as np
        HIDDEN_SIZE = 128
        NUM_EXPERTS = 8
        MOE_INTERMEDIATE_SIZE = 176
        NUM_EXPERTS_PER_TOK = 2
        SHARED_EXPERT_INTERMEDIATE_SIZE = 352
        B, T = (2, 128)
        W_SCALE = 0.02
        Bx, Tx, H = x.shape
        E = gate_w.shape[0]
        I = experts_down.shape[2]
        x_flat = x.reshape(Bx * Tx, H)
        logits = x_flat @ gate_w.T
        scores = jax.nn.softmax(logits, axis=-1)
        _, topk_ids = jax.lax.top_k(scores, NUM_EXPERTS_PER_TOK)
        in_topk = jax.nn.one_hot(topk_ids, E, dtype=x.dtype).sum(axis=1)
        w = scores * in_topk
        gu = jnp.einsum('nh,eih->nei', x_flat, experts_gate_up)
        g, u = (gu[..., :I], gu[..., I:])
        h = jax.nn.silu(g) * u
        expert_out = jnp.einsum('nei,ehi->neh', h, experts_down)
        out = jnp.einsum('neh,ne->nh', expert_out, w)
        shared = jax.nn.silu(x_flat @ shared_gate_w.T) * (x_flat @ shared_up_w.T) @ shared_down_w.T
        shared_weight = jax.nn.sigmoid(x_flat @ shared_expert_gate_w.T)
        out = out + shared_weight * shared
        return out.reshape(Bx, Tx, H)

    def _L2_attn_ref(q, w_qs, w_ks, w_vs, w_rel_pos_k, rel_embed_bias, rel_pos_bias, w_out, b_out):
        import math
        import jax, jax.numpy as jnp
        import numpy as np
        from jax.scipy.special import xlogy, gammaln

        def get_positional_embed(seq_len, feature_size):
            distances = jnp.arange(-seq_len + 1, seq_len, dtype=jnp.float32)
            n = feature_size // 6
            absd = jnp.abs(distances)[:, None]
            max_range = math.log(seq_len) / math.log(2.0)
            half_life = 2.0 ** jnp.linspace(3.0, max_range, n)
            feat_exp = jnp.exp(-math.log(2.0) / half_life[None, :] * absd)
            center_widths = 2.0 ** jnp.arange(1, n + 1, dtype=jnp.float32) - 1.0
            feat_cm = (center_widths[None, :] > absd).astype(jnp.float32)
            stddev = seq_len / (2.0 * n)
            start_mean = seq_len / n
            mean = jnp.linspace(start_mean, float(seq_len), n)[None, :]
            conc = (mean / stddev) ** 2
            rate = mean / stddev ** 2
            log_unnorm = xlogy(conc - 1.0, absd) - rate * absd
            log_norm = gammaln(conc) - conc * jnp.log(rate)
            probs = jnp.exp(log_unnorm - log_norm) + 1e-08
            feat_gamma = probs / jnp.max(probs, axis=-1, keepdims=True)
            emb = jnp.concatenate([feat_exp, feat_cm, feat_gamma], axis=-1)
            emb = jnp.concatenate([emb, jnp.sign(distances)[:, None] * emb], axis=-1)
            return emb

        def relative_shift(x):
            b, h, t1, t2m1 = x.shape
            x = jnp.pad(x, ((0, 0), (0, 0), (0, 0), (1, 0)))
            t2 = t2m1 + 1
            x = x.reshape(b, h, t2, t1)
            x = x[:, :, 1:, :]
            x = x.reshape(b, h, t1, t2 - 1)
            return x[..., :(t2 + 1) // 2]
        B, L, _ = q.shape
        H, Dk = (rel_embed_bias.shape[1], rel_embed_bias.shape[3])
        Dv = w_vs.shape[1] // H
        scale = Dk ** (-0.5)
        Q = (q @ w_qs).reshape(B, L, H, Dk).transpose(0, 2, 1, 3) * scale
        K = (q @ w_ks).reshape(B, L, H, Dk).transpose(0, 2, 1, 3)
        V = (q @ w_vs).reshape(B, L, H, Dv).transpose(0, 2, 1, 3)
        attn = jnp.einsum('bnqd,bnkd->bnqk', Q + rel_embed_bias, K)
        positions = get_positional_embed(L, w_rel_pos_k.shape[0])
        rel_k = (positions @ w_rel_pos_k).reshape(-1, H, Dk).transpose(1, 0, 2)
        attn_pos = jnp.einsum('bnqd,nkd->bnqk', Q + rel_pos_bias, rel_k)
        attn_pos = relative_shift(attn_pos)
        a = jax.nn.softmax(attn + attn_pos, axis=-1)
        out = jnp.einsum('bnqk,bnkd->bnqd', a, V)
        out = out.transpose(0, 2, 1, 3).reshape(B, L, H * Dv)
        return out @ w_out + b_out

    def _L2_ffn_ref(x, Wg, bg, W1, b1, W2, b2):
        import jax, jax.numpy as jnp
        import numpy as np
        B, T, D, H, E, K = (2, 256, 128, 512, 8, 2)
        EPS = 1e-12

        def moe_forward(x, Wg, bg, W1, b1, W2, b2):
            gates = jax.nn.softmax(x @ Wg + bg, axis=-1)
            _, top_idx = jax.lax.top_k(gates, K)
            mask = jax.nn.one_hot(top_idx, E, dtype=gates.dtype).sum(axis=-2)
            g = gates * mask
            g = g / jnp.maximum(jnp.sum(jnp.abs(g), axis=-1, keepdims=True), EPS)
            h = jnp.einsum('btd,edh->bteh', x, W1) + b1[None, None]
            h = jax.nn.gelu(h, approximate=False)
            eo = jnp.einsum('bteh,ehd->bted', h, W2) + b2[None, None]
            return jnp.einsum('bte,bted->btd', g, eo)
        return moe_forward(x, Wg, bg, W1, b1, W2, b2)

    def _L3_attn_ref(x, ln_g, ln_b, Wq, bq, Wk, bk, Wv, bv):
        import jax, jax.numpy as jnp
        import numpy as np
        import math
        H = 16
        EPS = 1e-05
        B, T, D = x.shape
        mu = jnp.mean(x, axis=-1, keepdims=True)
        var = jnp.mean(jnp.square(x - mu), axis=-1, keepdims=True)
        xn = (x - mu) * jax.lax.rsqrt(var + EPS) * ln_g + ln_b
        q = (xn @ Wq + bq).reshape(B, T, H, D // H)
        k = (xn @ Wk + bk).reshape(B, T, H, D // H)
        v = (xn @ Wv + bv).reshape(B, T, H, D // H)
        scale = 1.0 / math.sqrt(D // H)
        attn = jnp.einsum('bnhd,bmhd->bnmh', q, k) * scale
        w = jax.nn.softmax(attn, axis=2)
        y = jnp.einsum('bnmh,bmhd->bnhd', w, v).reshape(B, T, D)
        return y

    def _L3_ffn_ref(x, w_shared_in, w_shared_out, w1_shared, w2, w_gate, gate_bias):
        import jax, jax.numpy as jnp
        import numpy as np
        B, T, C, H, E, K = (4, 128, 128, 128, 8, 2)

        def _swiglu(x):
            a, b = jnp.split(x, 2, axis=-1)
            return jax.nn.silu(a) * b
        Bx, Tx, Cx = x.shape
        S = Bx * Tx
        fx = x.reshape(S, Cx)
        shared_out = _swiglu(fx @ w_shared_in) @ w_shared_out
        logits = fx @ w_gate + gate_bias
        probs = jax.nn.softmax(logits, axis=-1)
        top_val, top_idx = jax.lax.top_k(probs, K)
        wdense = jnp.zeros((S, E), probs.dtype).at[jnp.arange(S)[:, None], top_idx].add(top_val)
        hid = _swiglu(fx @ w1_shared)
        routed_out = jnp.zeros_like(shared_out)
        for e in range(E):
            routed_out = routed_out + wdense[:, e:e + 1] * (hid @ w2[e])
        return (shared_out + routed_out).reshape(Bx, Tx, Cx)
    x = L0_attn_hidden
    x = x + 0.5 * _L0_ffn_ref(_layernorm(x, axis=-1), L0_ffn_ln1_g, L0_ffn_ln1_b, L0_ffn_w1, L0_ffn_b1, L0_ffn_ln2_g, L0_ffn_ln2_b, L0_ffn_w2, L0_ffn_b2)
    x = x + _L0_attn_ref(_layernorm(x, axis=-1), L0_attn_norm1_w, L0_attn_norm2_w, L0_attn_g_wq, L0_attn_g_kv_down, L0_attn_g_k_up, L0_attn_g_v_up, L0_attn_g_wo, L0_attn_l_wq, L0_attn_l_wk, L0_attn_l_wv, L0_attn_l_wo)
    x = x + 0.5 * _L0_ffn_ref(_layernorm(x, axis=-1), L0_ffn_ln1_g, L0_ffn_ln1_b, L0_ffn_w1, L0_ffn_b1, L0_ffn_ln2_g, L0_ffn_ln2_b, L0_ffn_w2, L0_ffn_b2)
    x = x + 0.5 * _L1_ffn_ref(_layernorm(x, axis=-1), L1_ffn_gate_w, L1_ffn_experts_gate_up, L1_ffn_experts_down, L1_ffn_shared_gate_w, L1_ffn_shared_up_w, L1_ffn_shared_down_w, L1_ffn_shared_expert_gate_w)
    x = x + _L1_attn_ref(_layernorm(x, axis=-1), L1_attn_W_in, L1_attn_W_out, L1_attn_A_log, L1_attn_B, L1_attn_C, L1_attn_ln_in_g, L1_attn_ln_in_b, L1_attn_ln_out_g, L1_attn_ln_out_b)
    x = x + 0.5 * _L1_ffn_ref(_layernorm(x, axis=-1), L1_ffn_gate_w, L1_ffn_experts_gate_up, L1_ffn_experts_down, L1_ffn_shared_gate_w, L1_ffn_shared_up_w, L1_ffn_shared_down_w, L1_ffn_shared_expert_gate_w)
    x = x + 0.5 * _L2_ffn_ref(_layernorm(x, axis=-1), L2_ffn_Wg, L2_ffn_bg, L2_ffn_W1, L2_ffn_b1, L2_ffn_W2, L2_ffn_b2)
    x = x + _L2_attn_ref(_layernorm(x, axis=-1), L2_attn_w_qs, L2_attn_w_ks, L2_attn_w_vs, L2_attn_w_rel_pos_k, L2_attn_rel_embed_bias, L2_attn_rel_pos_bias, L2_attn_w_out, L2_attn_b_out)
    x = x + 0.5 * _L2_ffn_ref(_layernorm(x, axis=-1), L2_ffn_Wg, L2_ffn_bg, L2_ffn_W1, L2_ffn_b1, L2_ffn_W2, L2_ffn_b2)
    x = x + 0.5 * _L3_ffn_ref(_layernorm(x, axis=-1), L3_ffn_w_shared_in, L3_ffn_w_shared_out, L3_ffn_w1_shared, L3_ffn_w2, L3_ffn_w_gate, L3_ffn_gate_bias)
    x = x + _L3_attn_ref(_layernorm(x, axis=-1), L3_attn_ln_g, L3_attn_ln_b, L3_attn_Wq, L3_attn_bq, L3_attn_Wk, L3_attn_bk, L3_attn_Wv, L3_attn_bv)
    x = x + 0.5 * _L3_ffn_ref(_layernorm(x, axis=-1), L3_ffn_w_shared_in, L3_ffn_w_shared_out, L3_ffn_w1_shared, L3_ffn_w2, L3_ffn_w_gate, L3_ffn_gate_bias)
    return x

_drawn_inputs = setup_inputs


def setup_inputs(seed=0):
    import zlib

    import numpy as np

    out = dict(_drawn_inputs(seed))
    spreads = {'L0_attn_norm1_w': (1.0, 0.6),
     'L0_attn_norm2_w': (1.0, 0.6),
     'L0_ffn_ln1_g': (1.0, 0.2),
     'L0_ffn_ln1_b': (0.0, 0.34),
     'L0_ffn_b1': (0.0, 0.1),
     'L0_ffn_ln2_g': (1.0, 0.2),
     'L0_ffn_ln2_b': (0.0, 0.318),
     'L0_ffn_b2': (0.0, 0.1),
     'L1_attn_ln_in_g': (1.0, 0.6),
     'L1_attn_ln_in_b': (0.0, 0.8),
     'L1_attn_ln_out_g': (1.0, 0.6),
     'L1_attn_ln_out_b': (0.0, 0.1),
     'L3_attn_ln_g': (1.0, 0.6),
     'L3_attn_ln_b': (0.0, 0.313),
     'L3_attn_bq': (0.0, 2.0),
     'L3_attn_bk': (0.0, 2.0),
     'L3_attn_bv': (0.0, 0.439),
     'L3_ffn_gate_bias': (0.0, 0.8)}
    factors = {'L0_attn_g_wq': 8.0,
     'L0_attn_g_kv_down': 8.0,
     'L0_attn_g_k_up': 8.0,
     'L0_attn_g_v_up': 8.0,
     'L0_attn_g_wo': 8.0,
     'L0_attn_l_wq': 7.311,
     'L0_attn_l_wk': 6.931,
     'L0_attn_l_wv': 5.279,
     'L0_attn_l_wo': 5.443,
     'L1_attn_W_in': 8.0,
     'L1_attn_W_out': 8.0,
     'L1_attn_A_log': 8.0,
     'L1_attn_B': 8.0,
     'L1_attn_C': 8.0,
     'L1_ffn_gate_w': 8.0,
     'L1_ffn_experts_gate_up': 8.0,
     'L1_ffn_experts_down': 8.0,
     'L1_ffn_shared_gate_w': 8.0,
     'L1_ffn_shared_up_w': 8.0,
     'L1_ffn_shared_down_w': 8.0,
     'L1_ffn_shared_expert_gate_w': 8.0,
     'L2_attn_b_out': 5.154,
     'L2_ffn_bg': 4.112,
     'L2_ffn_b1': 7.933,
     'L2_ffn_b2': 5.685,
     'L3_ffn_w_shared_in': 8.0,
     'L3_ffn_w_shared_out': 8.0,
     'L3_ffn_w1_shared': 8.0,
     'L3_ffn_w2': 8.0,
     'L3_ffn_w_gate': 8.0}
    for name, (base, spread) in spreads.items():
        noise = np.random.default_rng([zlib.crc32(name.encode()), seed]).standard_normal(out[name].shape)
        drawn = base * np.exp(spread * noise) if base else spread * noise
        out[name] = jnp.asarray(drawn.astype(out[name].dtype))
    for name, factor in factors.items():
        out[name] = (out[name] * factor).astype(out[name].dtype)
    return out
```

```python
import math
from contextlib import ExitStack

import numpy as np
import concourse.bass as bass
from concourse import mybir

F32 = mybir.dt.float32
ALU = mybir.AluOpType
ACT = mybir.ActivationFunctionType
AX = mybir.AxisListType

P = 128
D = 128
NB = 8
SEQ = 256
PAIR = SEQ // P
NT = NB * PAIR
EPS = 1e-5


class Record:
    pass


def skewed(eng, lead, trail):
    lead(0, 0)
    with eng.Fori(0, NB // 2 - 1) as i:
        lead(1, 2 * i + 1)
        trail(0, 2 * i)
        lead(0, 2 * i + 2)
        trail(1, 2 * i + 1)
    lead(1, NB - 1)
    trail(0, NB - 2)
    trail(1, NB - 1)


SIGNALS_USED = []


def signal(nc, ctx, name):
    s = ctx.enter_context(nc.semaphore(name))
    SIGNALS_USED.append(s.num)
    return s


def clear_signals(nc):
    numbers = sorted(set(SIGNALS_USED))
    SIGNALS_USED.clear()
    runs = []
    for k in numbers:
        if runs and runs[-1][1] == k:
            runs[-1][1] = k + 1
        else:
            runs.append([k, k + 1])
    with nc.Block() as block:
        @block.sync
        def _(sp):
            for low, high in runs:
                sp.sem_clear(range(low, high))


def tile_of(buf, n, t):
    return buf[:, bass.ds(n, 1), t * D:(t + 1) * D].rearrange("p a f -> p (a f)")


def pair_of(buf, n):
    return buf[:, bass.ds(n, 1), :].rearrange("p a f -> p (a f)")


def make_norm(nc, ctx, tag):
    sb = lambda name, shape: ctx.enter_context(nc.sbuf_tensor(f"{tag}_{name}", shape, F32))
    nm = Record()
    nm.stats, nm.mv = sb("stats", [P, PAIR, 6]), sb("mv", [P, PAIR, 2])
    nm.var, nm.inv = sb("var", [P, PAIR]), sb("inv", [P, PAIR])
    nm.var_ready = signal(nc, ctx, f"{tag}_var_ready")
    nm.inv_ready = signal(nc, ctx, f"{tag}_inv_ready")
    return nm


def norm_begin(nc, nm, src, eps=EPS, rms=False):
    for t in range(PAIR):
        nc.vector.bn_stats(nm.stats[:, t, :], src(t))
    nc.vector.drain()
    for t in range(PAIR):
        nc.vector.bn_aggr(nm.mv[:, t, :], nm.stats[:, t, :])
    nc.vector.drain()
    if rms:
        nc.vector.tensor_tensor(nm.var[:, :], nm.mv[:, :, 0], nm.mv[:, :, 0], ALU.mult)
        nc.vector.drain()
        nc.vector.tensor_tensor(nm.var[:, :], nm.var[:, :], nm.mv[:, :, 1], ALU.add)
        nc.vector.drain()
        nc.vector.tensor_scalar(nm.var[:, :], nm.var[:, :], eps, None, ALU.add).then_inc(nm.var_ready, 1)
    else:
        nc.vector.tensor_scalar(nm.var[:, :], nm.mv[:, :, 1], eps, None, ALU.add).then_inc(nm.var_ready, 1)


def norm_end(nc, dve, nm, n, src, dst, rms=False):
    dve.wait_ge(nm.inv_ready, n + 1)
    for t in range(PAIR):
        if rms:
            last = nc.vector.tensor_scalar(dst(t), src(t), nm.inv[:, t:t + 1], None, ALU.mult)
        else:
            last = nc.vector.tensor_scalar(dst(t), src(t), nm.mv[:, t, 0:1], nm.inv[:, t:t + 1],
                                           ALU.subtract, ALU.mult)
    return last


def norm_tokens(nc, dve, nm, n, src, dst, eps=EPS, rms=False):
    norm_begin(nc, nm, src, eps, rms)
    return norm_end(nc, dve, nm, n, src, dst, rms)


def norm_power(nc, pool, m, nm, n):
    pool.wait_ge(nm.var_ready, n + 1)
    nc.gpsimd.tensor_tensor(nm.inv[:, :], nm.var[:, :], m.neg_half[:, 0:PAIR], ALU.pow).then_inc(nm.inv_ready, 1)


def residual_begin(nc, m, nm, n, src, scale):
    nc.vector.scalar_tensor_tensor(out=pair_of(m.X, n), in0=src, scalar=scale, in1=pair_of(m.X, n),
                                   op0=ALU.mult, op1=ALU.add)
    nc.vector.drain()
    norm_begin(nc, nm, lambda t: tile_of(m.X, n, t))


def residual_end(nc, dve, m, nm, n):
    norm_end(nc, dve, nm, n, lambda t: tile_of(m.X, n, t), lambda t: tile_of(m.XN, n, t))


def input_norm(nc, m):
    with ExitStack() as ctx:
        nm = make_norm(nc, ctx, "in")
        block = ctx.enter_context(nc.Block())

        @block.vector
        def _(dve):
            nc.vector.memset(m.gates[:, :, :], 0.0)
            dve.wait_ge(m.loaded["x"], 16)
            with dve.Fori(0, NB) as n:
                norm_tokens(nc, dve, nm, n, lambda t: tile_of(m.X, n, t), lambda t: tile_of(m.XN, n, t))

        @block.gpsimd
        def _(pool):
            pool.wait_ge(m.loaded["const"], m.total["const"])
            with pool.Fori(0, NB) as n:
                norm_power(nc, pool, m, nm, n)


def ternary_weights(nc, m):
    with ExitStack() as ctx:
        sb = lambda name, shape: ctx.enter_context(nc.sbuf_tensor("tq_" + name, shape, F32))
        sem = lambda name: signal(nc, ctx, "tq_" + name)
        part = sb("part", [P, 2])
        scale = sb("scale", [P, 2, 2])
        wq = sb("wq", [P, 512])
        part_ready, total_ready = sem("part_ready"), sem("total_ready")
        total = m.psum[:, 0, 0:2]
        weights = (m.f0_w1, m.f0_w2)
        block = ctx.enter_context(nc.Block())

        @block.vector
        def _(dve):
            dve.wait_ge(m.loaded["f0"], m.total["f0"])
            for j, w in enumerate(weights):
                last = nc.vector.tensor_reduce(part[:, j:j + 1], w[:, :], AX.X, ALU.add, apply_absolute_value=True)
            last.then_inc(part_ready, 1)
            dve.wait_ge(total_ready, 1)
            nc.vector.tensor_scalar(scale[:, 1, :], total, 1.0 / (512 * D), 1e-5, ALU.mult, ALU.max)
            nc.vector.drain()
            nc.vector.reciprocal(scale[:, 0, :], scale[:, 1, :])
            nc.vector.drain()
            nc.vector.reciprocal(scale[:, 1, :], scale[:, 0, :])
            nc.vector.drain()
            for j, w in enumerate(weights):
                nc.vector.tensor_scalar(wq[:, :], w[:, :], scale[:, 0, j:j + 1], 1.0, ALU.mult, ALU.min)
                nc.vector.drain()
                nc.vector.tensor_scalar(wq[:, :], wq[:, :], -1.0, 12582912.0, ALU.max, ALU.add)
                nc.vector.drain()
                nc.vector.tensor_scalar(wq[:, :], wq[:, :], 12582912.0, None, ALU.subtract)
                nc.vector.drain()
                nc.vector.tensor_scalar(wq[:, :], wq[:, :], scale[:, 1, j:j + 1], None, ALU.mult)
                nc.vector.drain()
                nc.vector.tensor_tensor(wq[:, :], wq[:, :], w[:, :], ALU.subtract)
                nc.vector.drain()
                nc.vector.tensor_tensor(w[:, :], wq[:, :], w[:, :], ALU.add)
                nc.vector.drain()

        @block.tensor
        def _(pe):
            pe.wait_ge(m.loaded["const"], m.total["const"])
            pe.wait_ge(part_ready, 1)
            nc.tensor.matmul(total, m.ones[:, :], part[:, :], start=True, stop=True).then_inc(total_ready, 1)


def ffn_ternary(nc, m, tag):
    HID, C = 512, 4
    with ExitStack() as ctx:
        sb = lambda name, shape: ctx.enter_context(nc.sbuf_tensor(f"{tag}_{name}", shape, F32))
        sem = lambda name: signal(nc, ctx, f"{tag}_{name}")
        z = sb("z", [P, 2, PAIR, D])
        hT = sb("hT", [P, 2, PAIR * P])
        hid = sb("hid", [P, 2, PAIR, HID])
        gT = sb("gT", [P, 2, C, PAIR * P])
        yb = sb("yb", [P, PAIR * D])
        zn, gn, xn = (make_norm(nc, ctx, f"{tag}_{k}") for k in ("zn", "gn", "xn"))
        ps_xT = m.psum[:, 0, :].rearrange("p (u f) -> p u f", u=2)
        ps_h = m.psum[:, 1:3, :]
        ps_g = m.psum[:, 3:5, :]
        ps_y = m.psum[:, 5, 0:PAIR * D]
        z_ready, xT_ready, hT_ready, h_ready = sem("z_ready"), sem("xT_ready"), sem("hT_ready"), sem("h_ready")
        hb_ready, g_ready, gn_ready = sem("hb_ready"), sem("g_ready"), sem("gn_ready")
        tr_ready, gT_ready, y_ready, y_used = sem("tr_ready"), sem("gT_ready"), sem("y_ready"), sem("y_used")
        block = ctx.enter_context(nc.Block())

        @block.tensor
        def _(pe):
            def lead(u, n):
                pe.wait_ge(z_ready, n + 1)
                for t in range(PAIR):
                    last = nc.tensor.transpose(ps_xT[:, u, t * P:(t + 1) * P], z[:, u, t, :], m.ident[:, :])
                last.then_inc(xT_ready, 1)
                pe.wait_ge(hT_ready, n + 1)
                for t in range(PAIR):
                    last = nc.tensor.matmul(ps_h[:, t, :], hT[:, u, t * P:(t + 1) * P], m.f0_w1[:, :],
                                            start=True, stop=True)
                last.then_inc(h_ready, 1)

            def trail(u, n):
                pe.wait_ge(gn_ready, n + 1)
                for t in range(PAIR):
                    for c in range(C):
                        last = nc.tensor.transpose(ps_g[:, t, c * P:(c + 1) * P], hid[:, u, t, c * P:(c + 1) * P],
                                                   m.ident[:, :])
                last.then_inc(tr_ready, 1)
                pe.wait_ge(gT_ready, n + 1)
                pe.wait_ge(y_used, n + 1)
                for t in range(PAIR):
                    for c in range(C):
                        last = nc.tensor.matmul(ps_y[:, t * D:(t + 1) * D], gT[:, u, c, t * P:(t + 1) * P],
                                                m.f0_w2[:, c * D:(c + 1) * D], start=(c == 0), stop=(c == C - 1))
                last.then_inc(y_ready, 1)
            skewed(pe, lead, trail)

        @block.scalar
        def _(act):
            nc.scalar.preload_act_table(ACT.Gelu)

            def lead(u, n):
                act.wait_ge(xT_ready, n + 1)
                nc.scalar.activation(hT[:, u, :], ps_xT[:, u, :], ACT.Identity, bias=m.f0_ln1_b[:, 0:1],
                                     scale=m.f0_ln1_g[:, 0:1]).then_inc(hT_ready, 1)
                act.wait_ge(hb_ready, n + 1)
                nc.scalar.activation(hid[:, u, :, :], hid[:, u, :, :], ACT.Gelu).then_inc(g_ready, 1)

            def trail(u, n):
                act.wait_ge(tr_ready, n + 1)
                for c in range(C):
                    last = nc.scalar.activation(gT[:, u, c, :].rearrange("p (t f) -> p t f", t=PAIR),
                                                ps_g[:, :, c * P:(c + 1) * P], ACT.Identity,
                                                bias=m.f0_ln2_b[:, c:c + 1], scale=m.f0_ln2_g[:, c:c + 1])
                last.then_inc(gT_ready, 1)
            skewed(act, lead, trail)

        @block.vector
        def _(dve):
            dve.sem_inc(y_used, 1)

            def lead(u, n):
                norm_tokens(nc, dve, zn, n, lambda t: tile_of(m.XN, n, t), lambda t: z[:, u, t, :]).then_inc(z_ready, 1)
                dve.wait_ge(h_ready, n + 1)
                nc.vector.tensor_tensor(hid[:, u, :, :], ps_h, m.f0_b1[:, :, :], ALU.add).then_inc(hb_ready, 1)
                dve.wait_ge(g_ready, n + 1)
                norm_tokens(nc, dve, gn, n, lambda t: hid[:, u, t, :], lambda t: hid[:, u, t, :]).then_inc(gn_ready, 1)

            def trail(u, n):
                dve.wait_ge(y_ready, n + 1)
                nc.vector.tensor_tensor(yb[:, :], ps_y, m.f0_b2[:, :], ALU.add).then_inc(y_used, 1)
                nc.vector.drain()
                residual_begin(nc, m, xn, n, yb[:, :], 0.5)
                residual_end(nc, dve, m, xn, n)
            skewed(dve, lead, trail)

        @block.gpsimd
        def _(pool):
            def lead(u, n):
                norm_power(nc, pool, m, zn, n)
                norm_power(nc, pool, m, gn, n)
            skewed(pool, lead, lambda u, n: norm_power(nc, pool, m, xn, n))


def route(nc, m, tag, w_gate, group, gate_bias=None, shared_gate=False, renormalise=False, bias2=None):
    E, E1 = 8, 9 if shared_gate else 8
    with ExitStack() as ctx:
        sb = lambda name, shape: ctx.enter_context(nc.sbuf_tensor(f"{tag}_{name}", shape, F32))
        sem = lambda name: signal(nc, ctx, f"{tag}_{name}")
        lg = sb("logits", [P, NT, E1])
        pr = sb("probs", [P, NT, E])
        left = sb("left", [P, NT, E])
        eq = sb("eq", [P, NT, E])
        mask = sb("mask", [P, NT, E])
        col = sb("col", [P, NT])
        gates_T = sb("gates_T", [P, P])
        tr_ready, xT_ready, lg_ready, sub_ready, exp_ready = (sem(k) for k in ("tr_ready", "xT_ready", "lg_ready", "sub_ready", "exp_ready"))
        gates_ready, gtr_ready, gT_ready, acc_ready = (sem(k) for k in ("gates_ready", "gtr_ready", "gT_ready", "acc_ready"))
        ps_lg = m.psum[:, 4, 0:NT * E1].rearrange("p (t e) -> p t e", e=E1)
        ps_gT = m.psum[:, 5, 0:P]
        block = ctx.enter_context(nc.Block())
        wide = lambda v: v.unsqueeze(2).to_broadcast([P, NT, E])

        @block.tensor
        def _(pe):
            for q in range(4):
                for t in range(4):
                    last = nc.tensor.transpose(m.psum[:, q, t * P:(t + 1) * P],
                                               m.XN[:, 2 * q + t // 2, (t % 2) * D:(t % 2 + 1) * D], m.ident[:, :])
                last.then_inc(tr_ready, 1)
            pe.wait_ge(m.loaded[group], m.total[group])
            for q in range(4):
                pe.wait_ge(xT_ready, q + 1)
                for t in range(4 * q, 4 * q + 4):
                    last = nc.tensor.matmul(ps_lg[:, t, :], m.XT[:, t * P:(t + 1) * P], w_gate, start=True, stop=True)
            last.then_inc(lg_ready, 1)
            if bias2 is not None:
                pe.wait_ge(gates_ready, 1)
                nc.tensor.transpose(ps_gT, left[:, :, :].rearrange("p t e -> p (t e)"), m.ident[:, :]).then_inc(gtr_ready, 1)
                pe.wait_ge(gT_ready, 1)
                for q in range(4):
                    last = nc.tensor.matmul(m.psum[:, q, :], gates_T[:, :], m.bias2_of_tile[:, q * 4 * D:(q + 1) * 4 * D],
                                            start=True, stop=True)
                last.then_inc(acc_ready, 1)

        @block.scalar
        def _(act):
            nc.scalar.preload_act_table(ACT.Exp)
            for q in range(4):
                act.wait_ge(tr_ready, q + 1)
                nc.scalar.activation(m.XT[:, q * 512:(q + 1) * 512], m.psum[:, q, :], ACT.Copy).then_inc(xT_ready, 1)
            act.wait_ge(sub_ready, 1)
            if shared_gate:
                nc.scalar.activation(lg[:, :, E], lg[:, :, E], ACT.Exp, scale=-1.0)
            nc.scalar.activation(pr[:, :, :], lg[:, :, 0:E], ACT.Exp).then_inc(exp_ready, 1)
            if bias2 is not None:
                act.wait_ge(gtr_ready, 1)
                nc.scalar.activation(gates_T[:, :], ps_gT, ACT.Copy).then_inc(gT_ready, 1)
                act.wait_ge(acc_ready, 1)
                for q in range(4):
                    nc.scalar.activation(m.acc[:, 2 * q:2 * q + 2, :].rearrange("p n f -> p (n f)"), m.psum[:, q, :], ACT.Copy)

        @block.vector
        def _(dve):
            if bias2 is not None:
                for t in range(NT):
                    nc.vector.tensor_scalar(m.bias2_of_tile[:, t * D:(t + 1) * D], bias2, m.tile_mask[:, t:t + 1], None, ALU.mult)
            dve.wait_ge(m.loaded[group], m.total[group])
            dve.wait_ge(lg_ready, 1)
            if gate_bias is not None:
                nc.vector.tensor_tensor(lg[:, :, :], ps_lg, gate_bias.unsqueeze(1).to_broadcast([P, NT, E1]), ALU.add)
            else:
                nc.vector.tensor_copy(lg[:, :, :], ps_lg)
            nc.vector.drain()
            nc.vector.tensor_reduce(col[:, :], lg[:, :, 0:E], AX.X, ALU.max)
            nc.vector.drain()
            nc.vector.tensor_tensor(lg[:, :, 0:E], lg[:, :, 0:E], wide(col[:, :]), ALU.subtract).then_inc(sub_ready, 1)
            dve.wait_ge(exp_ready, 1)
            nc.vector.tensor_reduce(col[:, :], pr[:, :, :], AX.X, ALU.add)
            if shared_gate:
                nc.vector.tensor_scalar(lg[:, :, E], lg[:, :, E], 1.0, None, ALU.add)
            nc.vector.drain()
            nc.vector.reciprocal(col[:, :], col[:, :])
            if shared_gate:
                nc.vector.reciprocal(m.gates[:, :, E], lg[:, :, E])
            nc.vector.drain()
            nc.vector.tensor_tensor(pr[:, :, :], pr[:, :, :], wide(col[:, :]), ALU.mult)
            nc.vector.drain()
            nc.vector.tensor_copy(left[:, :, :], pr[:, :, :])
            nc.vector.drain()
            for k in range(2):
                nc.vector.tensor_reduce(col[:, :], left[:, :, :], AX.X, ALU.max)
                nc.vector.drain()
                nc.vector.tensor_tensor(eq[:, :, :], left[:, :, :], wide(col[:, :]), ALU.is_equal)
                nc.vector.drain()
                nc.vector.tensor_tensor(eq[:, :, :], eq[:, :, :], m.countdown[:, :].unsqueeze(1).to_broadcast([P, NT, E]), ALU.mult)
                nc.vector.drain()
                nc.vector.tensor_reduce(col[:, :], eq[:, :, :], AX.X, ALU.max)
                nc.vector.drain()
                nc.vector.tensor_tensor(eq[:, :, :], eq[:, :, :], wide(col[:, :]), ALU.is_equal)
                nc.vector.drain()
                if k == 0:
                    nc.vector.tensor_copy(mask[:, :, :], eq[:, :, :])
                    nc.vector.scalar_tensor_tensor(out=left[:, :, :], in0=eq[:, :, :], scalar=-2.0, in1=left[:, :, :],
                                                   op0=ALU.mult, op1=ALU.add)
                else:
                    nc.vector.tensor_tensor(mask[:, :, :], mask[:, :, :], eq[:, :, :], ALU.add)
                nc.vector.drain()
            if renormalise:
                nc.vector.tensor_tensor(pr[:, :, :], pr[:, :, :], mask[:, :, :], ALU.mult)
                nc.vector.drain()
                nc.vector.tensor_reduce(col[:, :], pr[:, :, :], AX.X, ALU.add, apply_absolute_value=True)
                nc.vector.drain()
                nc.vector.tensor_scalar(col[:, :], col[:, :], 1e-12, None, ALU.max)
                nc.vector.drain()
                nc.vector.reciprocal(col[:, :], col[:, :])
                nc.vector.drain()
                nc.vector.tensor_tensor(m.gates[:, :, 0:E], pr[:, :, :], wide(col[:, :]), ALU.mult)
                last = nc.vector.tensor_tensor(left[:, :, :], pr[:, :, :], wide(col[:, :]), ALU.mult)
            else:
                last = nc.vector.tensor_tensor(m.gates[:, :, 0:E], pr[:, :, :], mask[:, :, :], ALU.mult)
            last.then_inc(gates_ready, 1)


def expert_steps(eng, count, step):
    for e in range(count):
        step(0, e, False, False)
    with eng.Fori(1, NB - 1) as n:
        for e in range(count):
            step(n, e, False, True)
    for e in range(count):
        step(NB - 1, e, e == count - 1, True)


def tokens_T(m, n):
    return m.XT[:, bass.ds(n * SEQ, SEQ)]


def gates_of(m, n):
    return m.gates[:, bass.ds(n * PAIR, PAIR), :]


def moe_gated(nc, m, tag):
    route(nc, m, tag + "r", m.m1_gate[:, :], "m1", shared_gate=True)
    S, I2 = 10, 88
    with ExitStack() as ctx:
        sb = lambda name, shape: ctx.enter_context(nc.sbuf_tensor(f"{tag}_{name}", shape, F32))
        sem = lambda name: signal(nc, ctx, f"{tag}_{name}")
        silu = sb("silu", [I2, 2, 2 * SEQ])
        hid = sb("hid", [I2, 2, 2 * SEQ])
        gates = sb("gates", [P, PAIR, 9])
        acc = sb("acc", [P, PAIR * D])
        xn = make_norm(nc, ctx, f"{tag}_xn")
        up_ready, silu_ready, hid_ready, y_ready, y_used = (sem(k) for k in ("up_ready", "silu_ready", "hid_ready", "y_ready", "y_used"))
        ps_up = lambda s: m.psum[0:I2, 2 * s:2 * s + 2, :].rearrange("p b f -> p (b f)")
        ps_y = lambda s: m.psum[:, 4 + s, 0:PAIR * D]
        block = ctx.enter_context(nc.Block())

        @block.tensor
        def _(pe):
            def up(n, e):
                for k in range(4):
                    last = nc.tensor.matmul(ps_up(e % 2)[:, k * SEQ:(k + 1) * SEQ], m.m1_up[:, e, k * I2:(k + 1) * I2],
                                            tokens_T(m, n), start=True, stop=True)
                last.then_inc(up_ready, 1)

            def step(n, e, last_step, has_prev):
                if e < S - 1:
                    up(n, e + 1)
                elif not last_step:
                    up(n + 1, 0)
                pe.wait_ge(hid_ready, n * S + e + 1)
                pe.wait_ge(y_used, n * S + e + 1)
                for t in range(PAIR):
                    for k in range(2):
                        last = nc.tensor.matmul(ps_y(e % 2)[:, t * D:(t + 1) * D], hid[:, e % 2, k * SEQ + t * P:k * SEQ + (t + 1) * P],
                                                m.m1_down[:, e, k, :], start=(k == 0), stop=(k == 1))
                last.then_inc(y_ready, 1)
            up(0, 0)
            expert_steps(pe, S, step)

        @block.scalar
        def _(act):
            nc.scalar.preload_act_table(ACT.Silu)

            def step(n, e, last_step, has_prev):
                act.wait_ge(up_ready, n * S + e + 1)
                nc.scalar.activation(silu[:, e % 2, :], ps_up(e % 2)[:, 0:2 * SEQ], ACT.Silu).then_inc(silu_ready, 1)
            expert_steps(act, S, step)

        @block.vector
        def _(dve):
            dve.sem_inc(y_used, 2)

            def step(n, e, last_step, has_prev):
                if e == 0:
                    nc.vector.tensor_copy(gates[:, :, :], gates_of(m, n))
                dve.wait_ge(silu_ready, n * S + e + 1)
                nc.vector.tensor_tensor(hid[:, e % 2, :], silu[:, e % 2, :], ps_up(e % 2)[:, 2 * SEQ:4 * SEQ], ALU.mult).then_inc(hid_ready, 1)
                nc.vector.drain()
                dve.wait_ge(y_ready, n * S + e + 1)
                g = min(e, 8)
                for t in range(PAIR):
                    y, a = ps_y(e % 2)[:, t * D:(t + 1) * D], acc[:, t * D:(t + 1) * D]
                    if e == 0:
                        last = nc.vector.tensor_scalar(a, y, gates[:, t, g:g + 1], None, ALU.mult)
                    else:
                        last = nc.vector.scalar_tensor_tensor(out=a, in0=y, scalar=gates[:, t, g:g + 1], in1=a,
                                                              op0=ALU.mult, op1=ALU.add)
                last.then_inc(y_used, 1)
                if e == S - 1:
                    nc.vector.drain()
                    residual_begin(nc, m, xn, n, acc[:, :], 0.5)
                    if last_step:
                        residual_end(nc, dve, m, xn, n)
                if e == 1 and has_prev:
                    residual_end(nc, dve, m, xn, n - 1)
            expert_steps(dve, S, step)

        @block.gpsimd
        def _(pool):
            with pool.Fori(0, NB) as n:
                norm_power(nc, pool, m, xn, n)


def moe_gelu(nc, m, tag):
    route(nc, m, tag + "r", m.m2_gate[:, :], "m2", gate_bias=m.m2_gate_b[:, :], renormalise=True, bias2=m.m2_b2[:, :])
    S, C = 8, 4
    with ExitStack() as ctx:
        sb = lambda name, shape: ctx.enter_context(nc.sbuf_tensor(f"{tag}_{name}", shape, F32))
        sem = lambda name: signal(nc, ctx, f"{tag}_{name}")
        hid = sb("hid", [P, 2, C * SEQ])
        gates = sb("gates", [P, PAIR, 9])
        acc = sb("acc", [P, PAIR * D])
        xn = make_norm(nc, ctx, f"{tag}_xn")
        up_ready, hid_ready, y_ready, y_used = (sem(k) for k in ("up_ready", "hid_ready", "y_ready", "y_used"))
        ps_up = lambda s: m.psum[:, 2 * s:2 * s + 2, :].rearrange("p b f -> p (b f)")
        ps_y = lambda s: m.psum[:, 4 + s, 0:PAIR * D]
        block = ctx.enter_context(nc.Block())

        @block.tensor
        def _(pe):
            def up(n, e):
                for c in range(C):
                    last = nc.tensor.matmul(ps_up(e % 2)[:, c * SEQ:(c + 1) * SEQ], m.m2_w1[:, e, c * P:(c + 1) * P],
                                            tokens_T(m, n), start=True, stop=True)
                last.then_inc(up_ready, 1)

            def step(n, e, last_step, has_prev):
                if e < S - 1:
                    up(n, e + 1)
                elif not last_step:
                    up(n + 1, 0)
                pe.wait_ge(hid_ready, n * S + e + 1)
                pe.wait_ge(y_used, n * S + e + 1)
                for t in range(PAIR):
                    for c in range(C):
                        last = nc.tensor.matmul(ps_y(e % 2)[:, t * D:(t + 1) * D], hid[:, e % 2, c * SEQ + t * P:c * SEQ + (t + 1) * P],
                                                m.m2_w2[:, e, c, :], start=(c == 0), stop=(c == C - 1))
                last.then_inc(y_ready, 1)
            up(0, 0)
            expert_steps(pe, S, step)

        @block.scalar
        def _(act):
            nc.scalar.preload_act_table(ACT.Gelu)

            def step(n, e, last_step, has_prev):
                act.wait_ge(up_ready, n * S + e + 1)
                for c in range(C):
                    last = nc.scalar.activation(hid[:, e % 2, c * SEQ:(c + 1) * SEQ], ps_up(e % 2)[:, c * SEQ:(c + 1) * SEQ],
                                                ACT.Gelu, bias=m.m2_b1[:, e * C + c:e * C + c + 1])
                last.then_inc(hid_ready, 1)
            expert_steps(act, S, step)

        @block.vector
        def _(dve):
            dve.sem_inc(y_used, 2)

            def step(n, e, last_step, has_prev):
                if e == 0:
                    nc.vector.tensor_copy(gates[:, :, :], gates_of(m, n))
                    nc.vector.tensor_copy(acc[:, :], pair_of(m.acc, n))
                nc.vector.drain()
                dve.wait_ge(y_ready, n * S + e + 1)
                for t in range(PAIR):
                    a = acc[:, t * D:(t + 1) * D]
                    last = nc.vector.scalar_tensor_tensor(out=a, in0=ps_y(e % 2)[:, t * D:(t + 1) * D], scalar=gates[:, t, e:e + 1],
                                                          in1=a, op0=ALU.mult, op1=ALU.add)
                last.then_inc(y_used, 1)
                if e == S - 1:
                    nc.vector.drain()
                    residual_begin(nc, m, xn, n, acc[:, :], 0.5)
                    if last_step:
                        residual_end(nc, dve, m, xn, n)
                if e == 1 and has_prev:
                    residual_end(nc, dve, m, xn, n - 1)
            expert_steps(dve, S, step)

        @block.gpsimd
        def _(pool):
            with pool.Fori(0, NB) as n:
                norm_power(nc, pool, m, xn, n)


def moe_common(nc, m, tag):
    route(nc, m, tag + "r", m.m3_gate[:, :], "m3", gate_bias=m.m3_gate_b[:, :])
    E = 8
    with ExitStack() as ctx:
        sb = lambda name, shape: ctx.enter_context(nc.sbuf_tensor(f"{tag}_{name}", shape, F32))
        sem = lambda name: signal(nc, ctx, f"{tag}_{name}")
        silu = sb("silu", [P, 2, 2 * SEQ])
        hid = sb("hid", [P, 2, 2 * SEQ])
        gates = sb("gates", [P, 2, PAIR, 9])
        acc = sb("acc", [P, PAIR * D])
        xn = make_norm(nc, ctx, f"{tag}_xn")
        up_ready, silu_ready, hid_ready, y_ready, y_used = (sem(k) for k in ("up_ready", "silu_ready", "hid_ready", "y_ready", "y_used"))
        ps_up = m.psum[:, 0:2, :].rearrange("p b f -> p (b f)")
        ps_y = lambda t: m.psum[:, 2 + 2 * t:4 + 2 * t, :].rearrange("p b f -> p (b f)")
        ps_s = lambda t: m.psum[:, 6 + t, 0:D]
        block = ctx.enter_context(nc.Block())

        @block.tensor
        def _(pe):
            def lead(u, n):
                for k in range(4):
                    last = nc.tensor.matmul(ps_up[:, k * SEQ:(k + 1) * SEQ], m.m3_up[:, k * P:(k + 1) * P],
                                            tokens_T(m, n), start=True, stop=True)
                last.then_inc(up_ready, 1)
                pe.wait_ge(hid_ready, n + 1)

            def trail(u, n):
                for t in range(PAIR):
                    pe.wait_ge(y_used, PAIR * n + t + 1)
                    nc.tensor.matmul(ps_s(t), hid[:, u, SEQ + t * P:SEQ + (t + 1) * P], m.m3_shared_out[:, :], start=True, stop=True)
                    for k in range(2):
                        last = nc.tensor.matmul(ps_y(t)[:, k * 512:(k + 1) * 512], hid[:, u, t * P:(t + 1) * P],
                                                m.m3_w2[:, k * 512:(k + 1) * 512], start=True, stop=True)
                    last.then_inc(y_ready, 1)
            skewed(pe, lead, trail)

        @block.scalar
        def _(act):
            nc.scalar.preload_act_table(ACT.Silu)

            def lead(u, n):
                act.wait_ge(up_ready, n + 1)
                nc.scalar.activation(silu[:, u, :], ps_up[:, 0:2 * SEQ], ACT.Silu).then_inc(silu_ready, 1)
            skewed(act, lead, lambda u, n: None)

        @block.vector
        def _(dve):
            dve.sem_inc(y_used, PAIR)

            def lead(u, n):
                nc.vector.tensor_copy(gates[:, u, :, :], gates_of(m, n))
                dve.wait_ge(silu_ready, n + 1)
                nc.vector.tensor_tensor(hid[:, u, :], silu[:, u, :], ps_up[:, 2 * SEQ:4 * SEQ], ALU.mult).then_inc(hid_ready, 1)

            def trail(u, n):
                for t in range(PAIR):
                    a = acc[:, t * D:(t + 1) * D]
                    dve.wait_ge(y_ready, PAIR * n + t + 1)
                    nc.vector.tensor_copy(a, ps_s(t))
                    for e in range(E):
                        nc.vector.drain()
                        last = nc.vector.scalar_tensor_tensor(out=a, in0=ps_y(t)[:, e * D:(e + 1) * D], scalar=gates[:, u, t, e:e + 1],
                                                              in1=a, op0=ALU.mult, op1=ALU.add)
                    last.then_inc(y_used, 1)
                nc.vector.drain()
                residual_begin(nc, m, xn, n, acc[:, :], 0.5)
                residual_end(nc, dve, m, xn, n)
                nc.vector.drain()
            skewed(dve, lead, trail)

        @block.gpsimd
        def _(pool):
            with pool.Fori(0, NB) as n:
                norm_power(nc, pool, m, xn, n)


def state_space(nc, m, tag):
    I2, HALVES, S = 96, 2, 8
    STEP = 16
    CH = SEQ // STEP
    WIDE = HALVES * NB * S
    xs = m.arena[0:I2, 0:2, :]
    gate = m.arena[0:I2, 2:4, :]
    xs_t = xs.rearrange("p c (b t) -> p c b t", b=NB)
    with ExitStack() as ctx:
        sb = lambda name, shape: ctx.enter_context(nc.sbuf_tensor(f"{tag}_{name}", shape, F32))
        sem = lambda name: signal(nc, ctx, f"{tag}_{name}")
        decay = sb("decay", [I2, HALVES, NB, S])
        cw = sb("cw", [I2, HALVES, NB, S])
        bw = sb("bw", [I2, HALVES, S])

        with ExitStack() as part:
            sbp = lambda name, shape: part.enter_context(nc.sbuf_tensor(f"{tag}p_{name}", shape, F32))
            semp = lambda name: signal(nc, part, f"{tag}p_{name}")
            z = sbp("z", [P, 2, PAIR, D])
            hT = sbp("hT", [P, 2, SEQ])
            gc = sbp("gc", [I2, 2, HALVES, SEQ])
            dk = sbp("dk", [I2, HALVES * S])
            zn = make_norm(nc, part, f"{tag}_zn")
            z_ready, xT_ready, hT_ready, p_ready, clip_ready, gate_ready = (
                semp(k) for k in ("z_ready", "xT_ready", "hT_ready", "p_ready", "clip_ready", "gate_ready"))
            alog_ready, exp_ready = semp("alog_ready"), semp("exp_ready")
            ps_xT = lambda u: m.psum[:, 5 + u, 0:SEQ]
            ps_p = lambda u: m.psum[0:I2, 1 + 2 * u:3 + 2 * u, :].rearrange("p b (c f) -> p (b c) f", c=2)
            block = part.enter_context(nc.Block())

            @block.tensor
            def _(pe):
                def lead(u, n):
                    pe.wait_ge(z_ready, n + 1)
                    for t in range(PAIR):
                        last = nc.tensor.transpose(ps_xT(u)[:, t * P:(t + 1) * P], z[:, u, t, :], m.ident[:, :])
                    last.then_inc(xT_ready, 1)

                def trail(u, n):
                    pe.wait_ge(hT_ready, n + 1)
                    pe.wait_ge(clip_ready, n + 1)
                    for c in range(4):
                        last = nc.tensor.matmul(ps_p(u)[:, c, :], m.a1_in[:, c * I2:(c + 1) * I2], hT[:, u, :],
                                                start=True, stop=True)
                    last.then_inc(p_ready, 1)
                skewed(pe, lead, trail)

            @block.scalar
            def _(act):
                nc.scalar.preload_act_table(ACT.Exp)
                act.wait_ge(m.loaded["a1"], m.total["a1"])
                act.wait_ge(alog_ready, 1)
                nc.scalar.activation(dk[:, :], dk[:, :], ACT.Exp).then_inc(exp_ready, 1)

                def lead(u, n):
                    act.wait_ge(xT_ready, n + 1)
                    nc.scalar.activation(hT[:, u, :], ps_xT(u), ACT.Identity, bias=m.a1_in_b[:, 0:1],
                                         scale=m.a1_in_g[:, 0:1]).then_inc(hT_ready, 1)

                def trail(u, n):
                    act.wait_ge(clip_ready, n + 3)
                    nc.scalar.activation(gate[:, :, bass.ds(n * SEQ, SEQ)], gc[:, u, :, :], ACT.Tanh).then_inc(gate_ready, 1)
                skewed(act, lead, trail)

            @block.vector
            def _(dve):
                dve.sem_inc(clip_ready, 2)
                dve.sem_inc(gate_ready, 2)
                dve.wait_ge(m.loaded["a1"], m.total["a1"])
                nc.vector.tensor_scalar(dk[:, :], m.a1_alog[:, :], -5.0, 0.0, ALU.max, ALU.min).then_inc(alog_ready, 1)
                dve.wait_ge(exp_ready, 1)
                nc.vector.tensor_scalar(dk[:, :], dk[:, :], -1.0, -2.0, ALU.mult, ALU.max)
                nc.vector.drain()
                nc.vector.tensor_scalar(dk[:, :], dk[:, :], -0.01, 0.9, ALU.min, ALU.mult)
                nc.vector.drain()
                state = lambda v: v.rearrange("p (c s) -> p c s", c=HALVES).unsqueeze(2).to_broadcast([I2, HALVES, NB, S])
                nc.vector.tensor_copy(decay[:, :, :, :], state(dk[:, :]))
                nc.vector.tensor_copy(cw[:, :, :, :], state(m.a1_c[:, :]))
                nc.vector.tensor_scalar(bw[:, :, :].rearrange("p c s -> p (c s)"), m.a1_b[:, :], 0.1, None, ALU.mult)

                def lead(u, n):
                    norm_tokens(nc, dve, zn, n, lambda t: tile_of(m.XN, n, t), lambda t: z[:, u, t, :]).then_inc(z_ready, 1)

                def trail(u, n):
                    dve.wait_ge(p_ready, n + 1)
                    nc.vector.tensor_scalar(xs[:, :, bass.ds(n * SEQ, SEQ)], ps_p(u)[:, 0:2, :], 5.0, -5.0, ALU.min, ALU.max)
                    dve.wait_ge(gate_ready, n + 1)
                    nc.vector.tensor_scalar(gc[:, u, :, :], ps_p(u)[:, 2:4, :], 5.0, -5.0, ALU.min, ALU.max).then_inc(clip_ready, 1)
                skewed(dve, lead, trail)

            @block.gpsimd
            def _(pool):
                with pool.Fori(0, NB) as n:
                    norm_power(nc, pool, m, zn, n)

        with ExitStack() as part:
            sbp = lambda name, shape: part.enter_context(nc.sbuf_tensor(f"{tag}s_{name}", shape, F32))
            semp = lambda name: signal(nc, part, f"{tag}s_{name}")
            drive = sbp("drive", [I2, 2, STEP, WIDE])
            hist = sbp("hist", [I2, 2, STEP, WIDE])
            read = sbp("read", [I2, STEP, WIDE])
            drive_ready, states_ready, states_used = semp("drive_ready"), semp("states_ready"), semp("states_used")
            block = part.enter_context(nc.Block())

            @block.vector
            def _(dve):
                dve.sem_inc(states_used, 2)
                nc.vector.memset(hist[:, 1, STEP - 1, :], 0.0)
                nc.vector.drain()
                dec = decay[:, :, :, :].rearrange("p c b s -> p (c b s)")
                with dve.Fori(0, CH // 2) as i:
                    for u in range(2):
                        dve.wait_ge(drive_ready, 2 * i + u + 1)
                        dve.wait_ge(states_used, 2 * i + u + 1)
                        for t in range(STEP):
                            before = hist[:, u, t - 1, :] if t else hist[:, 1 - u, STEP - 1, :]
                            now = hist[:, u, t, :]
                            nc.vector.tensor_tensor(now, before, dec, ALU.mult)
                            nc.vector.drain()
                            nc.vector.tensor_tensor(now, now, drive[:, u, t, :], ALU.add)
                            nc.vector.drain()
                            last = nc.vector.tensor_scalar(now, now, 5.0, -5.0, ALU.min, ALU.max)
                            if t < STEP - 1:
                                nc.vector.drain()
                        last.then_inc(states_ready, 1)
                        nc.vector.drain()

            @block.gpsimd
            def _(pool):
                def inputs(u, k):
                    for c in range(HALVES):
                        last = nc.gpsimd.tensor_tensor(
                            drive[:, u, :, c * NB * S:(c + 1) * NB * S].rearrange("p t (b s) -> p t b s", b=NB),
                            xs_t[:, c, :, bass.ds(k * STEP, STEP)].rearrange("p b t -> p t b").unsqueeze(3).to_broadcast([I2, STEP, NB, S]),
                            bw[:, c, :].unsqueeze(1).unsqueeze(1).to_broadcast([I2, STEP, NB, S]), ALU.mult)
                    last.then_inc(drive_ready, 1)

                def outputs(u, k):
                    pool.wait_ge(states_ready, k + 1)
                    nc.gpsimd.tensor_tensor(read[:, :, :], hist[:, u, :, :],
                                            cw[:, :, :, :].rearrange("p c b s -> p (c b s)").unsqueeze(1).to_broadcast([I2, STEP, WIDE]),
                                            ALU.mult).then_inc(states_used, 1)
                    nc.gpsimd.drain()
                    r = read[:, :, :].rearrange("p t (g s) -> p (t g) s", s=S)
                    nc.gpsimd.tensor_tensor(r[:, :, 0:4], r[:, :, 0:4], r[:, :, 4:8], ALU.add)
                    nc.gpsimd.drain()
                    nc.gpsimd.tensor_tensor(r[:, :, 0:2], r[:, :, 0:2], r[:, :, 2:4], ALU.add)
                    nc.gpsimd.drain()
                    r = read[:, :, :].rearrange("p t (c b s) -> p c b t s", c=HALVES, b=NB)
                    for c in range(HALVES):
                        nc.gpsimd.tensor_tensor(xs_t[:, c, :, bass.ds(k * STEP, STEP)], r[:, c, :, :, 0], r[:, c, :, :, 1], ALU.add)
                    nc.gpsimd.drain()

                inputs(0, 0)
                with pool.Fori(0, CH // 2 - 1) as i:
                    inputs(1, 2 * i + 1)
                    outputs(0, 2 * i)
                    inputs(0, 2 * i + 2)
                    outputs(1, 2 * i + 1)
                inputs(1, CH - 1)
                outputs(0, CH - 2)
                outputs(1, CH - 1)

        with ExitStack() as part:
            sbp = lambda name, shape: part.enter_context(nc.sbuf_tensor(f"{tag}o_{name}", shape, F32))
            semp = lambda name: signal(nc, part, f"{tag}o_{name}")
            gated = sbp("gated", [I2, 2, HALVES, SEQ])
            o = sbp("o", [P, PAIR, D])
            on, xn = make_norm(nc, part, f"{tag}_on"), make_norm(nc, part, f"{tag}_xn")
            gated_ready, y_ready = semp("gated_ready"), semp("y_ready")
            ps_y = lambda u: m.psum[:, u, 0:PAIR * D].rearrange("p (t f) -> p t f", t=PAIR)
            block = part.enter_context(nc.Block())

            @block.vector
            def _(dve):
                def lead(u, n):
                    nc.vector.tensor_scalar(gated[:, u, :, :], xs[:, :, bass.ds(n * SEQ, SEQ)], 5.0, -5.0, ALU.min, ALU.max)
                    nc.vector.drain()
                    nc.vector.tensor_tensor(gated[:, u, :, :], gated[:, u, :, :], gate[:, :, bass.ds(n * SEQ, SEQ)], ALU.mult).then_inc(gated_ready, 1)

                def trail(u, n):
                    dve.wait_ge(y_ready, n + 1)
                    nc.vector.tensor_scalar(o[:, :, :], ps_y(u), 5.0, -5.0, ALU.min, ALU.max)
                    nc.vector.drain()
                    norm_tokens(nc, dve, on, n, lambda t: o[:, t, :], lambda t: o[:, t, :])
                    nc.vector.drain()
                    nc.vector.tensor_tensor(o[:, :, :], o[:, :, :], m.a1_out_g[:, :].unsqueeze(1).to_broadcast([P, PAIR, D]), ALU.mult)
                    nc.vector.drain()
                    nc.vector.tensor_tensor(o[:, :, :], o[:, :, :], m.a1_out_b[:, :].unsqueeze(1).to_broadcast([P, PAIR, D]), ALU.add)
                    nc.vector.drain()
                    residual_begin(nc, m, xn, n, o[:, :, :].rearrange("p t f -> p (t f)"), 1.0)
                    residual_end(nc, dve, m, xn, n)
                    nc.vector.drain()
                skewed(dve, lead, trail)

            @block.tensor
            def _(pe):
                def unit(u, n):
                    pe.wait_ge(gated_ready, n + 1)
                    for t in range(PAIR):
                        for c in range(HALVES):
                            last = nc.tensor.matmul(ps_y(u)[:, t, :], gated[:, u, c, t * P:(t + 1) * P], m.a1_out[:, c, :],
                                                    start=(c == 0), stop=(c == HALVES - 1))
                    last.then_inc(y_ready, 1)
                skewed(pe, unit, lambda u, n: None)

            @block.gpsimd
            def _(pool):
                with pool.Fori(0, NB) as n:
                    norm_power(nc, pool, m, on, n)
                    norm_power(nc, pool, m, xn, n)


def threaded(eng, first, unit, tail):
    first()
    unit(0, 0, False, True)
    with eng.Fori(0, NB // 2 - 1) as i:
        unit(1, 2 * i + 1, True, True)
        unit(0, 2 * i + 2, True, True)
    unit(1, NB - 1, True, False)
    tail(1, NB - 1)


def grouped_attention(nc, m, tag, local):
    HEADS, KV, HD, GROUPS = 16, 4, 8, 8
    QK = HEADS + KV
    Q1 = 160 - P if local else P
    W0 = P + Q1
    W = W0 + P
    VW = HD + 1
    STREAM = 96
    VPAD = (KV - 1) * VW + STREAM
    w = m.a0l if local else m.a0g
    src = m.H1 if local else m.XN
    with ExitStack() as ctx:
        sb = lambda name, shape: ctx.enter_context(nc.sbuf_tensor(f"{tag}_{name}", shape, F32))
        sem = lambda name: signal(nc, ctx, f"{tag}_{name}")
        r = sb("r", [P, PAIR, D])
        xT = sb("xT", [P, SEQ])
        lat = sb("lat", [32, SEQ])
        rot = sb("rot", [P, PAIR, QK * HD])
        tmp = sb("tmp", [P, 2, PAIR, QK, HD // 2])
        ss = sb("ss", [P, PAIR * QK])
        inv = sb("inv", [P, PAIR * QK])
        qn = sb("qn", [P, PAIR, D])
        kn = sb("kn", [P, PAIR, D])
        qT = sb("qT", [P, 2, SEQ])
        kT = sb("kT", [P, 2, 4, SEQ])
        va = sb("va", [P, 2, PAIR, VPAD])
        pT = sb("pT", [P, 4, 2, W])
        rec = sb("rec", [P, PAIR * HEADS])
        o = sb("o", [P, PAIR, HEADS, HD])
        oT = sb("oT", [P, SEQ])
        r2 = sb("r2", [P, PAIR * D])
        rn, xn = make_norm(nc, ctx, f"{tag}_rn"), make_norm(nc, ctx, f"{tag}_xn")
        r_ready, rT_ready, xT_ready, lat_ready, latT_ready, p_ready = (sem(k) for k in ("r_ready", "rT_ready", "xT_ready", "lat_ready", "latT_ready", "p_ready"))
        ss_ready, ssinv_ready, qk_ready, qkT_ready, qT_ready, kT_ready = (sem(k) for k in ("ss_ready", "ssinv_ready", "qk_ready", "qkT_ready", "qT_ready", "kT_ready"))
        s_ready, e_ready, masked, av_ready, o_ready, otr_ready, oT_ready, y_ready = (sem(k) for k in ("s_ready", "e_ready", "masked", "av_ready", "o_ready", "otr_ready", "oT_ready", "y_ready"))
        ps_s = lambda g: m.psum[:, 2 * (g % 2):2 * (g % 2) + 2, :]
        ps_a, ps_b = m.psum[:, 4, 0:SEQ], m.psum[:, 5, 0:PAIR * 192].rearrange("p (t f) -> p t f", t=PAIR)
        ps_av = lambda t, slot: m.psum[:, 6, 256 * t + slot * VW:256 * t + slot * VW + STREAM]
        av_heads = m.psum[:, 6, :].rearrange("p (t f) -> p t f", t=PAIR)[:, :, 0:HEADS * VW].rearrange("p t (s f) -> p t s f", f=VW)
        ps_o = m.psum[:, 7, 0:SEQ]
        ps_y = m.psum[:, 7, 256:512]
        heads_of = lambda g: [(2 * (g % 2) + k, g // 2) for k in range(2)]
        block = ctx.enter_context(nc.Block())

        @block.tensor
        def _(pe):
            def start_a(u, n):
                pe.wait_ge(r_ready, n + 1)
                for t in range(PAIR):
                    last = nc.tensor.transpose(ps_a[:, t * P:(t + 1) * P], r[:, t, :], m.ident[:, :])
                last.then_inc(rT_ready, 1)

            def start_b(u, n):
                pe.wait_ge(xT_ready, n + 1)
                if not local:
                    nc.tensor.matmul(ps_a[0:32, :], w.down[:, :], xT[:, :], start=True, stop=True).then_inc(lat_ready, 1)
                else:
                    for t in range(PAIR):
                        last = nc.tensor.matmul(ps_b[:, t, :], xT[:, t * P:(t + 1) * P], w.qkv[:, :], start=True, stop=True)
                    last.then_inc(p_ready, 1)

            def start_c(u, n):
                if not local:
                    pe.wait_ge(latT_ready, n + 1)
                    for t in range(PAIR):
                        nc.tensor.matmul(ps_b[:, t, 0:P], xT[:, t * P:(t + 1) * P], w.q[:, :], start=True, stop=True)
                        last = nc.tensor.matmul(ps_b[:, t, P:192], lat[:, t * P:(t + 1) * P], w.kv[:, :], start=True, stop=True)
                    last.then_inc(p_ready, 1)

            def start_d(u, n):
                pe.wait_ge(qk_ready, n + 1)
                for t in range(PAIR):
                    nc.tensor.transpose(ps_a[:, t * P:(t + 1) * P], qn[:, t, :], m.ident[:, :])
                    last = nc.tensor.transpose(m.psum[:, 5, t * P:(t + 1) * P], kn[:, t, :], m.ident[:, :])
                last.then_inc(qkT_ready, 1)

            def scores(u, n, g):
                for k, (kv, j) in enumerate(heads_of(g)):
                    rows = slice(32 * kv, 32 * kv + 32)
                    nc.tensor.matmul(ps_s(g)[:, k, 0:W0], kT[rows, u, j, 0:P], qT[rows, u, 0:W0], start=True, stop=True)
                    last = nc.tensor.matmul(ps_s(g)[:, k, W0:W], kT[rows, u, j, P:SEQ], qT[rows, u, P:SEQ], start=True, stop=True)
                last.then_inc(s_ready, 1)

            def values(u, n, g):
                pe.wait_ge(masked, GROUPS * n + g + 1)
                for k, (kv, j) in enumerate(heads_of(g)):
                    slot = 2 * g + k
                    p = pT[:, g % 4, k, :]
                    v = lambda t: va[:, u, t, kv * VW:kv * VW + STREAM]
                    nc.tensor.matmul(ps_av(0, slot), p[:, 0:P], v(0), start=True, stop=True)
                    nc.tensor.matmul(ps_av(1, slot), p[:, W0:W], v(1), start=True, stop=local)
                    last = nc.tensor.matmul(ps_av(1, slot)[0:Q1, :], p[:, P:W0], v(0), start=False, stop=True,
                                            skip_group_check=local)
                if g == GROUPS - 1:
                    last.then_inc(av_ready, 1)

            def end_a(u, n):
                pe.wait_ge(o_ready, n + 1)
                for t in range(PAIR):
                    last = nc.tensor.transpose(ps_o[:, t * P:(t + 1) * P], o[:, t, :, :].rearrange("p h f -> p (h f)"), m.ident[:, :])
                last.then_inc(otr_ready, 1)

            def end_b(u, n):
                pe.wait_ge(oT_ready, n + 1)
                for t in range(PAIR):
                    last = nc.tensor.matmul(ps_y[:, t * D:(t + 1) * D], oT[:, t * P:(t + 1) * P], w.o[:, :], start=True, stop=True)
                last.then_inc(y_ready, 1)

            def ready(n):
                pe.wait_ge(qT_ready, n + 1)
                pe.wait_ge(kT_ready, n + 1)

            def first():
                pe.wait_ge(m.loaded["a0"], m.total["a0"])
                start_a(0, 0)
                start_b(0, 0)
                start_c(0, 0)
                start_d(0, 0)
                ready(0)
                scores(0, 0, 0)

            def unit(u, n, prev, next):
                for g in range(GROUPS):
                    if prev or g:
                        pe.wait_ge(e_ready, GROUPS * n + g)
                    if g < GROUPS - 1:
                        scores(u, n, g + 1)
                    elif next:
                        ready(n + 1)
                        scores(1 - u, n + 1, 0)
                    if prev and g == 1:
                        pe.wait_ge(o_ready, n)
                    if g:
                        values(u, n, g - 1)
                    elif prev:
                        values(1 - u, n - 1, GROUPS - 1)
                    if prev and g == 1:
                        end_a(1 - u, n - 1)
                    if prev and g == 2:
                        end_b(1 - u, n - 1)
                    if next and g in (2, 3, 4, 6):
                        {2: start_a, 3: start_b, 4: start_c, 6: start_d}[g](1 - u, n + 1)

            def tail(u, n):
                values(u, n, GROUPS - 1)
                end_a(u, n)
                end_b(u, n)
            threaded(pe, first, unit, tail)

        @block.scalar
        def _(act):
            nc.scalar.preload_act_table_set("natural_log_exp_and_others")

            def start_b(u, n):
                act.wait_ge(rT_ready, n + 1)
                nc.scalar.activation(xT[:, :], ps_a, ACT.Identity, scale=w.norm[:, 0:1]).then_inc(xT_ready, 1)

            def start_c(u, n):
                if not local:
                    act.wait_ge(lat_ready, n + 1)
                    nc.scalar.activation(lat[:, :], ps_a[0:32, :], ACT.Copy).then_inc(latT_ready, 1)

            def start_d(u, n):
                act.wait_ge(ss_ready, n + 1)
                nc.scalar.activation(inv[:, :], ss[:, :], ACT.Ln)
                nc.scalar.drain()
                nc.scalar.activation(inv[:, :], inv[:, :], ACT.Exp, scale=-0.5).then_inc(ssinv_ready, 1)

            def start_e(u, n):
                act.wait_ge(qkT_ready, n + 1)
                nc.scalar.activation(qT[:, u, :], ps_a, ACT.Copy).then_inc(qT_ready, 1)

            def exps(u, n, g):
                act.wait_ge(s_ready, GROUPS * n + g + 1)
                nc.scalar.activation(pT[:, g % 4, :, :], ps_s(g)[:, :, 0:W], ACT.Exp, scale=float(HD) ** -0.5).then_inc(e_ready, 1)

            def end_b(u, n):
                act.wait_ge(otr_ready, n + 1)
                nc.scalar.activation(oT[:, :], ps_o, ACT.Copy).then_inc(oT_ready, 1)

            def first():
                act.wait_ge(m.loaded["a0"], m.total["a0"])
                start_b(0, 0)
                start_c(0, 0)
                start_d(0, 0)
                start_e(0, 0)

            def unit(u, n, prev, next):
                for g in range(GROUPS):
                    if next and g == 6:
                        start_d(1 - u, n + 1)
                    if next and g == 7:
                        start_e(1 - u, n + 1)
                    exps(u, n, g)
                    if prev and g == 2:
                        end_b(1 - u, n - 1)
                    if next and g in (3, 4):
                        {3: start_b, 4: start_c}[g](1 - u, n + 1)
            threaded(act, first, unit, end_b)

        @block.vector
        def _(dve):
            def start_a(u, n):
                norm_begin(nc, rn, lambda t: tile_of(src, n, t), eps=1e-6, rms=True)

            def start_b(u, n):
                norm_end(nc, dve, rn, n, lambda t: tile_of(src, n, t), lambda t: r[:, t, :], rms=True).then_inc(r_ready, 1)

            def start_d(u, n):
                dve.wait_ge(p_ready, n + 1)
                even = ps_b[:, :, 0:QK * HD].rearrange("p t (h i two) -> p t h i two", h=QK, two=2)
                out = rot[:, :, :].rearrange("p t (h i two) -> p t h i two", h=QK, two=2)
                table = lambda v: v.unsqueeze(2).to_broadcast([P, PAIR, QK, HD // 2])
                nc.vector.tensor_copy(va[:, u, :, 0:KV * VW].rearrange("p t (g f) -> p t g f", f=VW)[:, :, :, 0:HD], ps_b[:, :, QK * HD:192].rearrange("p t (g f) -> p t g f", g=KV))
                for half, (a, b, op) in enumerate(((w.cos, w.sin, ALU.subtract), (w.sin, w.cos, ALU.add))):
                    nc.vector.tensor_tensor(tmp[:, 0, :, :, :], even[:, :, :, :, 0], table(a[:, :, :]), ALU.mult)
                    nc.vector.tensor_tensor(tmp[:, 1, :, :, :], even[:, :, :, :, 1], table(b[:, :, :]), ALU.mult)
                    nc.vector.drain()
                    nc.vector.tensor_tensor(out[:, :, :, :, half], tmp[:, 0, :, :, :], tmp[:, 1, :, :, :], op)
                    nc.vector.drain()
                sq = tmp[:, :, :, :, :].rearrange("p a t h i -> p (a t h i)")
                flat = rot[:, :, :].rearrange("p t f -> p (t f)")
                nc.vector.tensor_tensor(sq, flat, flat, ALU.mult)
                nc.vector.drain()
                nc.vector.tensor_reduce(ss[:, :], sq.rearrange("p (h f) -> p h f", f=HD), AX.X, ALU.add)
                nc.vector.drain()
                nc.vector.tensor_scalar(ss[:, :], ss[:, :], 1.0 / HD, 1e-6, ALU.mult, ALU.add).then_inc(ss_ready, 1)

            def start_d2(u, n):
                dve.wait_ge(ssinv_ready, n + 1)
                scale = inv[:, :].rearrange("p (t h) -> p t h", t=PAIR)
                for t in range(PAIR):
                    nc.vector.tensor_tensor(qn[:, t, :].rearrange("p (h f) -> p h f", f=HD), rot[:, t, 0:P].rearrange("p (h f) -> p h f", f=HD),
                                            scale[:, t, 0:HEADS].unsqueeze(2).to_broadcast([P, HEADS, HD]), ALU.mult)
                    last = nc.vector.tensor_tensor(
                        kn[:, t, :].rearrange("p (g j f) -> p g j f", g=KV, j=4),
                        rot[:, t, P:P + KV * HD].rearrange("p (g f) -> p g f", g=KV).unsqueeze(2).to_broadcast([P, KV, 4, HD]),
                        scale[:, t, HEADS:QK].unsqueeze(2).unsqueeze(2).to_broadcast([P, KV, 4, HD]), ALU.mult)
                last.then_inc(qk_ready, 1)

            def start_e(u, n):
                dve.wait_ge(qkT_ready, n + 1)
                for j in range(4):
                    last = nc.vector.tensor_scalar(kT[:, u, j, :], m.psum[:, 5, 0:SEQ], m.copy_mask[:, j:j + 1], None, ALU.mult)
                last.then_inc(kT_ready, 1)

            def mask(u, n, g):
                dve.wait_ge(e_ready, GROUPS * n + g + 1)
                if local:
                    p, k = pT[:, g % 4, :, :], m.window_mask[:, :].unsqueeze(1).to_broadcast([P, 2, W])
                else:
                    p = pT[:, g % 4, :, :].rearrange("p h (b f) -> p h b f", f=P)[:, :, 0:3:2, :]
                    k = m.causal_mask[:, :].unsqueeze(1).unsqueeze(1).to_broadcast([P, 2, 2, P])
                nc.vector.tensor_tensor(p, p, k, ALU.mult).then_inc(masked, 1)

            def end_a(u, n):
                dve.wait_ge(av_ready, n + 1)
                nc.vector.reciprocal(rec[:, :].rearrange("p (t h) -> p t h", t=PAIR), av_heads[:, :, :, HD])
                nc.vector.drain()
                for t in range(PAIR):
                    last = nc.vector.tensor_tensor(o[:, t, :, :].rearrange("p (kv j) f -> p j kv f", kv=KV),
                                                   av_heads[:, t, :, 0:HD].rearrange("p (j kv) f -> p j kv f", kv=KV),
                                                   rec[:, t * HEADS:(t + 1) * HEADS].rearrange("p (j kv) -> p j kv", kv=KV).unsqueeze(3).to_broadcast([P, 4, KV, HD]),
                                                   ALU.mult)
                last.then_inc(o_ready, 1)

            def end_c(u, n):
                dve.wait_ge(y_ready, n + 1)
                nc.vector.tensor_tensor(r2[:, :], ps_y, pair_of(src, n), ALU.add)
                nc.vector.drain()
                if local:
                    residual_begin(nc, m, xn, n, r2[:, :], 1.0)
                else:
                    nc.vector.tensor_copy(pair_of(m.H1, n), r2[:, :])
                nc.vector.drain()

            def first():
                dve.wait_ge(m.loaded["a0"], m.total["a0"])
                nc.vector.memset(va[:, :, :, :], 1.0)
                nc.vector.drain()
                start_a(0, 0)
                start_b(0, 0)
                start_d(0, 0)
                start_d2(0, 0)
                start_e(0, 0)

            def unit(u, n, prev, next):
                for g in range(GROUPS):
                    if next and g == 7:
                        start_e(1 - u, n + 1)
                    mask(u, n, g)
                    if prev and g == 0:
                        end_a(1 - u, n - 1)
                    if next and g == 0:
                        start_a(1 - u, n + 1)
                    if next and g == 1:
                        start_b(1 - u, n + 1)
                    if prev and g == 3:
                        end_c(1 - u, n - 1)
                    if prev and g == 4 and local:
                        residual_end(nc, dve, m, xn, n - 1)
                    if next and g == 5:
                        start_d(1 - u, n + 1)
                    if next and g == 6:
                        start_d2(1 - u, n + 1)

            def tail(u, n):
                end_a(u, n)
                end_c(u, n)
                if local:
                    residual_end(nc, dve, m, xn, n)
            threaded(dve, first, unit, tail)

        @block.gpsimd
        def _(pool):
            def unit(u, n, prev, next):
                if next:
                    norm_power(nc, pool, m, rn, n + 1)
                if prev and local:
                    norm_power(nc, pool, m, xn, n - 1)

            def tail(u, n):
                if local:
                    norm_power(nc, pool, m, xn, n)
            threaded(pool, lambda: norm_power(nc, pool, m, rn, 0), unit, tail)


def latent_and_local_attention(nc, m):
    grouped_attention(nc, m, "global", False)
    grouped_attention(nc, m, "local", True)


def full_attention(nc, m, tag):
    HEADS, HD, GROUPS = 16, 8, 8
    VW = HD + 1
    STREAM = 96
    VPAD = (HEADS - 1) * VW + STREAM
    with ExitStack() as ctx:
        sb = lambda name, shape: ctx.enter_context(nc.sbuf_tensor(f"{tag}_{name}", shape, F32))
        sem = lambda name: signal(nc, ctx, f"{tag}_{name}")
        z = sb("z", [P, PAIR, D])
        xT = sb("xT", [P, SEQ])
        qT = sb("qT", [P, 2, SEQ])
        kT = sb("kT", [P, 2, 4, SEQ])
        va = sb("va", [P, 2, PAIR, VPAD])
        nmax = sb("nmax", [P, 2, 4])
        p = sb("p", [P, 2, 4, SEQ])
        pT = sb("pT", [P, 2, 4, SEQ])
        rec = sb("rec", [P, PAIR * HEADS])
        o = sb("o", [P, PAIR, HEADS, HD])
        zn, xn = make_norm(nc, ctx, f"{tag}_zn"), make_norm(nc, ctx, f"{tag}_xn")
        z_ready, zT_ready, xT_ready, qk_ready, qkT_ready, v_ready, va_ready = (
            sem(k) for k in ("z_ready", "zT_ready", "xT_ready", "qk_ready", "qkT_ready", "v_ready", "va_ready"))
        s_ready, nmax_ready, e_ready, tr_ready, pT_ready, av_ready, av_used = (
            sem(k) for k in ("s_ready", "nmax_ready", "e_ready", "tr_ready", "pT_ready", "av_ready", "av_used"))
        ps_s = lambda g: m.psum[:, 2 * (g % 2):2 * (g % 2) + 2, :].rearrange("p b (t f) -> p (b t) f", t=PAIR)
        ps_t = m.psum[:, 4:6, :].rearrange("p b (t f) -> p (b t) f", t=PAIR)
        ps_av = lambda t, slot: m.psum[:, 6, 256 * t + slot * VW:256 * t + slot * VW + STREAM]
        av_heads = m.psum[:, 6, :].rearrange("p (t f) -> p t f", t=PAIR)[:, :, 0:HEADS * VW].rearrange("p t (s f) -> p t s f", f=VW)
        ps_x = m.psum[:, 7, :].rearrange("p (a f) -> p a f", a=2)
        heads_of = lambda g: [(2 * (g % 2) + k, g // 2) for k in range(2)]
        block = ctx.enter_context(nc.Block())

        @block.tensor
        def _(pe):
            def start_a(u, n):
                pe.wait_ge(z_ready, n + 1)
                for t in range(PAIR):
                    last = nc.tensor.transpose(ps_x[:, 0, t * P:(t + 1) * P], z[:, t, :], m.ident[:, :])
                last.then_inc(zT_ready, 1)

            def start_b(u, n):
                pe.wait_ge(xT_ready, n + 1)
                nc.tensor.matmul(ps_x[:, 0, :], m.a3_q[:, :], xT[:, :], start=True, stop=True)
                nc.tensor.matmul(ps_x[:, 1, :], m.a3_k[:, :], xT[:, :], start=True, stop=True).then_inc(qk_ready, 1)

            def start_c(u, n):
                pe.wait_ge(qkT_ready, n + 1)
                for t in range(PAIR):
                    last = nc.tensor.matmul(ps_x[:, 0, t * P:(t + 1) * P], xT[:, t * P:(t + 1) * P], m.a3_v[:, :], start=True, stop=True)
                last.then_inc(v_ready, 1)

            def scores(u, n, g):
                for k, (rg, j) in enumerate(heads_of(g)):
                    rows = slice(32 * rg, 32 * rg + 32)
                    for t in range(PAIR):
                        last = nc.tensor.matmul(ps_s(g)[:, 2 * k + t, :], qT[rows, u, t * P:(t + 1) * P], kT[rows, u, j, :],
                                                start=True, stop=True)
                last.then_inc(s_ready, 1)

            def turn(n, g):
                pe.wait_ge(e_ready, GROUPS * n + g + 1)
                for k in range(2):
                    for kt in range(2):
                        for t in range(PAIR):
                            last = nc.tensor.transpose(ps_t[:, 2 * k + kt, t * P:(t + 1) * P],
                                                       p[:, g % 2, 2 * k + t, kt * P:(kt + 1) * P], m.ident[:, :])
                last.then_inc(tr_ready, 1)

            def values(u, n, g):
                pe.wait_ge(pT_ready, GROUPS * n + g + 1)
                if g == 0:
                    pe.wait_ge(av_used, n + 1)
                    pe.wait_ge(va_ready, n + 1)
                for k, (rg, j) in enumerate(heads_of(g)):
                    h = 4 * rg + j
                    for t in range(PAIR):
                        for kt in range(2):
                            last = nc.tensor.matmul(ps_av(t, 2 * g + k), pT[:, g % 2, 2 * k + kt, t * P:(t + 1) * P],
                                                    va[:, u, kt, h * VW:h * VW + STREAM],
                                                    start=(kt == 0), stop=(kt == 1))
                if g == GROUPS - 1:
                    last.then_inc(av_ready, 1)

            def first():
                pe.wait_ge(m.loaded["a3"], m.total["a3"])
                start_a(0, 0)
                start_b(0, 0)
                start_c(0, 0)
                scores(0, 0, 0)

            def unit(u, n, prev, next):
                for g in range(GROUPS):
                    if g < GROUPS - 1:
                        scores(u, n, g + 1)
                    elif next:
                        scores(1 - u, n + 1, 0)
                    if g:
                        values(u, n, g - 1)
                    elif prev:
                        values(1 - u, n - 1, GROUPS - 1)
                    turn(n, g)
                    if next and g in (3, 4, 6):
                        {3: start_a, 4: start_b, 6: start_c}[g](1 - u, n + 1)
            threaded(pe, first, unit, lambda u, n: values(u, n, GROUPS - 1))

        @block.scalar
        def _(act):
            nc.scalar.preload_act_table(ACT.Exp)

            def start_b(u, n):
                act.wait_ge(zT_ready, n + 1)
                nc.scalar.activation(xT[:, :], ps_x[:, 0, :], ACT.Identity, bias=m.a3_ln_b[:, 0:1], scale=m.a3_ln_g[:, 0:1]).then_inc(xT_ready, 1)

            def exps(n, g):
                act.wait_ge(nmax_ready, GROUPS * n + g + 1)
                for k in range(4):
                    last = nc.scalar.activation(p[:, g % 2, k, :], ps_s(g)[:, k, :], ACT.Exp, bias=nmax[:, g % 2, k:k + 1])
                last.then_inc(e_ready, 1)

            def first():
                act.wait_ge(m.loaded["a3"], m.total["a3"])
                start_b(0, 0)
                exps(0, 0)

            def unit(u, n, prev, next):
                for g in range(GROUPS):
                    if g < GROUPS - 1:
                        exps(n, g + 1)
                    elif next:
                        exps(n + 1, 0)
                    if next and g == 3:
                        start_b(1 - u, n + 1)
            threaded(act, first, unit, lambda u, n: None)

        @block.vector
        def _(dve):
            def start_a(u, n):
                norm_begin(nc, zn, lambda t: tile_of(m.XN, n, t))

            def start_b(u, n):
                norm_end(nc, dve, zn, n, lambda t: tile_of(m.XN, n, t), lambda t: z[:, t, :]).then_inc(z_ready, 1)

            def start_c(u, n):
                dve.wait_ge(qk_ready, n + 1)
                nc.vector.tensor_scalar(qT[:, u, :], ps_x[:, 0, :], m.a3_bq[:, 0:1], float(HD) ** -0.5, ALU.add, ALU.mult)
                for j in range(4):
                    last = nc.vector.tensor_scalar(kT[:, u, j, :], ps_x[:, 1, :], m.a3_bk[:, 0:1], m.copy_mask[:, j:j + 1], ALU.add, ALU.mult)
                last.then_inc(qkT_ready, 1)

            def start_d(u, n):
                dve.wait_ge(v_ready, n + 1)
                nc.vector.tensor_tensor(va[:, u, :, 0:HEADS * VW].rearrange("p t (h f) -> p t h f", f=VW)[:, :, :, 0:HD], ps_x[:, 0, :].rearrange("p (t h f) -> p t h f", t=PAIR, h=HEADS),
                                        m.a3_bv[:, :].rearrange("p (h f) -> p h f", h=HEADS).unsqueeze(1).to_broadcast([P, PAIR, HEADS, HD]),
                                        ALU.add).then_inc(va_ready, 1)

            def maxima(n, g):
                dve.wait_ge(s_ready, GROUPS * n + g + 1)
                nc.vector.tensor_reduce(nmax[:, g % 2, :], ps_s(g), AX.X, ALU.max, negate=True).then_inc(nmax_ready, 1)

            def evacuate(n, g):
                dve.wait_ge(tr_ready, GROUPS * n + g + 1)
                nc.vector.tensor_copy(pT[:, g % 2, :, :], ps_t).then_inc(pT_ready, 1)

            def end(u, n):
                dve.wait_ge(av_ready, n + 1)
                nc.vector.reciprocal(rec[:, :].rearrange("p (t h) -> p t h", t=PAIR), av_heads[:, :, :, HD])
                nc.vector.drain()
                for t in range(PAIR):
                    last = nc.vector.tensor_tensor(o[:, t, :, :].rearrange("p (r j) f -> p j r f", r=4),
                                                   av_heads[:, t, :, 0:HD].rearrange("p (j r) f -> p j r f", r=4),
                                                   rec[:, t * HEADS:(t + 1) * HEADS].rearrange("p (j r) -> p j r", r=4).unsqueeze(3).to_broadcast([P, 4, 4, HD]),
                                                   ALU.mult)
                last.then_inc(av_used, 1)
                nc.vector.drain()
                residual_begin(nc, m, xn, n, o[:, :, :, :].rearrange("p t h f -> p (t h f)"), 1.0)

            def end_b(u, n):
                residual_end(nc, dve, m, xn, n)

            def first():
                dve.sem_inc(av_used, 1)
                dve.wait_ge(m.loaded["a3"], m.total["a3"])
                dve.wait_ge(m.loaded["a0"], m.total["a0"])
                nc.vector.memset(va[:, :, :, :], 1.0)
                nc.vector.drain()
                start_a(0, 0)
                start_b(0, 0)
                start_c(0, 0)
                start_d(0, 0)
                maxima(0, 0)

            def unit(u, n, prev, next):
                for g in range(GROUPS):
                    if g < GROUPS - 1:
                        maxima(n, g + 1)
                    elif next:
                        maxima(n + 1, 0)
                    evacuate(n, g)
                    if prev and g == 0:
                        end(1 - u, n - 1)
                    if prev and g == 1:
                        end_b(1 - u, n - 1)
                    if next and g in (1, 2, 5, 7):
                        {1: start_a, 2: start_b, 5: start_c, 7: start_d}[g](1 - u, n + 1)

            def tail(u, n):
                end(u, n)
                end_b(u, n)
            threaded(dve, first, unit, tail)

        @block.gpsimd
        def _(pool):
            def unit(u, n, prev, next):
                if prev:
                    norm_power(nc, pool, m, xn, n - 1)
                if next:
                    norm_power(nc, pool, m, zn, n + 1)
            threaded(pool, lambda: norm_power(nc, pool, m, zn, 0), unit, lambda u, n: norm_power(nc, pool, m, xn, n))


def relative_attention(nc, m, tag):
    H, WIN = 8, 384
    S4 = 4
    SCALE = float(D) ** -0.5
    rel_k = m.arena[:, 1:3, :].rearrange("p a (h r) -> p (a h) r", h=4)

    with ExitStack() as ctx:
        sb = lambda name, shape: ctx.enter_context(nc.sbuf_tensor(f"{tag}r_{name}", shape, F32))
        sem = lambda name: signal(nc, ctx, f"{tag}r_{name}")
        w_rel, positions = sb("w_rel", [96, 2, 1024]), sb("positions", [96, 2, 512])
        loaded, tr_ready, xT_ready, rel_ready, rel_moved = (sem(k) for k in ("loaded", "tr_ready", "xT_ready", "rel_ready", "rel_moved"))
        block = ctx.enter_context(nc.Block())

        @block.sync
        def _(sp):
            sp.dma_start(w_rel[:], m.a2_w_rel).then_inc(loaded, 16)
            sp.dma_start(positions[:], m.a2_positions).then_inc(loaded, 16)

        @block.tensor
        def _(pe):
            for q in range(4):
                for t in range(4):
                    last = nc.tensor.transpose(m.psum[:, q, t * P:(t + 1) * P],
                                               m.XN[:, 2 * q + t // 2, (t % 2) * D:(t % 2 + 1) * D], m.ident[:, :])
                last.then_inc(tr_ready, 1)
            pe.wait_ge(loaded, 32)
            for h in range(H):
                if h >= 4:
                    pe.wait_ge(rel_moved, h - 3)
                for c in range(2):
                    last = nc.tensor.matmul(m.psum[:, 4 + h % 4, :], w_rel[:, c, h * P:(h + 1) * P], positions[:, c, :],
                                            start=(c == 0), stop=(c == 1))
                last.then_inc(rel_ready, 1)

        @block.scalar
        def _(act):
            nc.scalar.preload_act_table(ACT.Exp)
            for h in range(H):
                act.wait_ge(rel_ready, h + 1)
                nc.scalar.activation(rel_k[:, h, :], m.psum[:, 4 + h % 4, :], ACT.Copy).then_inc(rel_moved, 1)

        @block.vector
        def _(dve):
            for q in range(4):
                dve.wait_ge(tr_ready, q + 1)
                nc.vector.tensor_copy(m.XT[:, q * 512:(q + 1) * 512], m.psum[:, q, :])

    with ExitStack() as ctx:
        sb = lambda name, shape: ctx.enter_context(nc.sbuf_tensor(f"{tag}_{name}", shape, F32))
        sem = lambda name: signal(nc, ctx, f"{tag}_{name}")
        xs = sb("xs", [P, 2, SEQ])
        q1, q2, kk = sb("q1", [P, S4, SEQ]), sb("q2", [P, 2, SEQ]), sb("kk", [P, S4, SEQ])
        v = sb("v", [P, S4, PAIR, P])
        pos = sb("pos", [P, 2, PAIR, WIN])
        shifted = sb("shifted", [P, S4, PAIR, SEQ])
        p = sb("p", [P, 2, PAIR, SEQ])
        nmax, total = sb("nmax", [P, 2, PAIR]), sb("total", [P, 2, PAIR])
        pT = sb("pT", [P, 2, PAIR, SEQ])
        oT = sb("oT", [P, 2, SEQ])
        acc = sb("acc", [P, PAIR * D])
        xn = make_norm(nc, ctx, f"{tag}_xn")
        scratch = nc.dram_tensor(f"{tag}_scratch", (S4, PAIR, P, WIN), F32).ap()
        names = ("xs_ready", "qk_ready", "q_ready", "v_ready", "v_moved", "pos_ready", "pos_moved", "pos_written", "pos_shifted",
                 "s_ready", "nmax_ready", "e_ready", "p_ready", "tr_ready", "pT_ready", "oT_ready", "o_moved", "y_ready", "y_used")
        (xs_ready, qk_ready, q_ready, v_ready, v_moved, pos_ready, pos_moved, pos_written, pos_shifted,
         s_ready, nmax_ready, e_ready, p_ready, tr_ready, pT_ready, oT_ready, o_moved, y_ready, y_used) = (sem(k) for k in names)
        ps_qk = m.psum[:, 0, :].rearrange("p (a f) -> p a f", a=2)
        ps_v = m.psum[:, 1, 0:SEQ]
        ps_s = m.psum[:, 2, :].rearrange("p (t f) -> p t f", t=PAIR)
        ps_pos = m.psum[:, 3:5, 0:WIN]
        ps_t = m.psum[:, 5, :].rearrange("p (t f) -> p t f", t=PAIR)
        ps_o = m.psum[:, 6, 0:SEQ]
        ps_y = m.psum[:, 7, 0:PAIR * D]
        block = ctx.enter_context(nc.Block())

        def run(eng, part_a, part_b, part_c, begin=None, end=None):
            begin, end = begin or (lambda u, n: None), end or (lambda u, n: None)

            def batch(u, n, prev, next):
                for h in range(H):
                    if h < H - 2:
                        part_a(u, n, h + 2)
                    elif next:
                        if h == H - 2:
                            begin(1 - u, n + 1)
                        part_a(1 - u, n + 1, h + 2 - H)
                    part_b(u, n, h)
                    if h:
                        part_c(u, n, h - 1)
                    elif prev:
                        part_c(1 - u, n - 1, H - 1)
                        end(1 - u, n - 1)

            def first():
                begin(0, 0)
                part_a(0, 0, 0)
                part_a(0, 0, 1)

            def tail(u, n):
                part_c(u, n, H - 1)
                end(u, n)
            threaded(eng, first, batch, tail)

        @block.tensor
        def _(pe):
            def part_a(u, n, h):
                s = H * n + h
                if h == 0:
                    pe.wait_ge(xs_ready, n + 1)
                for a in range(2):
                    last = nc.tensor.matmul(ps_qk[:, a, :], m.a2_w[:, a, h * P:(h + 1) * P], xs[:, u, :], start=True, stop=True)
                last.then_inc(qk_ready, 1)
                pe.wait_ge(v_moved, s + 1)
                for t in range(PAIR):
                    last = nc.tensor.matmul(ps_v[:, t * P:(t + 1) * P], xs[:, u, t * P:(t + 1) * P], m.a2_w[:, 2, h * P:(h + 1) * P],
                                            start=True, stop=True)
                last.then_inc(v_ready, 1)
                pe.wait_ge(q_ready, s + 1)
                pe.wait_ge(pos_moved, s + 1)
                for t in range(PAIR):
                    last = nc.tensor.matmul(ps_pos[:, t, :], q2[:, h % 2, t * P:(t + 1) * P],
                                            rel_k[:, h, P - P * t:P - P * t + WIN], start=True, stop=True)
                last.then_inc(pos_ready, 1)

            def part_b(u, n, h):
                for t in range(PAIR):
                    last = nc.tensor.matmul(ps_s[:, t, :], q1[:, h % S4, t * P:(t + 1) * P], kk[:, h % S4, :], start=True, stop=True)
                last.then_inc(s_ready, 1)

            def part_c(u, n, h):
                s = H * n + h
                pe.wait_ge(p_ready, s + 1)
                for kt in range(2):
                    for t in range(PAIR):
                        last = nc.tensor.transpose(ps_t[:, kt, t * P:(t + 1) * P], p[:, h % 2, t, kt * P:(kt + 1) * P], m.ident[:, :])
                last.then_inc(tr_ready, 1)
                pe.wait_ge(pT_ready, s + 1)
                for kt in range(2):
                    last = nc.tensor.matmul(ps_o, v[:, h % S4, kt, :], pT[:, h % 2, kt, :], start=(kt == 0), stop=(kt == 1))
                last.then_inc(oT_ready, 1)
                pe.wait_ge(o_moved, s + 1)
                pe.wait_ge(y_used, s + 1)
                for t in range(PAIR):
                    last = nc.tensor.matmul(ps_y[:, t * D:(t + 1) * D], oT[:, h % 2, t * P:(t + 1) * P], m.a2_out[:, h, :], start=True, stop=True)
                last.then_inc(y_ready, 1)
            pe.wait_ge(m.loaded["a2"], m.total["a2"])
            run(pe, part_a, part_b, part_c)

        @block.scalar
        def _(act):
            nc.scalar.preload_act_table(ACT.Exp)

            def part_a(u, n, h):
                s = H * n + h
                act.wait_ge(qk_ready, s + 1)
                nc.scalar.activation(q1[:, h % S4, :], ps_qk[:, 0, :], ACT.Identity, bias=m.a2_embed_bias[:, h:h + 1], scale=SCALE)
                nc.scalar.activation(q2[:, h % 2, :], ps_qk[:, 0, :], ACT.Identity, bias=m.a2_pos_bias[:, h:h + 1], scale=SCALE)
                nc.scalar.activation(kk[:, h % S4, :], ps_qk[:, 1, :], ACT.Copy).then_inc(q_ready, 1)
                act.wait_ge(pos_ready, s + 1)
                act.wait_ge(pos_written, 16 * s + 16)
                nc.scalar.activation(pos[:, h % 2, :, :], ps_pos, ACT.Copy).then_inc(pos_moved, 1)

            def part_b(u, n, h):
                act.wait_ge(nmax_ready, H * n + h + 1)
                for t in range(PAIR):
                    last = nc.scalar.activation(p[:, h % 2, t, :], p[:, h % 2, t, :], ACT.Exp, bias=nmax[:, h % 2, t:t + 1],
                                                accum_out=total[:, h % 2, t:t + 1])
                last.then_inc(e_ready, 1)

            def part_c(u, n, h):
                act.wait_ge(oT_ready, H * n + h + 1)
                nc.scalar.activation(oT[:, h % 2, :], ps_o, ACT.Copy).then_inc(o_moved, 1)
            run(act, part_a, part_b, part_c)

        @block.vector
        def _(dve):
            def part_a(u, n, h):
                dve.wait_ge(v_ready, H * n + h + 1)
                nc.vector.tensor_copy(v[:, h % S4, :, :].rearrange("p t f -> p (t f)"), ps_v).then_inc(v_moved, 1)

            def part_b(u, n, h):
                s = H * n + h
                dve.wait_ge(s_ready, s + 1)
                dve.wait_ge(pos_shifted, 16 * s + 16)
                nc.vector.tensor_tensor(p[:, h % 2, :, :], ps_s, shifted[:, h % S4, :, :], ALU.add)
                nc.vector.drain()
                nc.vector.tensor_reduce(nmax[:, h % 2, :], p[:, h % 2, :, :], AX.X, ALU.max, negate=True).then_inc(nmax_ready, 1)
                dve.wait_ge(e_ready, s + 1)
                nc.vector.reciprocal(total[:, h % 2, :], total[:, h % 2, :])
                nc.vector.drain()
                for t in range(PAIR):
                    last = nc.vector.tensor_scalar(p[:, h % 2, t, :], p[:, h % 2, t, :], total[:, h % 2, t:t + 1], None, ALU.mult)
                last.then_inc(p_ready, 1)

            def part_c(u, n, h):
                s = H * n + h
                dve.wait_ge(tr_ready, s + 1)
                nc.vector.tensor_copy(pT[:, h % 2, :, :], ps_t).then_inc(pT_ready, 1)
                dve.wait_ge(y_ready, s + 1)
                before = m.a2_b_out[:, :] if h == 0 else acc[:, :]
                nc.vector.tensor_tensor(acc[:, :], ps_y, before, ALU.add).then_inc(y_used, 1)
                nc.vector.drain()

            def end(u, n):
                residual_begin(nc, m, xn, n, acc[:, :], 1.0)
                residual_end(nc, dve, m, xn, n)
                nc.vector.drain()
            dve.sem_inc(v_moved, 1)
            dve.sem_inc(pos_moved, 1)
            dve.sem_inc(y_used, 1)
            dve.sem_inc(pos_written, 32)
            run(dve, part_a, part_b, part_c, end=end)

        @block.gpsimd
        def _(pool):
            def begin(u, n):
                nc.gpsimd.tensor_copy(xs[:, u, :], tokens_T(m, n)).then_inc(xs_ready, 1)
            nothing = lambda u, n, h: None
            run(pool, nothing, nothing, nothing, begin, lambda u, n: norm_power(nc, pool, m, xn, n))

        @block.sync
        def _(sp):
            def part_a(u, n, h):
                s = H * n + h
                sp.wait_ge(pos_moved, s + 2)
                sp.dma_start(scratch[h % S4].rearrange("t q r -> q t r"), pos[:, h % 2, :, :]).then_inc(pos_written, 16)
                sp.wait_ge(pos_written, 16 * s + 48)
                rows = scratch[h % S4].rearrange("t q r -> t (q r)")[:, P - 1:P - 1 + P * (WIN - 1)]
                skewed_rows = rows.rearrange("t (q r) -> q t r", r=WIN - 1)[:, :, 0:SEQ]
                sp.dma_start(shifted[:, h % S4, :, :], skewed_rows).then_inc(pos_shifted, 16)
            nothing = lambda u, n, h: None
            run(sp, part_a, nothing, nothing)


def build(nc, h, out, first, last):
    with ExitStack() as ctx:
        sb = lambda name, shape: ctx.enter_context(nc.sbuf_tensor(name, shape, F32))
        m = Record()
        m.loaded, m.total = {}, {}
        m.psum = ctx.enter_context(nc.psum_tensor("psum", [P, 8, 512], F32))
        m.X = sb("X", [P, NB, PAIR * D])
        m.XN = sb("XN", [P, NB, PAIR * D])
        loads = {}

        def load(group, name, dst, src):
            loads.setdefault(group, []).append((dst, src))

        def weight(group, name, shape):
            buf = sb(name, shape)
            load(group, name, buf[:], h[name])
            return buf
        load("x", "x", m.X[:].rearrange("p n (t d) -> p (n t) d", t=PAIR), h["x"].rearrange("(t p) d -> p t d", p=P))
        m.ident = weight("const", "ident", [P, P])
        m.ones = weight("const", "ones", [P, P])
        m.neg_half = weight("const", "neg_half", [P, 80])
        m.f0_w1 = weight("f0", "f0_w1", [P, 512])
        m.f0_w2 = weight("f0", "f0_w2", [P, 512])
        m.f0_b1 = sb("f0_b1", [P, PAIR, 512])
        for t in range(PAIR):
            load("f0", "f0_b1", m.f0_b1[:, t, :], h["f0_b1"].partition_broadcast(P))
        m.f0_b2 = sb("f0_b2", [P, PAIR * D])
        for t in range(PAIR):
            load("f0", "f0_b2", m.f0_b2[:, t * D:(t + 1) * D], h["f0_b2"].partition_broadcast(P))
        m.f0_ln1_g = weight("f0", "f0_ln1_g", [P, 1])
        m.f0_ln1_b = weight("f0", "f0_ln1_b", [P, 1])
        m.f0_ln2_g = weight("f0", "f0_ln2_g", [P, 4])
        m.f0_ln2_b = weight("f0", "f0_ln2_b", [P, 4])
        m.m1_gate = weight("m1", "m1_gate", [P, 9])
        m.m1_up = weight("m1", "m1_up", [P, 10, 352])
        m.m1_down = weight("m1", "m1_down", [88, 10, 2, D])
        m.m2_gate = weight("m2", "m2_gate", [P, 8])
        m.m2_gate_b = sb("m2_gate_b", [P, 8])
        load("m2", "m2_gate_b", m.m2_gate_b[:, :], h["m2_gate_b"].partition_broadcast(P))
        m.m2_b1 = weight("m2", "m2_b1", [P, 32])
        m.m2_w1 = weight("m2", "m2_w1", [P, 8, 512])
        m.m2_w2 = weight("m2", "m2_w2", [P, 8, 4, D])
        m.m2_b2 = sb("m2_b2", [P, D])
        for t in range(NT):
            load("const", "m2_b2", m.m2_b2[8 * t:8 * t + 8, :], h["m2_b2"])
        m.m3_gate = weight("m3", "m3_gate", [P, 8])
        m.m3_gate_b = sb("m3_gate_b", [P, 8])
        load("m3", "m3_gate_b", m.m3_gate_b[:, :], h["m3_gate_b"].partition_broadcast(P))
        m.m3_up = weight("m3", "m3_up", [P, 512])
        m.m3_shared_out = weight("m3", "m3_shared_out", [P, D])
        m.m3_w2 = weight("m3", "m3_w2", [P, 8 * D])
        m.countdown = weight("const", "countdown", [P, 8])
        m.tile_mask = weight("const", "tile_mask", [P, NT])
        m.gates = sb("gates", [P, NT, 9])
        m.arena = sb("arena", [P, 4, NB * SEQ])
        m.XT = m.arena[:, 0, :]
        m.acc = m.arena[:, 1, :].rearrange("p (n f) -> p n f", n=NB)
        m.bias2_of_tile = m.arena[:, 2, :]
        m.a1_in_g = weight("a1", "a1_in_g", [P, 1])
        m.a1_in_b = weight("a1", "a1_in_b", [P, 1])
        m.a1_in = weight("a1", "a1_in", [P, 384])
        m.a1_out = weight("a1", "a1_out", [96, 2, D])
        m.a1_alog = weight("a1", "a1_alog", [96, 16])
        m.a1_b = weight("a1", "a1_b", [96, 16])
        m.a1_c = weight("a1", "a1_c", [96, 16])
        for part in ("out_g", "out_b"):
            buf = sb("a1_" + part, [P, D])
            load("a1", "a1_" + part, buf[:, :], h["a1_" + part].partition_broadcast(P))
            if part == "out_g":
                m.a1_out_g = buf
            else:
                m.a1_out_b = buf
        m.H1 = m.arena[:, 3, :].rearrange("p (n f) -> p n f", n=NB)
        m.a0g, m.a0l = Record(), Record()
        m.a0g.norm, m.a0l.norm = weight("a0", "a0g_norm", [P, 1]), weight("a0", "a0l_norm", [P, 1])
        m.a0g.q = weight("a0", "a0g_q", [P, D])
        m.a0g.down = weight("a0", "a0g_down", [P, 32])
        m.a0g.kv = weight("a0", "a0g_kv", [32, 64])
        m.a0l.qkv = weight("a0", "a0l_qkv", [P, 192])
        m.a0g.o, m.a0l.o = weight("a0", "a0g_o", [P, D]), weight("a0", "a0l_o", [P, D])
        m.a0g.cos, m.a0g.sin = weight("a0", "a0g_cos", [P, PAIR, 4]), weight("a0", "a0g_sin", [P, PAIR, 4])
        m.a0l.cos, m.a0l.sin = weight("a0", "a0l_cos", [P, PAIR, 4]), weight("a0", "a0l_sin", [P, PAIR, 4])
        m.copy_mask = weight("a0", "copy_mask", [P, 4])
        m.causal_mask = weight("a0", "causal_mask", [P, P])
        m.window_mask = weight("a0", "window_mask", [P, 288])
        m.a3_ln_g, m.a3_ln_b = weight("a3", "a3_ln_g", [P, 1]), weight("a3", "a3_ln_b", [P, 1])
        m.a3_q, m.a3_k, m.a3_v = (weight("a3", "a3_" + k, [P, D]) for k in "qkv")
        m.a3_bq, m.a3_bk = weight("a3", "a3_bq", [P, 1]), weight("a3", "a3_bk", [P, 1])
        m.a3_bv = sb("a3_bv", [P, D])
        load("a3", "a3_bv", m.a3_bv[:, :], h["a3_bv"].partition_broadcast(P))
        m.a2_w = weight("a2", "a2_w", [P, 3, 8 * P])
        m.a2_out = weight("a2", "a2_out", [P, 8, D])
        m.a2_embed_bias, m.a2_pos_bias = weight("a2", "a2_embed_bias", [P, 8]), weight("a2", "a2_pos_bias", [P, 8])
        m.a2_b_out = sb("a2_b_out", [P, PAIR * D])
        for t in range(PAIR):
            load("a2", "a2_b_out", m.a2_b_out[:, t * D:(t + 1) * D], h["a2_b_out"].partition_broadcast(P))
        m.a2_w_rel, m.a2_positions = h["a2_w_rel"], h["a2_positions"]
        for group in loads:
            m.loaded[group] = ctx.enter_context(nc.semaphore("loaded_" + group))
            m.total[group] = 16 * len(loads[group])
        stored = ctx.enter_context(nc.semaphore("stored"))

        with nc.Block() as block:
            @block.sync
            def _(sp):
                for group, parts in loads.items():
                    for dst, src in parts:
                        sp.dma_start(dst, src).then_inc(m.loaded[group], 16)
        input_norm(nc, m)
        clear_signals(nc)
        stages = [
            lambda: (ternary_weights(nc, m), ffn_ternary(nc, m, "f0a")),
            lambda: latent_and_local_attention(nc, m),
            lambda: ffn_ternary(nc, m, "f0b"),
            lambda: moe_gated(nc, m, "m1a"),
            lambda: state_space(nc, m, "a1"),
            lambda: moe_gated(nc, m, "m1b"),
            lambda: moe_gelu(nc, m, "m2a"),
            lambda: relative_attention(nc, m, "a2"),
            lambda: moe_gelu(nc, m, "m2b"),
            lambda: moe_common(nc, m, "m3a"),
            lambda: full_attention(nc, m, "a3"),
            lambda: moe_common(nc, m, "m3b"),
        ]
        for stage in stages[first:last]:
            stage()
            clear_signals(nc)
        with nc.Block() as block:
            @block.sync
            def _(sp):
                for group in loads:
                    sp.wait_ge(m.loaded[group], m.total[group])
                sp.dma_start(out.rearrange("(t p) d -> p t d", p=P),
                             m.X[:].rearrange("p n (t d) -> p (n t) d", t=PAIR)).then_inc(stored, 16)
                sp.wait_ge(stored, 16)


FIRST, LAST = 0, 12


def position_features(length, size):
    f = np.float32
    n = size // 6
    distances = np.arange(-length + 1, length, dtype=f)
    far = np.abs(distances)[:, None]
    half_life = f(2.0) ** np.linspace(3.0, math.log(length) / math.log(2.0), n, dtype=f)
    decaying = np.exp(f(-math.log(2.0)) / half_life[None] * far)
    central = (f(2.0) ** np.arange(1, n + 1, dtype=f) - f(1.0) > far).astype(f)
    stddev = length / (2.0 * n)
    mean = np.linspace(length / n, float(length), n, dtype=f)[None]
    shape = (mean / f(stddev)) ** f(2.0)
    rate = mean / f(stddev ** 2)
    log_far = np.log(np.where(far > 0, far, f(1.0)))
    log_unnormed = np.where(far > 0, (shape - f(1.0)) * log_far, f(-np.inf)) - rate * far
    log_norm = np.array([[math.lgamma(float(v)) for v in shape[0]]], dtype=f) - shape * np.log(rate)
    gamma = np.exp(log_unnormed - log_norm).astype(f) + f(1e-8)
    gamma = gamma / np.max(gamma, axis=-1, keepdims=True)
    out = np.concatenate([decaying, central, gamma], -1)
    return np.concatenate([out, np.sign(distances)[:, None] * out], -1).astype(f)


def kernel(**a):
    import concourse.bacc as bacc
    from concourse.bass_utils import run_bass_kernel_spmd as run
    c = lambda v: np.ascontiguousarray(v)
    a = {k: np.asarray(v) for k, v in a.items()}
    arrays = {
        "x": c(a["L0_attn_hidden"].reshape(NB * SEQ, D)),
        "ident": np.eye(P, dtype=np.float32),
        "ones": np.ones((P, P), np.float32),
        "neg_half": np.full((P, 80), -0.5, np.float32),
        "f0_w1": c(a["L0_ffn_w1"].T),
        "f0_w2": c(a["L0_ffn_w2"].reshape(D, 4, P).transpose(2, 1, 0).reshape(P, 512)),
        "f0_b1": a["L0_ffn_b1"], "f0_b2": a["L0_ffn_b2"],
        "f0_ln1_g": c(a["L0_ffn_ln1_g"].reshape(P, 1)), "f0_ln1_b": c(a["L0_ffn_ln1_b"].reshape(P, 1)),
        "f0_ln2_g": c(a["L0_ffn_ln2_g"].reshape(4, P).T), "f0_ln2_b": c(a["L0_ffn_ln2_b"].reshape(4, P).T),
    }
    eu = a["L1_ffn_experts_gate_up"].transpose(2, 0, 1)
    sg, su = (a[f"L1_ffn_shared_{k}_w"].reshape(2, 176, D).transpose(2, 0, 1) for k in ("gate", "up"))
    arrays["m1_up"] = c(np.concatenate([eu, np.concatenate([sg, su], 2)], 1))
    ed = a["L1_ffn_experts_down"].reshape(8, D, 2, 88).transpose(3, 0, 2, 1)
    sd = a["L1_ffn_shared_down_w"].reshape(D, 2, 2, 88).transpose(3, 1, 2, 0)
    arrays["m1_down"] = c(np.concatenate([ed, sd], 1))
    arrays["m1_gate"] = c(np.concatenate([a["L1_ffn_gate_w"], a["L1_ffn_shared_expert_gate_w"]], 0).T)
    arrays["m2_gate"], arrays["m2_gate_b"] = a["L2_ffn_Wg"], a["L2_ffn_bg"]
    arrays["m2_b1"] = c(a["L2_ffn_b1"].reshape(32, P).T)
    arrays["m2_w1"] = c(a["L2_ffn_W1"].transpose(1, 0, 2))
    arrays["m2_w2"] = c(a["L2_ffn_W2"].reshape(8, 4, P, D).transpose(2, 0, 1, 3))
    arrays["m2_b2"] = a["L2_ffn_b2"]
    arrays["m3_gate"], arrays["m3_gate_b"] = a["L3_ffn_w_gate"], a["L3_ffn_gate_bias"]
    arrays["a1_in_g"], arrays["a1_in_b"] = a["L1_attn_ln_in_g"].reshape(P, 1), a["L1_attn_ln_in_b"].reshape(P, 1)
    arrays["a1_in"] = c(a["L1_attn_W_in"].T)
    arrays["a1_out"] = c(a["L1_attn_W_out"].T.reshape(2, 96, D).transpose(1, 0, 2))
    for k, v in (("alog", "A_log"), ("b", "B"), ("c", "C")):
        arrays["a1_" + k] = c(a["L1_attn_" + v].reshape(2, 96, 8).transpose(1, 0, 2).reshape(96, 16))
    arrays["a1_out_g"], arrays["a1_out_b"] = a["L1_attn_ln_out_g"], a["L1_attn_ln_out_b"]
    arrays["a0g_norm"], arrays["a0l_norm"] = a["L0_attn_norm1_w"].reshape(P, 1), a["L0_attn_norm2_w"].reshape(P, 1)
    arrays["a0g_q"], arrays["a0g_down"] = a["L0_attn_g_wq"], a["L0_attn_g_kv_down"]
    arrays["a0g_kv"] = c(np.concatenate([a["L0_attn_g_k_up"], a["L0_attn_g_v_up"]], 1))
    arrays["a0l_qkv"] = c(np.concatenate([a["L0_attn_l_wq"], a["L0_attn_l_wk"], a["L0_attn_l_wv"]], 1))
    arrays["a0g_o"], arrays["a0l_o"] = a["L0_attn_g_wo"], a["L0_attn_l_wo"]
    for k, base in (("g", 1000000.0), ("l", 10000.0)):
        inv_freq = (np.float32(1.0) / np.float32(base) ** (np.arange(0, 8, 2, dtype=np.float32) / np.float32(8))).astype(np.float32)
        angle = np.arange(SEQ, dtype=np.float32)[:, None] * inv_freq[None]
        for name, fn in (("cos", np.cos), ("sin", np.sin)):
            arrays[f"a0{k}_{name}"] = c(fn(angle).astype(np.float32).reshape(PAIR, P, 4).transpose(1, 0, 2))
    row = np.arange(P)
    arrays["copy_mask"] = (row[:, None] % 32 // 8 == np.arange(4)[None]).astype(np.float32)
    arrays["causal_mask"] = (row[:, None] <= row[None]).astype(np.float32)
    gap = np.arange(160)[None] - row[:, None]
    window = ((gap >= 0) & (gap < 32)).astype(np.float32)
    arrays["window_mask"] = c(np.concatenate([window, window[:, :P]], 1))
    arrays["a3_ln_g"], arrays["a3_ln_b"] = a["L3_attn_ln_g"].reshape(P, 1), a["L3_attn_ln_b"].reshape(P, 1)
    arrays["a3_q"], arrays["a3_k"], arrays["a3_v"] = (a["L3_attn_W" + k] for k in "qkv")
    arrays["a3_bq"], arrays["a3_bk"], arrays["a3_bv"] = a["L3_attn_bq"].reshape(P, 1), a["L3_attn_bk"].reshape(P, 1), a["L3_attn_bv"]
    arrays["a2_w"] = c(np.stack([a["L2_attn_w_qs"], a["L2_attn_w_ks"], a["L2_attn_w_vs"]], 1))
    arrays["a2_out"] = c(a["L2_attn_w_out"].reshape(8, P, D).transpose(1, 0, 2))
    arrays["a2_embed_bias"], arrays["a2_pos_bias"] = c(a["L2_attn_rel_embed_bias"].reshape(8, P).T), c(a["L2_attn_rel_pos_bias"].reshape(8, P).T)
    arrays["a2_b_out"] = a["L2_attn_b_out"]
    arrays["a2_w_rel"] = c(a["L2_attn_w_rel_pos_k"].reshape(2, 96, 1024).transpose(1, 0, 2))
    arrays["a2_positions"] = c(np.pad(position_features(SEQ, 192), ((0, 1), (0, 0))).T.reshape(2, 96, 512).transpose(1, 0, 2))
    w1, ws = a["L3_ffn_w1_shared"], a["L3_ffn_w_shared_in"]
    arrays["m3_up"] = c(np.concatenate([w1[:, :P], ws[:, :P], w1[:, P:], ws[:, P:]], 1))
    arrays["m3_shared_out"] = a["L3_ffn_w_shared_out"]
    arrays["m3_w2"] = c(a["L3_ffn_w2"].transpose(1, 0, 2).reshape(P, 8 * D))
    arrays["countdown"] = np.tile(np.arange(8, 0, -1, dtype=np.float32), (P, 1))
    arrays["tile_mask"] = np.repeat(np.eye(NT, dtype=np.float32), 8, 0)
    nc = bacc.Bacc("TRN2", target_bir_lowering=False, num_devices=1)
    ins, h = {}, {}
    for name, v in arrays.items():
        ins["in_" + name] = v
        h[name] = nc.dram_tensor("in_" + name, v.shape, F32, kind="ExternalInput").ap()
    out = nc.dram_tensor("out", (NB * SEQ, D), F32, kind="ExternalOutput").ap()
    build(nc, h, out, FIRST, LAST)
    r = run(nc, [ins], core_ids=[0])
    return np.asarray(r.results[0]["out"]).reshape(NB, SEQ, D)
```

```python
import math
from contextlib import ExitStack

import numpy as np
import concourse.bass as bass
from concourse import mybir

F32 = mybir.dt.float32
F32R = mybir.dt.float32r
ALU = mybir.AluOpType
ACT = mybir.ActivationFunctionType
AX = mybir.AxisListType

P = 128
D = 128
NB = 8
SEQ = 256
PAIR = SEQ // P
NT = NB * PAIR
EPS = 1e-5


class Record:
    pass


def pipelined(eng, parts):
    first, last = min(ahead for ahead, part in parts), max(ahead for ahead, part in parts)

    def peeled(k):
        for ahead, part in parts:
            if 0 <= k + ahead < NB:
                part((k + ahead) % 2, k + ahead)
    pairs = (NB - last + first) // 2
    for k in range(-last, -first):
        peeled(k)
    with eng.Fori(0, pairs) as i:
        for k in range(2):
            for ahead, part in parts:
                part((k - first + ahead) % 2, 2 * i + k - first + ahead)
    for k in range(2 * pairs - first, NB - first):
        peeled(k)


def split_matmul(nc, out, lhsT, rhs):
    nc.tensor.matmul(out, lhsT[0], rhs[0], start=True, stop=False)
    nc.tensor.matmul(out, lhsT[0], rhs[1], start=False, stop=False)
    return nc.tensor.matmul(out, lhsT[1], rhs[0], start=False, stop=True)


SIGNALS_USED = []


def signal(nc, ctx, name):
    s = ctx.enter_context(nc.semaphore(name))
    SIGNALS_USED.append(s.num)
    return s


def clear_signals(nc):
    numbers = sorted(set(SIGNALS_USED))
    SIGNALS_USED.clear()
    runs = []
    for k in numbers:
        if runs and runs[-1][1] == k:
            runs[-1][1] = k + 1
        else:
            runs.append([k, k + 1])
    with nc.Block() as block:
        @block.sync
        def _(sp):
            for low, high in runs:
                sp.sem_clear(range(low, high))


def tile_of(buf, n, t):
    return buf[:, bass.ds(n, 1), t * D:(t + 1) * D].rearrange("p a f -> p (a f)")


def pair_of(buf, n):
    return buf[:, bass.ds(n, 1), :].rearrange("p a f -> p (a f)")


def make_norm(nc, ctx, tag):
    sb = lambda name, shape: ctx.enter_context(nc.sbuf_tensor(f"{tag}_{name}", shape, F32))
    nm = Record()
    nm.stats, nm.mv = sb("stats", [P, PAIR, 6]), sb("mv", [P, PAIR, 2])
    nm.var, nm.inv = sb("var", [P, PAIR]), sb("inv", [P, PAIR])
    nm.var_ready = signal(nc, ctx, f"{tag}_var_ready")
    nm.inv_ready = signal(nc, ctx, f"{tag}_inv_ready")
    return nm


def norm_begin(nc, nm, src, eps=EPS, rms=False):
    for t in range(PAIR):
        nc.vector.bn_stats(nm.stats[:, t, :], src(t))
    nc.vector.drain()
    for t in range(PAIR):
        nc.vector.bn_aggr(nm.mv[:, t, :], nm.stats[:, t, :])
    nc.vector.drain()
    if rms:
        nc.vector.tensor_tensor(nm.var[:, :], nm.mv[:, :, 0], nm.mv[:, :, 0], ALU.mult)
        nc.vector.drain()
        nc.vector.tensor_tensor(nm.var[:, :], nm.var[:, :], nm.mv[:, :, 1], ALU.add)
        nc.vector.drain()
        nc.vector.tensor_scalar(nm.var[:, :], nm.var[:, :], eps, None, ALU.add).then_inc(nm.var_ready, 1)
    else:
        nc.vector.tensor_scalar(nm.var[:, :], nm.mv[:, :, 1], eps, None, ALU.add).then_inc(nm.var_ready, 1)


def norm_end(nc, dve, nm, n, src, dst, rms=False):
    dve.wait_ge(nm.inv_ready, n + 1)
    for t in range(PAIR):
        if rms:
            last = nc.vector.tensor_scalar(dst(t), src(t), nm.inv[:, t:t + 1], None, ALU.mult)
        else:
            last = nc.vector.tensor_scalar(dst(t), src(t), nm.mv[:, t, 0:1], nm.inv[:, t:t + 1],
                                           ALU.subtract, ALU.mult)
    return last


def norm_power(nc, pool, m, nm, n):
    pool.wait_ge(nm.var_ready, n + 1)
    nc.gpsimd.tensor_tensor(nm.inv[:, :], nm.var[:, :], m.neg_half[:, 0:PAIR], ALU.pow).then_inc(nm.inv_ready, 1)


def residual_begin(nc, m, nm, n, src, scale):
    nc.vector.scalar_tensor_tensor(out=pair_of(m.X, n), in0=src, scalar=scale, in1=pair_of(m.X, n),
                                   op0=ALU.mult, op1=ALU.add)
    nc.vector.drain()
    norm_begin(nc, nm, lambda t: tile_of(m.X, n, t))


def residual_end(nc, dve, m, nm, n):
    norm_end(nc, dve, nm, n, lambda t: tile_of(m.X, n, t), lambda t: tile_of(m.XN, n, t))


def input_norm(nc, m):
    with ExitStack() as ctx:
        nms = [make_norm(nc, ctx, f"in{u}") for u in range(2)]
        block = ctx.enter_context(nc.Block())

        @block.sync
        def _(sp):
            m.issue_early(sp)

        @block.vector
        def _(dve):
            nc.vector.memset(m.gates[:, :, :], 0.0)
            dve.wait_ge(m.loaded["x"], 16)
            sources = lambda n: lambda t: tile_of(m.X, n, t)
            pipelined(dve, [(1, lambda u, n: norm_begin(nc, nms[u], sources(n))),
                            (0, lambda u, n: norm_end(nc, dve, nms[u], n // 2, sources(n), lambda t: tile_of(m.XN, n, t)))])

        @block.gpsimd
        def _(pool):
            pool.wait_ge(m.loaded["const"], m.total["const"])
            pipelined(pool, [(0, lambda u, n: norm_power(nc, pool, m, nms[u], n // 2))])


def ternary_weights(nc, m):
    with ExitStack() as ctx:
        sb = lambda name, shape: ctx.enter_context(nc.sbuf_tensor("tq_" + name, shape, F32))
        sem = lambda name: signal(nc, ctx, "tq_" + name)
        part = sb("part", [P, 2])
        scale = sb("scale", [P, 2, 2])
        wq = sb("wq", [P, 2, 512])
        part_ready, total_ready = sem("part_ready"), sem("total_ready")
        total = m.psum[:, 0, 0:2]
        weights = (m.f0_w1, m.f0_w2)
        block = ctx.enter_context(nc.Block())

        @block.vector
        def _(dve):
            dve.wait_ge(m.loaded["f0"], m.total["f0"])
            for j, w in enumerate(weights):
                last = nc.vector.tensor_reduce(part[:, j:j + 1], w[:, :], AX.X, ALU.add, apply_absolute_value=True)
            last.then_inc(part_ready, 1)
            dve.wait_ge(total_ready, 1)
            nc.vector.tensor_scalar(scale[:, 1, :], total, 1.0 / (512 * D), 1e-5, ALU.mult, ALU.max)
            nc.vector.drain()
            nc.vector.reciprocal(scale[:, 0, :], scale[:, 1, :])
            nc.vector.drain()
            nc.vector.reciprocal(scale[:, 1, :], scale[:, 0, :])
            nc.vector.drain()
            both = list(enumerate(weights))
            for j, w in both:
                nc.vector.tensor_scalar(wq[:, j, :], w[:, :], scale[:, 0, j:j + 1], 1.0, ALU.mult, ALU.min)
            nc.vector.drain()
            nc.vector.tensor_scalar(wq[:, :, :], wq[:, :, :], -1.0, 12582912.0, ALU.max, ALU.add)
            nc.vector.drain()
            for j, w in both:
                nc.vector.tensor_scalar(wq[:, j, :], wq[:, j, :], 12582912.0, scale[:, 1, j:j + 1], ALU.subtract, ALU.mult)
            nc.vector.drain()
            for j, w in both:
                nc.vector.tensor_tensor(wq[:, j, :], wq[:, j, :], w[:, :], ALU.subtract)
            nc.vector.drain()
            for j, w in both:
                nc.vector.tensor_tensor(w[:, :], wq[:, j, :], w[:, :], ALU.add)

        @block.tensor
        def _(pe):
            pe.wait_ge(m.loaded["const"], m.total["const"])
            pe.wait_ge(part_ready, 1)
            nc.tensor.matmul(total, m.ones[:, :], part[:, :], start=True, stop=True).then_inc(total_ready, 1)


def ffn_ternary(nc, m, tag, issue_loads=None):
    HID, C = 512, 4
    with ExitStack() as ctx:
        sb = lambda name, shape: ctx.enter_context(nc.sbuf_tensor(f"{tag}_{name}", shape, F32))
        sem = lambda name: signal(nc, ctx, f"{tag}_{name}")
        z = sb("z", [P, 2, PAIR, D])
        hT = sb("hT", [P, 2, PAIR * P])
        hid = sb("hid", [P, 2, PAIR, HID])
        gT = sb("gT", [P, C, PAIR * P])
        yb = sb("yb", [P, PAIR * D])
        zn, gn, xn = (make_norm(nc, ctx, f"{tag}_{k}") for k in ("zn", "gn", "xn"))
        ps_xT = m.psum[:, 0, 0:PAIR * P]
        ps_h = m.psum[:, 1:3, :]
        ps_g = m.psum[:, 3:5, :]
        ps_y = m.psum[:, 5, 0:PAIR * D]
        z_ready, xT_ready, hT_ready, h_ready = sem("z_ready"), sem("xT_ready"), sem("hT_ready"), sem("h_ready")
        hb_ready, g_ready, gn_ready = sem("hb_ready"), sem("g_ready"), sem("gn_ready")
        tr_ready, gT_ready, y_ready, y_used = sem("tr_ready"), sem("gT_ready"), sem("y_ready"), sem("y_used")
        block = ctx.enter_context(nc.Block())

        @block.tensor
        def _(pe):
            def turn_tokens(u, n):
                pe.wait_ge(z_ready, n + 1)
                for t in range(PAIR):
                    last = nc.tensor.transpose(ps_xT[:, t * P:(t + 1) * P], z[:, u, t, :], m.ident[:, :])
                last.then_inc(xT_ready, 1)

            def hidden(u, n):
                pe.wait_ge(hT_ready, n + 1)
                pe.wait_ge(hb_ready, n + 1)
                for t in range(PAIR):
                    last = nc.tensor.matmul(ps_h[:, t, :], hT[:, u, t * P:(t + 1) * P], m.f0_w1[:, :],
                                            start=True, stop=True)
                last.then_inc(h_ready, 1)

            def turn_hidden(u, n):
                pe.wait_ge(gn_ready, n + 1)
                for t in range(PAIR):
                    for c in range(C):
                        last = nc.tensor.transpose(ps_g[:, t, c * P:(c + 1) * P], hid[:, u, t, c * P:(c + 1) * P],
                                                   m.ident[:, :])
                last.then_inc(tr_ready, 1)

            def result(u, n):
                pe.wait_ge(gT_ready, n + 1)
                pe.wait_ge(y_used, n + 1)
                for t in range(PAIR):
                    for c in range(C):
                        last = nc.tensor.matmul(ps_y[:, t * D:(t + 1) * D], gT[:, c, t * P:(t + 1) * P],
                                                m.f0_w2[:, c * D:(c + 1) * D], start=(c == 0), stop=(c == C - 1))
                last.then_inc(y_ready, 1)
            pipelined(pe, [(0, turn_hidden), (2, hidden), (0, result), (3, turn_tokens)])

        @block.scalar
        def _(act):
            nc.scalar.preload_act_table(ACT.Gelu)

            def move_tokens(u, n):
                act.wait_ge(xT_ready, n + 1)
                nc.scalar.activation(hT[:, u, :], ps_xT, ACT.Identity, bias=m.f0_ln1_b[:, 0:1],
                                     scale=m.f0_ln1_g[:, 0:1]).then_inc(hT_ready, 1)

            def gelu(u, n):
                act.wait_ge(hb_ready, n + 2)
                nc.scalar.activation(hid[:, u, :, :], hid[:, u, :, :], ACT.Gelu).then_inc(g_ready, 1)

            def move_hidden(u, n):
                act.wait_ge(tr_ready, n + 1)
                for c in range(C):
                    last = nc.scalar.activation(gT[:, c, :].rearrange("p (t f) -> p t f", t=PAIR),
                                                ps_g[:, :, c * P:(c + 1) * P], ACT.Identity,
                                                bias=m.f0_ln2_b[:, c:c + 1], scale=m.f0_ln2_g[:, c:c + 1])
                last.then_inc(gT_ready, 1)
            pipelined(act, [(1, gelu), (0, move_hidden), (3, move_tokens)])

        @block.vector
        def _(dve):
            dve.sem_inc(y_used, 1)
            dve.sem_inc(hb_ready, 1)

            def tokens_begin(u, n):
                norm_begin(nc, zn, lambda t: tile_of(m.XN, n, t))

            def tokens_end(u, n):
                norm_end(nc, dve, zn, n, lambda t: tile_of(m.XN, n, t), lambda t: z[:, u, t, :]).then_inc(z_ready, 1)

            def bias(u, n):
                dve.wait_ge(h_ready, n + 1)
                nc.vector.tensor_tensor(hid[:, u, :, :], ps_h, m.f0_b1[:, :, :], ALU.add).then_inc(hb_ready, 1)

            def hidden_begin(u, n):
                dve.wait_ge(g_ready, n + 1)
                norm_begin(nc, gn, lambda t: hid[:, u, t, :])

            def hidden_end(u, n):
                norm_end(nc, dve, gn, n, lambda t: hid[:, u, t, :], lambda t: hid[:, u, t, :]).then_inc(gn_ready, 1)

            def result_begin(u, n):
                dve.wait_ge(y_ready, n + 1)
                nc.vector.tensor_tensor(yb[:, :], ps_y, m.f0_b2[:, :], ALU.add).then_inc(y_used, 1)
                nc.vector.drain()
                residual_begin(nc, m, xn, n, yb[:, :], 0.5)

            def result_end(u, n):
                residual_end(nc, dve, m, xn, n)
            pipelined(dve, [(1, bias), (-1, result_end), (3, tokens_begin), (1, hidden_begin), (3, tokens_end),
                            (1, hidden_end), (0, result_begin)])

        @block.gpsimd
        def _(pool):
            power = lambda nm: lambda u, n: norm_power(nc, pool, m, nm, n)
            pipelined(pool, [(3, power(zn)), (1, power(gn)), (0, power(xn))])

        if issue_loads:
            @block.sync
            def _(sp):
                issue_loads(sp)


def route(nc, m, ctx, tag, w_gate, group, gate_bias=None, shared_gate=False, renormalise=False, bias2=None, split=False):
    E, E1 = 8, 9 if shared_gate else 8
    sb = lambda name, shape: ctx.enter_context(nc.sbuf_tensor(f"{tag}_{name}", shape, F32))
    sem = lambda name: signal(nc, ctx, f"{tag}_{name}")
    lg = sb("logits", [P, NT, E1])
    pr = sb("probs", [P, NT, E])
    left = sb("left", [P, NT, E])
    eq = sb("eq", [P, NT, E])
    mask = sb("mask", [P, NT, E])
    col = sb("col", [P, NT])
    gates_T = sb("gates_T", [P, P])
    XT = sb("XT", [P, NB * SEQ]) if split else m.XT
    tr_ready, xT_ready, lg_ready, sub_ready, exp_ready = (sem(k) for k in ("tr_ready", "xT_ready", "lg_ready", "sub_ready", "exp_ready"))
    gates_ready, gtr_ready, gT_ready, high_ready, low_ready = (
        sem(k) for k in ("gates_ready", "gtr_ready", "gT_ready", "high_ready", "low_ready"))
    ps_lg = m.psum[:, 4, 0:NT * E1].rearrange("p (t e) -> p t e", e=E1)
    ps_gT = m.psum[:, 6, 0:P]
    r = Record()
    wide = lambda v: v.unsqueeze(2).to_broadcast([P, NT, E])

    def tensor(pe):
        for q in range(4):
            for t in range(4):
                last = nc.tensor.transpose(m.psum[:, q, t * P:(t + 1) * P],
                                           m.XN[:, 2 * q + t // 2, (t % 2) * D:(t % 2 + 1) * D], m.ident[:, :])
            last.then_inc(tr_ready, 1)
        pe.wait_ge(m.loaded[group], m.total[group])
        for q in range(4):
            pe.wait_ge(xT_ready, q + 1)
            for t in range(4 * q, 4 * q + 4):
                last = nc.tensor.matmul(ps_lg[:, t, :], XT[:, t * P:(t + 1) * P], w_gate, start=True, stop=True)
        last.then_inc(lg_ready, 1)
        if split:
            pe.wait_ge(high_ready, 4)
            pe.wait_ge(low_ready, 4)

    def turn_gates(pe):
        pe.wait_ge(gates_ready, 1)
        nc.tensor.transpose(ps_gT, left[:, :, :].rearrange("p t e -> p (t e)"), m.ident[:, :]).then_inc(gtr_ready, 1)
        pe.wait_ge(gT_ready, 1)

    def scalar(act):
        nc.scalar.preload_act_table(ACT.Exp)
        for q in range(4):
            act.wait_ge(tr_ready, q + 1)
            nc.scalar.activation(XT[:, q * 512:(q + 1) * 512], m.psum[:, q, :], ACT.Copy).then_inc(xT_ready, 1)
            if split:
                nc.scalar.activation(m.XT_high[:, q * 512:(q + 1) * 512], m.psum[:, q, :], ACT.Copy).then_inc(high_ready, 1)
        act.wait_ge(sub_ready, 1)
        if shared_gate:
            nc.scalar.activation(lg[:, :, E], lg[:, :, E], ACT.Exp, scale=-1.0)
        nc.scalar.activation(pr[:, :, :], lg[:, :, 0:E], ACT.Exp).then_inc(exp_ready, 1)

    def vector(dve):
        dve.wait_ge(m.loaded[group], m.total[group])
        if bias2 is not None:
            for t in range(NT):
                nc.vector.tensor_scalar(m.bias2_of_tile[:, t * D:(t + 1) * D], bias2, m.tile_mask[:, t:t + 1], None, ALU.mult)
        if split:
            for q in range(4):
                dve.wait_ge(high_ready, q + 1)
                part = slice(q * 512, (q + 1) * 512)
                nc.vector.tensor_tensor(m.XT_low[:, part], XT[:, part], m.XT_high[:, part].bitcast(F32), ALU.subtract).then_inc(low_ready, 1)
        dve.wait_ge(lg_ready, 1)
        if gate_bias is not None:
            nc.vector.tensor_tensor(lg[:, :, :], ps_lg, gate_bias.unsqueeze(1).to_broadcast([P, NT, E1]), ALU.add)
        else:
            nc.vector.tensor_copy(lg[:, :, :], ps_lg)
        nc.vector.drain()
        nc.vector.tensor_reduce(col[:, :], lg[:, :, 0:E], AX.X, ALU.max)
        nc.vector.drain()
        nc.vector.tensor_tensor(lg[:, :, 0:E], lg[:, :, 0:E], wide(col[:, :]), ALU.subtract).then_inc(sub_ready, 1)
        dve.wait_ge(exp_ready, 1)
        nc.vector.tensor_reduce(col[:, :], pr[:, :, :], AX.X, ALU.add)
        if shared_gate:
            nc.vector.tensor_scalar(lg[:, :, E], lg[:, :, E], 1.0, None, ALU.add)
        nc.vector.drain()
        nc.vector.reciprocal(col[:, :], col[:, :])
        if shared_gate:
            nc.vector.reciprocal(m.gates[:, :, E], lg[:, :, E])
        nc.vector.drain()
        nc.vector.tensor_tensor(pr[:, :, :], pr[:, :, :], wide(col[:, :]), ALU.mult)
        nc.vector.drain()
        nc.vector.tensor_copy(left[:, :, :], pr[:, :, :])
        nc.vector.drain()
        for k in range(2):
            nc.vector.tensor_reduce(col[:, :], left[:, :, :], AX.X, ALU.max)
            nc.vector.drain()
            nc.vector.tensor_tensor(eq[:, :, :], left[:, :, :], wide(col[:, :]), ALU.is_equal)
            nc.vector.drain()
            nc.vector.tensor_tensor(eq[:, :, :], eq[:, :, :], m.countdown[:, :].unsqueeze(1).to_broadcast([P, NT, E]), ALU.mult)
            nc.vector.drain()
            nc.vector.tensor_reduce(col[:, :], eq[:, :, :], AX.X, ALU.max)
            nc.vector.drain()
            nc.vector.tensor_tensor(eq[:, :, :], eq[:, :, :], wide(col[:, :]), ALU.is_equal)
            nc.vector.drain()
            if k == 0:
                nc.vector.tensor_copy(mask[:, :, :], eq[:, :, :])
                nc.vector.scalar_tensor_tensor(out=left[:, :, :], in0=eq[:, :, :], scalar=-2.0, in1=left[:, :, :],
                                               op0=ALU.mult, op1=ALU.add)
            else:
                nc.vector.tensor_tensor(mask[:, :, :], mask[:, :, :], eq[:, :, :], ALU.add)
            nc.vector.drain()
        if renormalise:
            nc.vector.tensor_tensor(pr[:, :, :], pr[:, :, :], mask[:, :, :], ALU.mult)
            nc.vector.drain()
            nc.vector.tensor_reduce(col[:, :], pr[:, :, :], AX.X, ALU.add, apply_absolute_value=True)
            nc.vector.drain()
            nc.vector.tensor_scalar(col[:, :], col[:, :], 1e-12, None, ALU.max)
            nc.vector.drain()
            nc.vector.reciprocal(col[:, :], col[:, :])
            nc.vector.drain()
            nc.vector.tensor_tensor(m.gates[:, :, 0:E], pr[:, :, :], wide(col[:, :]), ALU.mult)
            last = nc.vector.tensor_tensor(left[:, :, :], pr[:, :, :], wide(col[:, :]), ALU.mult)
        else:
            last = nc.vector.tensor_tensor(m.gates[:, :, 0:E], pr[:, :, :], mask[:, :, :], ALU.mult)
        last.then_inc(gates_ready, 1)
        if bias2 is not None:
            dve.wait_ge(gtr_ready, 1)
            nc.vector.tensor_copy(gates_T[:, :], ps_gT).then_inc(gT_ready, 1)
        nc.vector.drain()
    r.tensor, r.scalar, r.vector, r.turn_gates, r.gates_T = tensor, scalar, vector, turn_gates, gates_T
    return r


def split_weights(nc, m, stack, group, raw):
    high, low = (stack.enter_context(nc.sbuf_tensor(f"{group}_{k}", raw.shape, F32R)) for k in ("high", "low"))
    with ExitStack() as ctx:
        high_ready = signal(nc, ctx, group + "_high_ready")
        block = ctx.enter_context(nc.Block())
        parts = range(0, raw.shape[1], 2)

        @block.scalar
        def _(act):
            act.wait_ge(m.loaded[group], m.total[group])
            for e in parts:
                nc.scalar.activation(high[:, e:e + 2, :], raw[:, e:e + 2, :], ACT.Copy).then_inc(high_ready, 1)

        @block.vector
        def _(dve):
            for e in parts:
                dve.wait_ge(high_ready, e // 2 + 1)
                nc.vector.tensor_tensor(low[:, e:e + 2, :], raw[:, e:e + 2, :], high[:, e:e + 2, :].bitcast(F32), ALU.subtract)
    clear_signals(nc)
    return high, low


def expert_steps(eng, count, step):
    for e in range(count):
        step(0, e, False, False)
    with eng.Fori(1, NB - 1) as n:
        for e in range(count):
            step(n, e, False, True)
    for e in range(count):
        step(NB - 1, e, e == count - 1, True)


def tokens_T(m, n):
    return m.XT[:, bass.ds(n * SEQ, SEQ)]


def split_tokens_T(m, n):
    return m.XT_high[:, bass.ds(n * SEQ, SEQ)], m.XT_low[:, bass.ds(n * SEQ, SEQ)]


def gates_of(m, n):
    return m.gates[:, bass.ds(n * PAIR, PAIR), :]


def moe_gated(nc, m, tag, issue_loads=None):
    S, I2 = 10, 88
    with ExitStack() as ctx:
        m.XT_high, m.XT_low = (ctx.enter_context(nc.sbuf_tensor(f"{tag}_XT_{k}", [P, NB * SEQ], F32R)) for k in ("high", "low"))
        routing = route(nc, m, ctx, tag + "r", m.m1_gate[:, :], "m1", shared_gate=True, split=True)
        sb = lambda name, shape: ctx.enter_context(nc.sbuf_tensor(f"{tag}_{name}", shape, F32))
        sem = lambda name: signal(nc, ctx, f"{tag}_{name}")
        silu = sb("silu", [I2, 2, 2 * SEQ])
        hid = sb("hid", [I2, 2, 2 * SEQ])
        gates = sb("gates", [P, PAIR, 9])
        acc = sb("acc", [P, PAIR * D])
        xn = make_norm(nc, ctx, f"{tag}_xn")
        up_ready, silu_ready, hid_ready, y_ready, y_used = (sem(k) for k in ("up_ready", "silu_ready", "hid_ready", "y_ready", "y_used"))
        ps_up = lambda s: m.psum[0:I2, 2 * s:2 * s + 2, :].rearrange("p b f -> p (b f)")
        ps_y = lambda s: m.psum[:, 4 + s, 0:PAIR * D]
        block = ctx.enter_context(nc.Block())

        @block.tensor
        def _(pe):
            def up(n, e):
                for k in range(4):
                    last = split_matmul(nc, ps_up(e % 2)[:, k * SEQ:(k + 1) * SEQ], [w[:, e, k * I2:(k + 1) * I2] for w in m.m1_up],
                                        split_tokens_T(m, n))
                last.then_inc(up_ready, 1)

            def step(n, e, last_step, has_prev):
                if e < S - 1:
                    up(n, e + 1)
                elif not last_step:
                    up(n + 1, 0)
                pe.wait_ge(hid_ready, n * S + e + 1)
                pe.wait_ge(y_used, n * S + e + 1)
                for t in range(PAIR):
                    for k in range(2):
                        last = nc.tensor.matmul(ps_y(e % 2)[:, t * D:(t + 1) * D], hid[:, e % 2, k * SEQ + t * P:k * SEQ + (t + 1) * P],
                                                m.m1_down[:, e, k, :], start=(k == 0), stop=(k == 1))
                last.then_inc(y_ready, 1)
            routing.tensor(pe)
            up(0, 0)
            expert_steps(pe, S, step)

        @block.scalar
        def _(act):
            routing.scalar(act)
            nc.scalar.preload_act_table(ACT.Silu)

            def step(n, e, last_step, has_prev):
                act.wait_ge(up_ready, n * S + e + 1)
                nc.scalar.activation(silu[:, e % 2, :], ps_up(e % 2)[:, 0:2 * SEQ], ACT.Silu).then_inc(silu_ready, 1)
            expert_steps(act, S, step)

        @block.vector
        def _(dve):
            dve.sem_inc(y_used, 2)

            def add(n, e, last_step):
                dve.wait_ge(y_ready, n * S + e + 1)
                g = min(e, 8)
                for t in range(PAIR):
                    y, a = ps_y(e % 2)[:, t * D:(t + 1) * D], acc[:, t * D:(t + 1) * D]
                    if e == 0:
                        last = nc.vector.tensor_scalar(a, y, gates[:, t, g:g + 1], None, ALU.mult)
                    else:
                        last = nc.vector.scalar_tensor_tensor(out=a, in0=y, scalar=gates[:, t, g:g + 1], in1=a,
                                                              op0=ALU.mult, op1=ALU.add)
                last.then_inc(y_used, 1)
                if e == S - 1:
                    nc.vector.drain()
                    residual_begin(nc, m, xn, n, acc[:, :], 0.5)
                    if last_step:
                        residual_end(nc, dve, m, xn, n)

            def step(n, e, last_step, has_prev):
                dve.wait_ge(silu_ready, n * S + e + 1)
                nc.vector.tensor_tensor(hid[:, e % 2, :], silu[:, e % 2, :], ps_up(e % 2)[:, 2 * SEQ:4 * SEQ], ALU.mult).then_inc(hid_ready, 1)
                nc.vector.drain()
                if e:
                    add(n, e - 1, False)
                else:
                    if has_prev:
                        add(n - 1, S - 1, False)
                    nc.vector.tensor_copy(gates[:, :, :], gates_of(m, n))
                if e == 2 and has_prev:
                    residual_end(nc, dve, m, xn, n - 1)
                if last_step:
                    nc.vector.drain()
                    add(n, e, True)
            routing.vector(dve)
            expert_steps(dve, S, step)

        @block.gpsimd
        def _(pool):
            with pool.Fori(0, NB) as n:
                norm_power(nc, pool, m, xn, n)

        if issue_loads:
            @block.sync
            def _(sp):
                issue_loads(sp)


def moe_gelu(nc, m, tag):
    S, C = 8, 4
    with ExitStack() as ctx:
        m.XT_high, m.XT_low = (ctx.enter_context(nc.sbuf_tensor(f"{tag}_XT_{k}", [P, NB * SEQ], F32R)) for k in ("high", "low"))
        routing = route(nc, m, ctx, tag + "r", m.m2_gate[:, :], "m2", gate_bias=m.m2_gate_b[:, :], renormalise=True,
                        bias2=m.m2_b2[:, :], split=True)
        sb = lambda name, shape: ctx.enter_context(nc.sbuf_tensor(f"{tag}_{name}", shape, F32))
        sem = lambda name: signal(nc, ctx, f"{tag}_{name}")
        hid = sb("hid", [P, 2, C * SEQ])
        gates = sb("gates", [P, PAIR, 9])
        acc = sb("acc", [P, PAIR * D])
        xn = make_norm(nc, ctx, f"{tag}_xn")
        up_ready, hid_ready, y_ready, y_used, bias_ready = (sem(k) for k in ("up_ready", "hid_ready", "y_ready", "y_used", "bias_ready"))
        ps_bias = m.psum[:, 7, 0:PAIR * D]
        ps_up = lambda s: m.psum[:, 2 * s:2 * s + 2, :].rearrange("p b f -> p (b f)")
        ps_y = lambda s: m.psum[:, 4 + s, 0:PAIR * D]
        block = ctx.enter_context(nc.Block())

        @block.tensor
        def _(pe):
            def up(n, e):
                for c in range(C):
                    last = split_matmul(nc, ps_up(e % 2)[:, c * SEQ:(c + 1) * SEQ], [w[:, e, c * P:(c + 1) * P] for w in m.m2_w1],
                                        split_tokens_T(m, n))
                last.then_inc(up_ready, 1)

            def step(n, e, last_step, has_prev):
                if e < S - 1:
                    up(n, e + 1)
                elif not last_step:
                    up(n + 1, 0)
                if e == 0:
                    if not has_prev:
                        routing.turn_gates(pe)
                    nc.tensor.matmul(ps_bias, routing.gates_T[:, :], m.bias2_of_tile[:, bass.ds(n * PAIR * D, PAIR * D)],
                                     start=True, stop=True).then_inc(bias_ready, 1)
                pe.wait_ge(hid_ready, n * S + e + 1)
                pe.wait_ge(y_used, n * S + e + 1)
                for t in range(PAIR):
                    for c in range(C):
                        last = nc.tensor.matmul(ps_y(e % 2)[:, t * D:(t + 1) * D], hid[:, e % 2, c * SEQ + t * P:c * SEQ + (t + 1) * P],
                                                m.m2_w2[:, e, c, :], start=(c == 0), stop=(c == C - 1))
                last.then_inc(y_ready, 1)
            routing.tensor(pe)
            up(0, 0)
            expert_steps(pe, S, step)

        @block.scalar
        def _(act):
            routing.scalar(act)
            nc.scalar.preload_act_table(ACT.Gelu)

            def step(n, e, last_step, has_prev):
                act.wait_ge(up_ready, n * S + e + 1)
                for c in range(C):
                    last = nc.scalar.activation(hid[:, e % 2, c * SEQ:(c + 1) * SEQ], ps_up(e % 2)[:, c * SEQ:(c + 1) * SEQ],
                                                ACT.Gelu, bias=m.m2_b1[:, e * C + c:e * C + c + 1])
                last.then_inc(hid_ready, 1)
            expert_steps(act, S, step)

        @block.vector
        def _(dve):
            dve.sem_inc(y_used, 2)

            def step(n, e, last_step, has_prev):
                if e == 0:
                    nc.vector.tensor_copy(gates[:, :, :], gates_of(m, n))
                    dve.wait_ge(bias_ready, n + 1)
                    nc.vector.tensor_copy(acc[:, :], ps_bias)
                nc.vector.drain()
                dve.wait_ge(y_ready, n * S + e + 1)
                for t in range(PAIR):
                    a = acc[:, t * D:(t + 1) * D]
                    last = nc.vector.scalar_tensor_tensor(out=a, in0=ps_y(e % 2)[:, t * D:(t + 1) * D], scalar=gates[:, t, e:e + 1],
                                                          in1=a, op0=ALU.mult, op1=ALU.add)
                last.then_inc(y_used, 1)
                if e == S - 1:
                    nc.vector.drain()
                    residual_begin(nc, m, xn, n, acc[:, :], 0.5)
                    if last_step:
                        residual_end(nc, dve, m, xn, n)
                if e == 1 and has_prev:
                    residual_end(nc, dve, m, xn, n - 1)
            routing.vector(dve)
            expert_steps(dve, S, step)

        @block.gpsimd
        def _(pool):
            with pool.Fori(0, NB) as n:
                norm_power(nc, pool, m, xn, n)


def moe_common(nc, m, tag):
    E = 8
    with ExitStack() as ctx:
        routing = route(nc, m, ctx, tag + "r", m.m3_gate[:, :], "m3", gate_bias=m.m3_gate_b[:, :])
        sb = lambda name, shape: ctx.enter_context(nc.sbuf_tensor(f"{tag}_{name}", shape, F32))
        sem = lambda name: signal(nc, ctx, f"{tag}_{name}")
        silu = sb("silu", [P, 2, 2 * SEQ])
        hid = sb("hid", [P, 2, 2 * SEQ])
        gates = sb("gates", [P, 2, PAIR, 9])
        prod = sb("prod", [P, PAIR, E + 1, D])
        acc = sb("acc", [P, PAIR * D])
        xn = make_norm(nc, ctx, f"{tag}_xn")
        up_ready, silu_ready, hid_ready, y_ready, shared_used, prod_ready, prod_used = (
            sem(k) for k in ("up_ready", "silu_ready", "hid_ready", "y_ready", "shared_used", "prod_ready", "prod_used"))
        ps_up = m.psum[:, 0:2, :].rearrange("p b f -> p (b f)")
        ps_y = lambda t: m.psum[:, 2 + 2 * t:4 + 2 * t, :].rearrange("p b f -> p (b f)")
        ps_s = lambda t: m.psum[:, 6 + t, 0:D]
        block = ctx.enter_context(nc.Block())

        @block.tensor
        def _(pe):
            def up(u, n):
                pe.wait_ge(hid_ready, n + 1)
                for k in range(4):
                    last = nc.tensor.matmul(ps_up[:, k * SEQ:(k + 1) * SEQ], m.m3_up[:, k * P:(k + 1) * P],
                                            tokens_T(m, n), start=True, stop=True)
                last.then_inc(up_ready, 1)

            def down(u, n):
                pe.wait_ge(hid_ready, n + 2)
                for t in range(PAIR):
                    pe.wait_ge(shared_used, PAIR * n + t + 1)
                    pe.wait_ge(prod_ready, PAIR * n + t + 1)
                    nc.tensor.matmul(ps_s(t), hid[:, u, SEQ + t * P:SEQ + (t + 1) * P], m.m3_shared_out[:, :], start=True, stop=True)
                    for k in range(2):
                        last = nc.tensor.matmul(ps_y(t)[:, k * 512:(k + 1) * 512], hid[:, u, t * P:(t + 1) * P],
                                                m.m3_w2[:, k * 512:(k + 1) * 512], start=True, stop=True)
                    last.then_inc(y_ready, 1)
            routing.tensor(pe)
            pipelined(pe, [(0, down), (2, up)])

        @block.scalar
        def _(act):
            routing.scalar(act)
            nc.scalar.preload_act_table(ACT.Silu)

            def silus(u, n):
                act.wait_ge(up_ready, n + 1)
                nc.scalar.activation(silu[:, u, :], ps_up[:, 0:2 * SEQ], ACT.Silu).then_inc(silu_ready, 1)

            def gating(u, n):
                for t in range(PAIR):
                    act.wait_ge(y_ready, PAIR * n + t + 1)
                    act.wait_ge(prod_used, PAIR * n + t + 1)
                    for e in range(E):
                        last = nc.scalar.activation(prod[:, t, e, :], ps_y(t)[:, e * D:(e + 1) * D], ACT.Copy, scale=gates[:, u, t, e:e + 1])
                    last.then_inc(prod_ready, 1)
            pipelined(act, [(0, gating), (2, silus)])

        @block.vector
        def _(dve):
            dve.sem_inc(hid_ready, 1)
            dve.sem_inc(shared_used, PAIR)
            dve.sem_inc(prod_ready, PAIR)
            dve.sem_inc(prod_used, PAIR)

            def hidden(u, n):
                nc.vector.tensor_copy(gates[:, u, :, :], gates_of(m, n))
                dve.wait_ge(silu_ready, n + 1)
                nc.vector.tensor_tensor(hid[:, u, :], silu[:, u, :], ps_up[:, 2 * SEQ:4 * SEQ], ALU.mult).then_inc(hid_ready, 1)

            def result_begin(u, n):
                for t in range(PAIR):
                    dve.wait_ge(y_ready, PAIR * n + t + 1)
                    nc.vector.tensor_copy(prod[:, t, E, :], ps_s(t)).then_inc(shared_used, 1)
                    nc.vector.drain()
                    dve.wait_ge(prod_ready, PAIR * n + t + 3)
                    nc.vector.tensor_reduce(acc[:, t * D:(t + 1) * D], prod[:, t, :, :].rearrange("p e d -> p d e"),
                                            AX.X, ALU.add).then_inc(prod_used, 1)
                nc.vector.drain()
                residual_begin(nc, m, xn, n, acc[:, :], 0.5)

            def result_end(u, n):
                residual_end(nc, dve, m, xn, n)
            routing.vector(dve)
            pipelined(dve, [(0, result_begin), (2, hidden), (0, result_end)])

        @block.gpsimd
        def _(pool):
            with pool.Fori(0, NB) as n:
                norm_power(nc, pool, m, xn, n)


def state_space(nc, m, tag):
    I2, HALVES, S = 96, 2, 8
    STEP = 16
    CH = SEQ // STEP
    WIDE = HALVES * NB * S
    xs = m.arena[0:I2, 0:2, :]
    gate = m.arena[0:I2, 2:4, :]
    xs_t = xs.rearrange("p c (b t) -> p c b t", b=NB)
    with ExitStack() as ctx:
        sb = lambda name, shape: ctx.enter_context(nc.sbuf_tensor(f"{tag}_{name}", shape, F32))
        sem = lambda name: signal(nc, ctx, f"{tag}_{name}")
        decay = sb("decay", [I2, HALVES, NB, S])
        cw = sb("cw", [I2, HALVES, NB, S])
        bw = sb("bw", [I2, HALVES, S])

        with ExitStack() as part:
            sbp = lambda name, shape: part.enter_context(nc.sbuf_tensor(f"{tag}p_{name}", shape, F32))
            semp = lambda name: signal(nc, part, f"{tag}p_{name}")
            z = sbp("z", [P, 2, PAIR, D])
            hT = sbp("hT", [P, 2, SEQ])
            gc = sbp("gc", [I2, 2, HALVES, SEQ])
            dk = sbp("dk", [I2, HALVES * S])
            zn = make_norm(nc, part, f"{tag}_zn")
            z_ready, xT_ready, hT_ready, p_ready, clip_ready, gate_ready = (
                semp(k) for k in ("z_ready", "xT_ready", "hT_ready", "p_ready", "clip_ready", "gate_ready"))
            alog_ready, exp_ready = semp("alog_ready"), semp("exp_ready")
            ps_xT = lambda u: m.psum[:, 5 + u, 0:SEQ]
            ps_p = lambda u: m.psum[0:I2, 1 + 2 * u:3 + 2 * u, :].rearrange("p b (c f) -> p (b c) f", c=2)
            block = part.enter_context(nc.Block())

            @block.tensor
            def _(pe):
                def turn(u, n):
                    pe.wait_ge(z_ready, n + 1)
                    for t in range(PAIR):
                        last = nc.tensor.transpose(ps_xT(u)[:, t * P:(t + 1) * P], z[:, u, t, :], m.ident[:, :])
                    last.then_inc(xT_ready, 1)

                def project(u, n):
                    pe.wait_ge(hT_ready, n + 1)
                    pe.wait_ge(clip_ready, n + 1)
                    for c in range(4):
                        last = nc.tensor.matmul(ps_p(u)[:, c, :], m.a1_in[:, c * I2:(c + 1) * I2], hT[:, u, :],
                                                start=True, stop=True)
                    last.then_inc(p_ready, 1)
                pipelined(pe, [(1, project), (2, turn)])

            @block.scalar
            def _(act):
                nc.scalar.preload_act_table(ACT.Exp)
                act.wait_ge(m.loaded["a1"], m.total["a1"])
                act.wait_ge(alog_ready, 1)
                nc.scalar.activation(dk[:, :], dk[:, :], ACT.Exp).then_inc(exp_ready, 1)

                def move(u, n):
                    act.wait_ge(xT_ready, n + 1)
                    nc.scalar.activation(hT[:, u, :], ps_xT(u), ACT.Identity, bias=m.a1_in_b[:, 0:1],
                                         scale=m.a1_in_g[:, 0:1]).then_inc(hT_ready, 1)

                def tanh(u, n):
                    act.wait_ge(clip_ready, n + 3)
                    nc.scalar.activation(gate[:, :, bass.ds(n * SEQ, SEQ)], gc[:, u, :, :], ACT.Tanh).then_inc(gate_ready, 1)
                pipelined(act, [(0, tanh), (2, move)])

            @block.vector
            def _(dve):
                dve.sem_inc(clip_ready, 2)
                dve.sem_inc(gate_ready, 2)
                dve.wait_ge(m.loaded["a1"], m.total["a1"])
                nc.vector.tensor_scalar(dk[:, :], m.a1_alog[:, :], -5.0, 0.0, ALU.max, ALU.min).then_inc(alog_ready, 1)
                dve.wait_ge(exp_ready, 1)
                nc.vector.tensor_scalar(dk[:, :], dk[:, :], -1.0, -2.0, ALU.mult, ALU.max)
                nc.vector.drain()
                nc.vector.tensor_scalar(dk[:, :], dk[:, :], -0.01, 0.9, ALU.min, ALU.mult)
                nc.vector.drain()
                state = lambda v: v.rearrange("p (c s) -> p c s", c=HALVES).unsqueeze(2).to_broadcast([I2, HALVES, NB, S])
                nc.vector.tensor_copy(decay[:, :, :, :], state(dk[:, :]))
                nc.vector.tensor_copy(cw[:, :, :, :], state(m.a1_c[:, :]))
                nc.vector.tensor_scalar(bw[:, :, :].rearrange("p c s -> p (c s)"), m.a1_b[:, :], 0.1, None, ALU.mult)

                def tokens_begin(u, n):
                    norm_begin(nc, zn, lambda t: tile_of(m.XN, n, t))

                def tokens_end(u, n):
                    norm_end(nc, dve, zn, n, lambda t: tile_of(m.XN, n, t), lambda t: z[:, u, t, :]).then_inc(z_ready, 1)

                def clip(u, n):
                    dve.wait_ge(p_ready, n + 1)
                    nc.vector.tensor_scalar(xs[:, :, bass.ds(n * SEQ, SEQ)], ps_p(u)[:, 0:2, :], 5.0, -5.0, ALU.min, ALU.max)
                    dve.wait_ge(gate_ready, n + 1)
                    nc.vector.tensor_scalar(gc[:, u, :, :], ps_p(u)[:, 2:4, :], 5.0, -5.0, ALU.min, ALU.max).then_inc(clip_ready, 1)
                pipelined(dve, [(2, tokens_begin), (0, clip), (2, tokens_end)])

            @block.gpsimd
            def _(pool):
                with pool.Fori(0, NB) as n:
                    norm_power(nc, pool, m, zn, n)

        with ExitStack() as part:
            sbp = lambda name, shape: part.enter_context(nc.sbuf_tensor(f"{tag}s_{name}", shape, F32))
            semp = lambda name: signal(nc, part, f"{tag}s_{name}")
            drive = sbp("drive", [I2, 2, STEP, WIDE])
            hist = sbp("hist", [I2, 2, STEP, WIDE])
            read = sbp("read", [I2, STEP, WIDE])
            drive_ready, states_used = semp("drive_ready"), semp("states_used")
            done = [semp("done0"), semp("done1")]
            block = part.enter_context(nc.Block())

            @block.vector
            def _(dve):
                dve.sem_inc(states_used, 2)
                nc.vector.memset(hist[:, 1, STEP - 1, :], 0.0)
                nc.vector.drain()
                dec = decay[:, :, :, :].rearrange("p c b s -> p (c b s)")
                parts = [slice(c * WIDE // 2, (c + 1) * WIDE // 2) for c in range(2)]
                for c in range(2):
                    dve.sem_inc(done[c], 1)
                with dve.Fori(0, CH // 2) as i:
                    for u in range(2):
                        dve.wait_ge(drive_ready, 2 * i + u + 1)
                        dve.wait_ge(states_used, 2 * i + u + 1)
                        for t in range(STEP):
                            ops = 3 * (2 * STEP * i + STEP * u + t)
                            before = hist[:, u, t - 1, :] if t else hist[:, 1 - u, STEP - 1, :]
                            now = hist[:, u, t, :]
                            for c, part in enumerate(parts):
                                dve.wait_ge(done[c], ops + 1)
                                nc.vector.tensor_tensor(now[:, part], before[:, part], dec[:, part], ALU.mult).then_inc(done[c], 1)
                            for c, part in enumerate(parts):
                                dve.wait_ge(done[c], ops + 2)
                                nc.vector.tensor_tensor(now[:, part], now[:, part], drive[:, u, t, part], ALU.add).then_inc(done[c], 1)
                            for c, part in enumerate(parts):
                                dve.wait_ge(done[c], ops + 3)
                                nc.vector.tensor_scalar(now[:, part], now[:, part], 5.0, -5.0, ALU.min, ALU.max).then_inc(done[c], 1)

            @block.gpsimd
            def _(pool):
                def inputs(u, k):
                    for c in range(HALVES):
                        last = nc.gpsimd.tensor_tensor(
                            drive[:, u, :, c * NB * S:(c + 1) * NB * S].rearrange("p t (b s) -> p t b s", b=NB),
                            xs_t[:, c, :, bass.ds(k * STEP, STEP)].rearrange("p b t -> p t b").unsqueeze(3).to_broadcast([I2, STEP, NB, S]),
                            bw[:, c, :].unsqueeze(1).unsqueeze(1).to_broadcast([I2, STEP, NB, S]), ALU.mult)
                    last.then_inc(drive_ready, 1)

                def outputs(u, k):
                    for c in range(2):
                        pool.wait_ge(done[c], 3 * STEP * (k + 1) + 1)
                    nc.gpsimd.tensor_tensor(read[:, :, :], hist[:, u, :, :],
                                            cw[:, :, :, :].rearrange("p c b s -> p (c b s)").unsqueeze(1).to_broadcast([I2, STEP, WIDE]),
                                            ALU.mult).then_inc(states_used, 1)
                    nc.gpsimd.drain()
                    r = read[:, :, :].rearrange("p t (g s) -> p (t g) s", s=S)
                    nc.gpsimd.tensor_tensor(r[:, :, 0:4], r[:, :, 0:4], r[:, :, 4:8], ALU.add)
                    nc.gpsimd.drain()
                    nc.gpsimd.tensor_tensor(r[:, :, 0:2], r[:, :, 0:2], r[:, :, 2:4], ALU.add)
                    nc.gpsimd.drain()
                    r = read[:, :, :].rearrange("p t (c b s) -> p c b t s", c=HALVES, b=NB)
                    for c in range(HALVES):
                        nc.gpsimd.tensor_tensor(xs_t[:, c, :, bass.ds(k * STEP, STEP)], r[:, c, :, :, 0], r[:, c, :, :, 1], ALU.add)
                    nc.gpsimd.drain()

                inputs(0, 0)
                with pool.Fori(0, CH // 2 - 1) as i:
                    inputs(1, 2 * i + 1)
                    outputs(0, 2 * i)
                    inputs(0, 2 * i + 2)
                    outputs(1, 2 * i + 1)
                inputs(1, CH - 1)
                outputs(0, CH - 2)
                outputs(1, CH - 1)

        with ExitStack() as part:
            sbp = lambda name, shape: part.enter_context(nc.sbuf_tensor(f"{tag}o_{name}", shape, F32))
            semp = lambda name: signal(nc, part, f"{tag}o_{name}")
            gated = sbp("gated", [I2, 2, HALVES, SEQ])
            o = sbp("o", [P, PAIR, D])
            on, xn = make_norm(nc, part, f"{tag}_on"), make_norm(nc, part, f"{tag}_xn")
            gated_ready, y_ready = semp("gated_ready"), semp("y_ready")
            ps_y = lambda u: m.psum[:, u, 0:PAIR * D].rearrange("p (t f) -> p t f", t=PAIR)
            block = part.enter_context(nc.Block())

            @block.vector
            def _(dve):
                def gating(u, n):
                    nc.vector.tensor_scalar(gated[:, u, :, :], xs[:, :, bass.ds(n * SEQ, SEQ)], 5.0, -5.0, ALU.min, ALU.max)
                    nc.vector.drain()
                    nc.vector.tensor_tensor(gated[:, u, :, :], gated[:, u, :, :], gate[:, :, bass.ds(n * SEQ, SEQ)], ALU.mult).then_inc(gated_ready, 1)

                def norm_out(u, n):
                    dve.wait_ge(y_ready, n + 1)
                    nc.vector.tensor_scalar(o[:, :, :], ps_y(u), 5.0, -5.0, ALU.min, ALU.max)
                    nc.vector.drain()
                    norm_begin(nc, on, lambda t: o[:, t, :])

                def result_begin(u, n):
                    for t in range(PAIR):
                        nc.vector.scalar_tensor_tensor(out=o[:, t, :], in0=o[:, t, :], scalar=on.mv[:, t, 0:1], in1=m.a1_out_g[:, :],
                                                       op0=ALU.subtract, op1=ALU.mult)
                    nc.vector.drain()
                    dve.wait_ge(on.inv_ready, n + 1)
                    for t in range(PAIR):
                        nc.vector.scalar_tensor_tensor(out=o[:, t, :], in0=o[:, t, :], scalar=on.inv[:, t:t + 1], in1=m.a1_out_b[:, :],
                                                       op0=ALU.mult, op1=ALU.add)
                    nc.vector.drain()
                    residual_begin(nc, m, xn, n, o[:, :, :].rearrange("p t f -> p (t f)"), 1.0)

                def result_end(u, n):
                    residual_end(nc, dve, m, xn, n)
                pipelined(dve, [(0, norm_out), (2, gating), (-1, result_end), (0, result_begin)])

            @block.tensor
            def _(pe):
                def unit(u, n):
                    pe.wait_ge(gated_ready, n + 1)
                    for t in range(PAIR):
                        for c in range(HALVES):
                            last = nc.tensor.matmul(ps_y(u)[:, t, :], gated[:, u, c, t * P:(t + 1) * P], m.a1_out[:, c, :],
                                                    start=(c == 0), stop=(c == HALVES - 1))
                    last.then_inc(y_ready, 1)
                pipelined(pe, [(0, unit)])

            @block.gpsimd
            def _(pool):
                with pool.Fori(0, NB) as n:
                    norm_power(nc, pool, m, on, n)
                    norm_power(nc, pool, m, xn, n)


def threaded(eng, first, unit, tail):
    first()
    unit(0, 0, False, True)
    with eng.Fori(0, NB // 2 - 1) as i:
        unit(1, 2 * i + 1, True, True)
        unit(0, 2 * i + 2, True, True)
    unit(1, NB - 1, True, False)
    tail(1, NB - 1)


def grouped_attention(nc, m, tag, local):
    HEADS, KV, HD, GROUPS = 16, 4, 8, 8
    QK = HEADS + KV
    Q1 = 160 - P if local else P
    W0 = P + Q1
    W = W0 + P
    VW = HD + 1
    STREAM = SEQ - (HEADS - 1) * VW
    VPAD = (KV - 1) * VW + STREAM
    w = m.a0l if local else m.a0g
    src = m.H1 if local else m.XN
    with ExitStack() as ctx:
        sb = lambda name, shape: ctx.enter_context(nc.sbuf_tensor(f"{tag}_{name}", shape, F32))
        sem = lambda name: signal(nc, ctx, f"{tag}_{name}")
        r = sb("r", [P, PAIR, D])
        xT = sb("xT", [P, SEQ])
        lat = sb("lat", [32, SEQ])
        rot = sb("rot", [P, PAIR, QK * HD])
        tmp = sb("tmp", [P, 2, PAIR, QK, HD // 2])
        ss = sb("ss", [P, PAIR * QK])
        inv = sb("inv", [P, PAIR * QK])
        qn = sb("qn", [P, PAIR, D])
        kn = sb("kn", [P, PAIR, D])
        qT = sb("qT", [P, 2, KV, SEQ])
        kT = sb("kT", [P, 2, 4, SEQ])
        va = sb("va", [P, 2, PAIR, VPAD])
        pT = sb("pT", [P, 4, 2, W])
        rec = sb("rec", [P, PAIR * HEADS])
        o = sb("o", [P, PAIR, HEADS, HD])
        oT = sb("oT", [P, SEQ])
        r2 = sb("r2", [P, PAIR * D])
        rn, xn = make_norm(nc, ctx, f"{tag}_rn"), make_norm(nc, ctx, f"{tag}_xn")
        r_ready, rT_ready, xT_ready, lat_ready, latT_ready, p_ready = (sem(k) for k in ("r_ready", "rT_ready", "xT_ready", "lat_ready", "latT_ready", "p_ready"))
        ss_ready, ssinv_ready, qk_ready, qkT_ready, qT_ready, kT_ready = (sem(k) for k in ("ss_ready", "ssinv_ready", "qk_ready", "qkT_ready", "qT_ready", "kT_ready"))
        s_ready, e_ready, masked, av_ready, o_ready, otr_ready, oT_ready, y_ready = (sem(k) for k in ("s_ready", "e_ready", "masked", "av_ready", "o_ready", "otr_ready", "oT_ready", "y_ready"))
        ps_s = lambda g: m.psum[:, 2 * (g % 2):2 * (g % 2) + 2, :]
        ps_a, ps_b = m.psum[:, 4, 0:SEQ], m.psum[:, 5, 0:PAIR * 192].rearrange("p (t f) -> p t f", t=PAIR)
        ps_av = lambda t, slot: m.psum[:, 6, 256 * t + slot * VW:256 * t + slot * VW + STREAM]
        av_heads = m.psum[:, 6, :].rearrange("p (t f) -> p t f", t=PAIR)[:, :, 0:HEADS * VW].rearrange("p t (s f) -> p t s f", f=VW)
        ps_o = m.psum[:, 7, 0:SEQ]
        ps_y = m.psum[:, 7, 256:512]
        heads_of = lambda g: [(2 * (g % 2) + k, g // 2) for k in range(2)]
        block = ctx.enter_context(nc.Block())

        @block.tensor
        def _(pe):
            def start_a(u, n):
                pe.wait_ge(r_ready, n + 1)
                for t in range(PAIR):
                    last = nc.tensor.transpose(ps_a[:, t * P:(t + 1) * P], r[:, t, :], m.ident[:, :])
                last.then_inc(rT_ready, 1)

            def start_b(u, n):
                pe.wait_ge(xT_ready, n + 1)
                if not local:
                    nc.tensor.matmul(ps_a[0:32, :], w.down[:, :], xT[:, :], start=True, stop=True).then_inc(lat_ready, 1)
                else:
                    for t in range(PAIR):
                        last = nc.tensor.matmul(ps_b[:, t, :], xT[:, t * P:(t + 1) * P], w.qkv[:, :], start=True, stop=True)
                    last.then_inc(p_ready, 1)

            def start_c(u, n):
                if not local:
                    pe.wait_ge(latT_ready, n + 1)
                    for t in range(PAIR):
                        nc.tensor.matmul(ps_b[:, t, 0:P], xT[:, t * P:(t + 1) * P], w.q[:, :], start=True, stop=True)
                        last = nc.tensor.matmul(ps_b[:, t, P:192], lat[:, t * P:(t + 1) * P], w.kv[:, :], start=True, stop=True)
                    last.then_inc(p_ready, 1)

            def start_d(u, n):
                pe.wait_ge(qk_ready, n + 1)
                for t in range(PAIR):
                    nc.tensor.transpose(ps_a[:, t * P:(t + 1) * P], qn[:, t, :], m.ident[:, :])
                    last = nc.tensor.transpose(m.psum[:, 5, t * P:(t + 1) * P], kn[:, t, :], m.ident[:, :])
                last.then_inc(qkT_ready, 1)

            def scores(u, n, g):
                for k, (kv, j) in enumerate(heads_of(g)):
                    nc.tensor.matmul(ps_s(g)[:, k, 0:W0], kT[:, u, j, 0:P], qT[:, u, kv, 0:W0], start=True, stop=True)
                    last = nc.tensor.matmul(ps_s(g)[:, k, W0:W], kT[:, u, j, P:SEQ], qT[:, u, kv, P:SEQ], start=True, stop=True)
                last.then_inc(s_ready, 1)

            def values(u, n, g):
                pe.wait_ge(masked, GROUPS * n + g + 1)
                for k, (kv, j) in enumerate(heads_of(g)):
                    slot = 2 * g + k
                    p = pT[:, g % 4, k, :]
                    v = lambda t: va[:, u, t, kv * VW:kv * VW + STREAM]
                    nc.tensor.matmul(ps_av(0, slot), p[:, 0:P], v(0), start=True, stop=True)
                    nc.tensor.matmul(ps_av(1, slot), p[:, W0:W], v(1), start=True, stop=local)
                    last = nc.tensor.matmul(ps_av(1, slot)[0:Q1, :], p[:, P:W0], v(0), start=False, stop=True,
                                            skip_group_check=local)
                if g == GROUPS - 1:
                    last.then_inc(av_ready, 1)

            def end_a(u, n):
                pe.wait_ge(o_ready, n + 1)
                for t in range(PAIR):
                    last = nc.tensor.transpose(ps_o[:, t * P:(t + 1) * P], o[:, t, :, :].rearrange("p h f -> p (h f)"), m.ident[:, :])
                last.then_inc(otr_ready, 1)

            def end_b(u, n):
                pe.wait_ge(oT_ready, n + 1)
                for t in range(PAIR):
                    last = nc.tensor.matmul(ps_y[:, t * D:(t + 1) * D], oT[:, t * P:(t + 1) * P], w.o[:, :], start=True, stop=True)
                last.then_inc(y_ready, 1)

            def ready(n):
                pe.wait_ge(qT_ready, n + 1)
                pe.wait_ge(kT_ready, n + 1)

            def first():
                pe.wait_ge(m.loaded["a0"], m.total["a0"])
                start_a(0, 0)
                start_b(0, 0)
                start_c(0, 0)
                start_d(0, 0)
                ready(0)
                scores(0, 0, 0)

            def unit(u, n, prev, next):
                for g in range(GROUPS):
                    if g < GROUPS - 1:
                        if prev or g:
                            pe.wait_ge(e_ready, GROUPS * n + g)
                        scores(u, n, g + 1)
                    if next and g == 6:
                        start_d(1 - u, n + 1)
                    if prev and g == 1:
                        pe.wait_ge(o_ready, n)
                    if g:
                        values(u, n, g - 1)
                    elif prev:
                        values(1 - u, n - 1, GROUPS - 1)
                    if next and g == GROUPS - 1:
                        pe.wait_ge(e_ready, GROUPS * n + g)
                        ready(n + 1)
                        scores(1 - u, n + 1, 0)
                    if prev and g == 1:
                        end_a(1 - u, n - 1)
                    if prev and g == 2:
                        end_b(1 - u, n - 1)
                    if next and g in (1, 2, 3):
                        {1: start_a, 2: start_b, 3: start_c}[g](1 - u, n + 1)

            def tail(u, n):
                values(u, n, GROUPS - 1)
                end_a(u, n)
                end_b(u, n)
            threaded(pe, first, unit, tail)

        @block.scalar
        def _(act):
            nc.scalar.preload_act_table_set("natural_log_exp_and_others")

            def start_b(u, n):
                act.wait_ge(rT_ready, n + 1)
                nc.scalar.activation(xT[:, :], ps_a, ACT.Identity, scale=w.norm[:, 0:1]).then_inc(xT_ready, 1)

            def start_c(u, n):
                if not local:
                    act.wait_ge(lat_ready, n + 1)
                    nc.scalar.activation(lat[:, :], ps_a[0:32, :], ACT.Copy).then_inc(latT_ready, 1)

            def start_d(u, n):
                act.wait_ge(ss_ready, n + 1)
                nc.scalar.activation(inv[:, :], ss[:, :], ACT.Ln)
                nc.scalar.drain()
                nc.scalar.activation(inv[:, :], inv[:, :], ACT.Exp, scale=-0.5).then_inc(ssinv_ready, 1)

            def start_e(u, n):
                act.wait_ge(qkT_ready, n + 1)
                for kv in range(KV):
                    last = nc.scalar.activation(qT[:, u, kv, :], ps_a, ACT.Identity, scale=m.head_mask[:, kv:kv + 1])
                last.then_inc(qT_ready, 1)

            def exps(u, n, g):
                act.wait_ge(s_ready, GROUPS * n + g + 1)
                nc.scalar.activation(pT[:, g % 4, :, :], ps_s(g)[:, :, 0:W], ACT.Exp, scale=float(HD) ** -0.5).then_inc(e_ready, 1)

            def end_b(u, n):
                act.wait_ge(otr_ready, n + 1)
                nc.scalar.activation(oT[:, :], ps_o, ACT.Copy).then_inc(oT_ready, 1)

            def first():
                act.wait_ge(m.loaded["a0"], m.total["a0"])
                start_b(0, 0)
                start_c(0, 0)
                start_d(0, 0)
                start_e(0, 0)

            def unit(u, n, prev, next):
                for g in range(GROUPS):
                    if next and g == 6:
                        start_d(1 - u, n + 1)
                    if next and g == 7:
                        start_e(1 - u, n + 1)
                    exps(u, n, g)
                    if prev and g == 2:
                        end_b(1 - u, n - 1)
                    if next and g in (2, 3):
                        {2: start_b, 3: start_c}[g](1 - u, n + 1)
            threaded(act, first, unit, end_b)

        @block.vector
        def _(dve):
            def start_a(u, n):
                norm_begin(nc, rn, lambda t: tile_of(src, n, t), eps=1e-6, rms=True)

            def start_b(u, n):
                norm_end(nc, dve, rn, n, lambda t: tile_of(src, n, t), lambda t: r[:, t, :], rms=True).then_inc(r_ready, 1)

            def start_d(u, n):
                dve.wait_ge(p_ready, n + 1)
                even = ps_b[:, :, 0:QK * HD].rearrange("p t (h i two) -> p t h i two", h=QK, two=2)
                out = rot[:, :, :].rearrange("p t (h i two) -> p t h i two", h=QK, two=2)
                table = lambda v: v.unsqueeze(2).to_broadcast([P, PAIR, QK, HD // 2])
                nc.vector.tensor_copy(va[:, u, :, 0:KV * VW].rearrange("p t (g f) -> p t g f", f=VW)[:, :, :, 0:HD], ps_b[:, :, QK * HD:192].rearrange("p t (g f) -> p t g f", g=KV))
                for half, (a, b, op) in enumerate(((w.cos, w.sin, ALU.subtract), (w.sin, w.cos, ALU.add))):
                    nc.vector.tensor_tensor(tmp[:, 0, :, :, :], even[:, :, :, :, 0], table(a[:, :, :]), ALU.mult)
                    nc.vector.tensor_tensor(tmp[:, 1, :, :, :], even[:, :, :, :, 1], table(b[:, :, :]), ALU.mult)
                    nc.vector.drain()
                    nc.vector.tensor_tensor(out[:, :, :, :, half], tmp[:, 0, :, :, :], tmp[:, 1, :, :, :], op)
                    nc.vector.drain()
                sq = tmp[:, :, :, :, :].rearrange("p a t h i -> p (a t h i)")
                flat = rot[:, :, :].rearrange("p t f -> p (t f)")
                nc.vector.tensor_tensor(sq, flat, flat, ALU.mult)
                nc.vector.drain()
                nc.vector.tensor_reduce(ss[:, :], sq.rearrange("p (h f) -> p h f", f=HD), AX.X, ALU.add)
                nc.vector.drain()
                nc.vector.tensor_scalar(ss[:, :], ss[:, :], 1.0 / HD, 1e-6, ALU.mult, ALU.add).then_inc(ss_ready, 1)

            def start_d2(u, n):
                dve.wait_ge(ssinv_ready, n + 1)
                scale = inv[:, :].rearrange("p (t h) -> p t h", t=PAIR)
                for t in range(PAIR):
                    nc.vector.tensor_tensor(qn[:, t, :].rearrange("p (h f) -> p h f", f=HD), rot[:, t, 0:P].rearrange("p (h f) -> p h f", f=HD),
                                            scale[:, t, 0:HEADS].unsqueeze(2).to_broadcast([P, HEADS, HD]), ALU.mult)
                    last = nc.vector.tensor_tensor(
                        kn[:, t, :].rearrange("p (g j f) -> p g j f", g=KV, j=4),
                        rot[:, t, P:P + KV * HD].rearrange("p (g f) -> p g f", g=KV).unsqueeze(2).to_broadcast([P, KV, 4, HD]),
                        scale[:, t, HEADS:QK].unsqueeze(2).unsqueeze(2).to_broadcast([P, KV, 4, HD]), ALU.mult)
                last.then_inc(qk_ready, 1)

            def start_e(u, n):
                dve.wait_ge(qkT_ready, n + 1)
                for j in range(4):
                    last = nc.vector.tensor_scalar(kT[:, u, j, :], m.psum[:, 5, 0:SEQ], m.copy_mask[:, j:j + 1], None, ALU.mult)
                last.then_inc(kT_ready, 1)

            def mask(u, n, g):
                dve.wait_ge(e_ready, GROUPS * n + g + 1)
                if local:
                    p, k = pT[:, g % 4, :, :], m.window_mask[:, :].unsqueeze(1).to_broadcast([P, 2, W])
                else:
                    p = pT[:, g % 4, :, :].rearrange("p h (b f) -> p h b f", f=P)[:, :, 0:3:2, :]
                    k = m.causal_mask[:, :].unsqueeze(1).unsqueeze(1).to_broadcast([P, 2, 2, P])
                nc.vector.tensor_tensor(p, p, k, ALU.mult).then_inc(masked, 1)

            def end_a(u, n):
                dve.wait_ge(av_ready, n + 1)
                nc.vector.reciprocal(rec[:, :].rearrange("p (t h) -> p t h", t=PAIR), av_heads[:, :, :, HD])
                nc.vector.drain()
                for t in range(PAIR):
                    last = nc.vector.tensor_tensor(o[:, t, :, :].rearrange("p (kv j) f -> p j kv f", kv=KV),
                                                   av_heads[:, t, :, 0:HD].rearrange("p (j kv) f -> p j kv f", kv=KV),
                                                   rec[:, t * HEADS:(t + 1) * HEADS].rearrange("p (j kv) -> p j kv", kv=KV).unsqueeze(3).to_broadcast([P, 4, KV, HD]),
                                                   ALU.mult)
                last.then_inc(o_ready, 1)

            def end_c(u, n):
                dve.wait_ge(y_ready, n + 1)
                nc.vector.tensor_tensor(r2[:, :], ps_y, pair_of(src, n), ALU.add)
                nc.vector.drain()
                if local:
                    residual_begin(nc, m, xn, n, r2[:, :], 1.0)
                else:
                    nc.vector.tensor_copy(pair_of(m.H1, n), r2[:, :])
                nc.vector.drain()

            def first():
                dve.wait_ge(m.loaded["a0"], m.total["a0"])
                nc.vector.memset(va[:, :, :, :], 1.0)
                nc.vector.drain()
                start_a(0, 0)
                start_b(0, 0)
                start_d(0, 0)
                start_d2(0, 0)
                start_e(0, 0)

            def unit(u, n, prev, next):
                for g in range(GROUPS):
                    if next and g in (1, 6, 7):
                        {1: start_b, 6: start_d2, 7: start_e}[g](1 - u, n + 1)
                    mask(u, n, g)
                    if prev and g == 0:
                        end_a(1 - u, n - 1)
                    if next and g == 0:
                        start_a(1 - u, n + 1)
                    if prev and g == 3:
                        end_c(1 - u, n - 1)
                    if prev and g == 4 and local:
                        residual_end(nc, dve, m, xn, n - 1)
                    if next and g == 4:
                        start_d(1 - u, n + 1)

            def tail(u, n):
                end_a(u, n)
                end_c(u, n)
                if local:
                    residual_end(nc, dve, m, xn, n)
            threaded(dve, first, unit, tail)

        @block.gpsimd
        def _(pool):
            def unit(u, n, prev, next):
                if next:
                    norm_power(nc, pool, m, rn, n + 1)
                if prev and local:
                    norm_power(nc, pool, m, xn, n - 1)

            def tail(u, n):
                if local:
                    norm_power(nc, pool, m, xn, n)
            threaded(pool, lambda: norm_power(nc, pool, m, rn, 0), unit, tail)


def latent_and_local_attention(nc, m):
    grouped_attention(nc, m, "global", False)
    grouped_attention(nc, m, "local", True)


def full_attention(nc, m, tag):
    HEADS, HD, GROUPS = 16, 8, 8
    VW = HD + 1
    STREAM = SEQ - (HEADS - 1) * VW
    VPAD = (HEADS - 1) * VW + STREAM
    with ExitStack() as ctx:
        sb = lambda name, shape: ctx.enter_context(nc.sbuf_tensor(f"{tag}_{name}", shape, F32))
        sem = lambda name: signal(nc, ctx, f"{tag}_{name}")
        z = sb("z", [P, PAIR, D])
        xT = sb("xT", [P, SEQ])
        qk = sb("qk", [P, 5, SEQ])
        qk_high, qk_low = (ctx.enter_context(nc.sbuf_tensor(f"{tag}_qk_{k}", [P, 2, 5, SEQ], F32R)) for k in ("high", "low"))
        va = sb("va", [P, 2, PAIR, VPAD])
        nmax = sb("nmax", [P, 2, 4])
        p = sb("p", [P, 2, 4, SEQ])
        pT = sb("pT", [P, 4, 4, SEQ])
        rec = sb("rec", [P, PAIR * HEADS])
        o = sb("o", [P, PAIR, HEADS, HD])
        zn, xn = make_norm(nc, ctx, f"{tag}_zn"), make_norm(nc, ctx, f"{tag}_xn")
        z_ready, zT_ready, xT_ready, qk_ready, qkT_ready, high_ready, parts_ready, v_ready, va_ready = (
            sem(k) for k in ("z_ready", "zT_ready", "xT_ready", "qk_ready", "qkT_ready", "high_ready", "parts_ready", "v_ready", "va_ready"))
        s_ready, nmax_ready, e_ready, tr_ready, pT_ready, av_ready, av_used = (
            sem(k) for k in ("s_ready", "nmax_ready", "e_ready", "tr_ready", "pT_ready", "av_ready", "av_used"))
        ps_s = lambda g: m.psum[:, 2 * (g % 2):2 * (g % 2) + 2, :].rearrange("p b (t f) -> p (b t) f", t=PAIR)
        ps_t = m.psum[:, 4:6, :].rearrange("p b (t f) -> p (b t) f", t=PAIR)
        ps_av = lambda t, slot: m.psum[:, 6, 256 * t + slot * VW:256 * t + slot * VW + STREAM]
        av_heads = m.psum[:, 6, :].rearrange("p (t f) -> p t f", t=PAIR)[:, :, 0:HEADS * VW].rearrange("p t (s f) -> p t s f", f=VW)
        ps_x = m.psum[:, 7, :].rearrange("p (a f) -> p a f", a=2)
        heads_of = lambda g: [(2 * (g % 2) + k, g // 2) for k in range(2)]
        block = ctx.enter_context(nc.Block())

        @block.tensor
        def _(pe):
            def start_a(u, n):
                pe.wait_ge(z_ready, n + 1)
                for t in range(PAIR):
                    last = nc.tensor.transpose(ps_x[:, 0, t * P:(t + 1) * P], z[:, t, :], m.ident[:, :])
                last.then_inc(zT_ready, 1)

            def start_b(u, n):
                pe.wait_ge(xT_ready, n + 1)
                nc.tensor.matmul(ps_x[:, 0, :], m.a3_q[:, :], xT[:, :], start=True, stop=True)
                nc.tensor.matmul(ps_x[:, 1, :], m.a3_k[:, :], xT[:, :], start=True, stop=True).then_inc(qk_ready, 1)

            def start_c(u, n):
                pe.wait_ge(qkT_ready, n + 1)
                for t in range(PAIR):
                    last = nc.tensor.matmul(ps_x[:, 0, t * P:(t + 1) * P], xT[:, t * P:(t + 1) * P], m.a3_v[:, :], start=True, stop=True)
                last.then_inc(v_ready, 1)

            def scores(u, n, g):
                if g == 0:
                    pe.wait_ge(parts_ready, n + 1)
                for k, (rg, j) in enumerate(heads_of(g)):
                    rows = slice(32 * rg, 32 * rg + 32)
                    for t in range(PAIR):
                        last = split_matmul(nc, ps_s(g)[:, 2 * k + t, :], [v[rows, u, 0, t * P:(t + 1) * P] for v in (qk_high, qk_low)],
                                            [v[rows, u, 1 + j, :] for v in (qk_high, qk_low)])
                last.then_inc(s_ready, 1)

            def turn(n, g, prev):
                pe.wait_ge(e_ready, GROUPS * n + g + 1)
                if prev or g:
                    pe.wait_ge(pT_ready, GROUPS * n + g)
                for k in range(2):
                    for kt in range(2):
                        for t in range(PAIR):
                            last = nc.tensor.transpose(ps_t[:, 2 * k + kt, t * P:(t + 1) * P],
                                                       p[:, g % 2, 2 * k + t, kt * P:(kt + 1) * P], m.ident[:, :])
                last.then_inc(tr_ready, 1)

            def values(u, n, g):
                pe.wait_ge(pT_ready, GROUPS * n + g + 1)
                if g == 0:
                    pe.wait_ge(av_used, n + 1)
                    pe.wait_ge(va_ready, n + 1)
                for k, (rg, j) in enumerate(heads_of(g)):
                    h = 4 * rg + j
                    for t in range(PAIR):
                        for kt in range(2):
                            last = nc.tensor.matmul(ps_av(t, 2 * g + k), pT[:, g % 4, 2 * k + kt, t * P:(t + 1) * P],
                                                    va[:, u, kt, h * VW:h * VW + STREAM],
                                                    start=(kt == 0), stop=(kt == 1))
                if g == GROUPS - 1:
                    last.then_inc(av_ready, 1)

            def first():
                pe.wait_ge(m.loaded["a3"], m.total["a3"])
                start_a(0, 0)
                start_b(0, 0)
                start_c(0, 0)
                scores(0, 0, 0)

            def unit(u, n, prev, next):
                for g in range(GROUPS):
                    if g < GROUPS - 1:
                        scores(u, n, g + 1)
                    elif next:
                        scores(1 - u, n + 1, 0)
                    if g > 1:
                        values(u, n, g - 2)
                    elif prev:
                        values(1 - u, n - 1, GROUPS + g - 2)
                    turn(n, g, prev)
                    if next and g in (2, 3, 5):
                        {2: start_a, 3: start_b, 5: start_c}[g](1 - u, n + 1)

            def tail(u, n):
                values(u, n, GROUPS - 2)
                values(u, n, GROUPS - 1)
            threaded(pe, first, unit, tail)

        @block.scalar
        def _(act):
            nc.scalar.preload_act_table(ACT.Exp)

            def start_b(u, n):
                act.wait_ge(zT_ready, n + 1)
                nc.scalar.activation(xT[:, :], ps_x[:, 0, :], ACT.Identity, bias=m.a3_ln_b[:, 0:1], scale=m.a3_ln_g[:, 0:1]).then_inc(xT_ready, 1)

            def exps(n, g):
                act.wait_ge(nmax_ready, GROUPS * n + g + 1)
                for k in range(4):
                    last = nc.scalar.activation(p[:, g % 2, k, :], ps_s(g)[:, k, :], ACT.Exp, bias=nmax[:, g % 2, k:k + 1])
                last.then_inc(e_ready, 1)

            def first():
                act.wait_ge(m.loaded["a3"], m.total["a3"])
                start_b(0, 0)
                exps(0, 0)

            def unit(u, n, prev, next):
                for g in range(GROUPS):
                    if g < GROUPS - 1:
                        exps(n, g + 1)
                    elif next:
                        exps(n + 1, 0)
                    if next and g == 2:
                        start_b(1 - u, n + 1)
            threaded(act, first, unit, lambda u, n: None)

        @block.vector
        def _(dve):
            def start_a(u, n):
                norm_begin(nc, zn, lambda t: tile_of(m.XN, n, t))

            def start_b(u, n):
                norm_end(nc, dve, zn, n, lambda t: tile_of(m.XN, n, t), lambda t: z[:, t, :]).then_inc(z_ready, 1)

            def start_c(u, n):
                dve.wait_ge(qk_ready, n + 1)
                nc.vector.tensor_scalar(qk[:, 0, :], ps_x[:, 0, :], m.a3_bq[:, 0:1], float(HD) ** -0.5, ALU.add, ALU.mult)
                for j in range(4):
                    last = nc.vector.tensor_scalar(qk[:, 1 + j, :], ps_x[:, 1, :], m.a3_bk[:, 0:1], m.copy_mask[:, j:j + 1], ALU.add, ALU.mult)
                last.then_inc(qkT_ready, 1)

            def start_d(u, n):
                dve.wait_ge(v_ready, n + 1)
                nc.vector.tensor_tensor(va[:, u, :, 0:HEADS * VW].rearrange("p t (h f) -> p t h f", f=VW)[:, :, :, 0:HD], ps_x[:, 0, :].rearrange("p (t h f) -> p t h f", t=PAIR, h=HEADS),
                                        m.a3_bv[:, :].rearrange("p (h f) -> p h f", h=HEADS).unsqueeze(1).to_broadcast([P, PAIR, HEADS, HD]),
                                        ALU.add).then_inc(va_ready, 1)

            def maxima(n, g):
                dve.wait_ge(s_ready, GROUPS * n + g + 1)
                nc.vector.tensor_reduce(nmax[:, g % 2, :], ps_s(g), AX.X, ALU.max, negate=True).then_inc(nmax_ready, 1)

            def evacuate(n, g):
                dve.wait_ge(tr_ready, GROUPS * n + g + 1)
                nc.vector.tensor_copy(pT[:, g % 4, :, :], ps_t).then_inc(pT_ready, 1)

            def end(u, n):
                dve.wait_ge(av_ready, n + 1)
                nc.vector.reciprocal(rec[:, :].rearrange("p (t h) -> p t h", t=PAIR), av_heads[:, :, :, HD])
                nc.vector.drain()
                for t in range(PAIR):
                    last = nc.vector.tensor_tensor(o[:, t, :, :].rearrange("p (r j) f -> p j r f", r=4),
                                                   av_heads[:, t, :, 0:HD].rearrange("p (j r) f -> p j r f", r=4),
                                                   rec[:, t * HEADS:(t + 1) * HEADS].rearrange("p (j r) -> p j r", r=4).unsqueeze(3).to_broadcast([P, 4, 4, HD]),
                                                   ALU.mult)
                last.then_inc(av_used, 1)
                nc.vector.drain()
                residual_begin(nc, m, xn, n, o[:, :, :, :].rearrange("p t h f -> p (t h f)"), 1.0)

            def end_b(u, n):
                residual_end(nc, dve, m, xn, n)

            def first():
                dve.sem_inc(av_used, 1)
                dve.wait_ge(m.loaded["a3"], m.total["a3"])
                dve.wait_ge(m.loaded["a0"], m.total["a0"])
                nc.vector.memset(va[:, :, :, :], 1.0)
                nc.vector.drain()
                start_a(0, 0)
                start_b(0, 0)
                start_c(0, 0)
                start_d(0, 0)
                maxima(0, 0)

            def unit(u, n, prev, next):
                for g in range(GROUPS):
                    if g < GROUPS - 1:
                        maxima(n, g + 1)
                    elif next:
                        maxima(n + 1, 0)
                    evacuate(n, g)
                    if prev and g == 1:
                        end(1 - u, n - 1)
                    if prev and g == 2:
                        end_b(1 - u, n - 1)
                    if next and g in (0, 1, 4, 6):
                        {0: start_a, 1: start_b, 4: start_c, 6: start_d}[g](1 - u, n + 1)

            def tail(u, n):
                end(u, n)
                end_b(u, n)
            threaded(dve, first, unit, tail)

        @block.gpsimd
        def _(pool):
            def parts(u, n):
                pool.wait_ge(qkT_ready, n + 1)
                nc.gpsimd.tensor_tensor(qk_high[:, u, :, :], qk[:, :, :], m.ones[:, 0:5].unsqueeze(2).to_broadcast([P, 5, SEQ]),
                                        ALU.mult).then_inc(high_ready, 1)
                pool.wait_ge(high_ready, n + 1)
                nc.gpsimd.tensor_tensor(qk_low[:, u, :, :], qk[:, :, :], qk_high[:, u, :, :].bitcast(F32), ALU.subtract).then_inc(parts_ready, 1)

            def first():
                norm_power(nc, pool, m, zn, 0)
                parts(0, 0)

            def unit(u, n, prev, next):
                if prev:
                    norm_power(nc, pool, m, xn, n - 1)
                if next:
                    norm_power(nc, pool, m, zn, n + 1)
                    parts(1 - u, n + 1)
            threaded(pool, first, unit, lambda u, n: norm_power(nc, pool, m, xn, n))


def relative_attention(nc, m, tag):
    H, WIN = 8, 384
    S4 = 4
    SCALE = float(D) ** -0.5
    rel_k = m.arena[:, 1:3, :].rearrange("p a (h r) -> p (a h) r", h=4)

    with ExitStack() as ctx:
        sb = lambda name, shape: ctx.enter_context(nc.sbuf_tensor(f"{tag}r_{name}", shape, F32))
        sem = lambda name: signal(nc, ctx, f"{tag}r_{name}")
        w_rel, positions = sb("w_rel", [96, 2, 1024]), sb("positions", [96, 2, 512])
        loaded, tr_ready, rel_ready, rel_moved = (sem(k) for k in ("loaded", "tr_ready", "rel_ready", "rel_moved"))
        block = ctx.enter_context(nc.Block())

        @block.sync
        def _(sp):
            sp.dma_start(w_rel[:], m.a2_w_rel).then_inc(loaded, 16)
            sp.dma_start(positions[:], m.a2_positions).then_inc(loaded, 16)

        @block.tensor
        def _(pe):
            for q in range(4):
                for t in range(4):
                    last = nc.tensor.transpose(m.psum[:, q, t * P:(t + 1) * P],
                                               m.XN[:, 2 * q + t // 2, (t % 2) * D:(t % 2 + 1) * D], m.ident[:, :])
                last.then_inc(tr_ready, 1)
            pe.wait_ge(loaded, 32)
            for h in range(H):
                if h >= 4:
                    pe.wait_ge(rel_moved, h - 3)
                for c in range(2):
                    last = nc.tensor.matmul(m.psum[:, 4 + h % 4, :], w_rel[:, c, h * P:(h + 1) * P], positions[:, c, :],
                                            start=(c == 0), stop=(c == 1))
                last.then_inc(rel_ready, 1)

        @block.scalar
        def _(act):
            nc.scalar.preload_act_table(ACT.Exp)
            for h in range(H):
                act.wait_ge(rel_ready, h + 1)
                nc.scalar.activation(rel_k[:, h, :], m.psum[:, 4 + h % 4, :], ACT.Copy).then_inc(rel_moved, 1)

        @block.vector
        def _(dve):
            for q in range(4):
                dve.wait_ge(tr_ready, q + 1)
                nc.vector.tensor_copy(m.XT[:, q * 512:(q + 1) * 512], m.psum[:, q, :])

    with ExitStack() as ctx:
        sb = lambda name, shape: ctx.enter_context(nc.sbuf_tensor(f"{tag}_{name}", shape, F32))
        sem = lambda name: signal(nc, ctx, f"{tag}_{name}")
        xs = sb("xs", [P, 2, SEQ])
        q1, q2, kk = sb("q1", [P, S4, SEQ]), sb("q2", [P, SEQ]), sb("kk", [P, S4, SEQ])
        v = sb("v", [P, H, PAIR, P])
        pos = sb("pos", [P, 2, PAIR, WIN])
        shifted = sb("shifted", [P, S4, PAIR, SEQ])
        p = sb("p", [P, 2, PAIR, SEQ])
        nmax, total = sb("nmax", [P, 2, PAIR]), sb("total", [P, 2, PAIR])
        pT = sb("pT", [P, PAIR, SEQ])
        oT = sb("oT", [P, 2, SEQ])
        acc = sb("acc", [P, PAIR * D])
        xn = make_norm(nc, ctx, f"{tag}_xn")
        scratch = nc.dram_tensor(f"{tag}_scratch", (S4, PAIR, P, WIN), F32).ap()
        names = ("xs_ready", "qk_ready", "q_ready", "v_ready", "v_moved", "pos_ready", "pos_moved", "s_ready", "s_used",
                 "nmax_ready", "e_ready", "p_ready", "tr_ready", "pT_ready", "oT_ready", "o_moved", "y_ready", "y_used")
        (xs_ready, qk_ready, q_ready, v_ready, v_moved, pos_ready, pos_moved, s_ready, s_used,
         nmax_ready, e_ready, p_ready, tr_ready, pT_ready, oT_ready, o_moved, y_ready, y_used) = (sem(k) for k in names)
        pos_written = [sem(f"pos_written{j}") for j in range(2)]
        pos_shifted = [sem(f"pos_shifted{j}") for j in range(S4)]
        ps_qk = m.psum[:, 0, :].rearrange("p (a f) -> p a f", a=2)
        ps_v = m.psum[:, 1, 0:SEQ]
        ps_s = m.psum[:, 2, :].rearrange("p (t f) -> p t f", t=PAIR)
        ps_pos = m.psum[:, 3:5, 0:WIN]
        ps_t = m.psum[:, 5, :].rearrange("p (t f) -> p t f", t=PAIR)
        ps_o = m.psum[:, 6, 0:SEQ]
        ps_y = m.psum[:, 7, 0:PAIR * D]
        block = ctx.enter_context(nc.Block())

        def run(eng, parts):
            def slot(u, n, k, batches):
                for ahead, part in parts:
                    b, h = divmod(k + ahead, H)
                    if b in batches:
                        part((u + b) % 2, n + b, h)

            def first():
                for k in range(-max(ahead for ahead, part in parts), 0):
                    slot(0, 0, k, (0,))

            def batch(u, n, prev, next):
                for k in range(H):
                    slot(u, n, k, (-1,) * prev + (0,) + (1,) * next)

            def tail(u, n):
                for k in range(H, H - min(ahead for ahead, part in parts)):
                    slot(u, n, k, (0,))
            threaded(eng, first, batch, tail)

        @block.tensor
        def _(pe):
            def scores(u, n, h):
                pe.wait_ge(s_used, H * n + h + 1)
                for t in range(PAIR):
                    last = nc.tensor.matmul(ps_s[:, t, :], q1[:, h % S4, t * P:(t + 1) * P], kk[:, h % S4, :], start=True, stop=True)
                last.then_inc(s_ready, 1)

            def positions(u, n, h):
                pe.wait_ge(q_ready, H * n + h + 1)
                pe.wait_ge(pos_moved, H * n + h + 1)
                for t in range(PAIR):
                    last = nc.tensor.matmul(ps_pos[:, t, :], q2[:, t * P:(t + 1) * P],
                                            rel_k[:, h, P - P * t:P - P * t + WIN], start=True, stop=True)
                last.then_inc(pos_ready, 1)

            def transposes(u, n, h):
                pe.wait_ge(p_ready, H * n + h + 1)
                for kt in range(2):
                    for t in range(PAIR):
                        last = nc.tensor.transpose(ps_t[:, kt, t * P:(t + 1) * P], p[:, h % 2, t, kt * P:(kt + 1) * P], m.ident[:, :])
                last.then_inc(tr_ready, 1)

            def projections(u, n, h):
                if h == 0:
                    pe.wait_ge(xs_ready, n + 1)
                for a in range(2):
                    last = nc.tensor.matmul(ps_qk[:, a, :], m.a2_w[:, a, h * P:(h + 1) * P], xs[:, u, :], start=True, stop=True)
                last.then_inc(qk_ready, 1)
                pe.wait_ge(v_moved, H * n + h + 1)
                for t in range(PAIR):
                    last = nc.tensor.matmul(ps_v[:, t * P:(t + 1) * P], xs[:, u, t * P:(t + 1) * P], m.a2_w[:, 2, h * P:(h + 1) * P],
                                            start=True, stop=True)
                last.then_inc(v_ready, 1)

            def values(u, n, h):
                pe.wait_ge(pT_ready, H * n + h + 1)
                pe.wait_ge(o_moved, H * n + h + 1)
                for kt in range(2):
                    last = nc.tensor.matmul(ps_o, v[:, h, kt, :], pT[:, kt, :], start=(kt == 0), stop=(kt == 1))
                last.then_inc(oT_ready, 1)

            def share(u, n, h):
                pe.wait_ge(o_moved, H * n + h + 2)
                pe.wait_ge(y_used, H * n + h + 1)
                for t in range(PAIR):
                    last = nc.tensor.matmul(ps_y[:, t * D:(t + 1) * D], oT[:, h % 2, t * P:(t + 1) * P], m.a2_out[:, h, :], start=True, stop=True)
                last.then_inc(y_ready, 1)
            pe.wait_ge(m.loaded["a2"], m.total["a2"])
            run(pe, [(0, scores), (3, positions), (-1, transposes), (4, projections), (-1, values), (-2, share)])

        @block.scalar
        def _(act):
            nc.scalar.preload_act_table(ACT.Exp)

            def exponentials(u, n, h):
                act.wait_ge(nmax_ready, H * n + h + 1)
                for t in range(PAIR):
                    last = nc.scalar.activation(p[:, h % 2, t, :], p[:, h % 2, t, :], ACT.Exp, bias=nmax[:, h % 2, t:t + 1],
                                                accum_out=total[:, h % 2, t:t + 1])
                last.then_inc(e_ready, 1)

            def positions(u, n, h):
                act.wait_ge(pos_ready, H * n + h + 1)
                act.wait_ge(pos_written[h % 2], 16 * (H // 2 * n + h // 2) + 16)
                nc.scalar.activation(pos[:, h % 2, :, :], ps_pos, ACT.Copy).then_inc(pos_moved, 1)

            def projections(u, n, h):
                act.wait_ge(qk_ready, H * n + h + 1)
                nc.scalar.activation(q1[:, h % S4, :], ps_qk[:, 0, :], ACT.Identity, bias=m.a2_embed_bias[:, h:h + 1], scale=SCALE)
                nc.scalar.activation(q2[:, :], ps_qk[:, 0, :], ACT.Identity, bias=m.a2_pos_bias[:, h:h + 1], scale=SCALE)
                nc.scalar.activation(kk[:, h % S4, :], ps_qk[:, 1, :], ACT.Copy).then_inc(q_ready, 1)

            def values(u, n, h):
                act.wait_ge(oT_ready, H * n + h + 1)
                nc.scalar.activation(oT[:, h % 2, :], ps_o, ACT.Copy).then_inc(o_moved, 1)
            run(act, [(0, exponentials), (3, positions), (4, projections), (-1, values)])

        @block.vector
        def _(dve):
            def maxima(u, n, h):
                dve.wait_ge(s_ready, H * n + h + 1)
                dve.wait_ge(pos_shifted[h % S4], 16 * (H // S4 * n + h // S4) + 16)
                nc.vector.tensor_tensor(p[:, h % 2, :, :], ps_s, shifted[:, h % S4, :, :], ALU.add).then_inc(s_used, 1)
                nc.vector.drain()
                nc.vector.tensor_reduce(nmax[:, h % 2, :], p[:, h % 2, :, :], AX.X, ALU.max, negate=True).then_inc(nmax_ready, 1)

            def transposes(u, n, h):
                dve.wait_ge(tr_ready, H * n + h + 1)
                nc.vector.tensor_copy(pT[:, :, :], ps_t).then_inc(pT_ready, 1)

            def division(u, n, h):
                dve.wait_ge(e_ready, H * n + h + 1)
                nc.vector.reciprocal(total[:, h % 2, :], total[:, h % 2, :])
                nc.vector.drain()
                for t in range(PAIR):
                    last = nc.vector.tensor_scalar(p[:, h % 2, t, :], p[:, h % 2, t, :], total[:, h % 2, t:t + 1], None, ALU.mult)
                last.then_inc(p_ready, 1)

            def projections(u, n, h):
                dve.wait_ge(v_ready, H * n + h + 1)
                nc.vector.tensor_copy(v[:, h, :, :].rearrange("p t f -> p (t f)"), ps_v).then_inc(v_moved, 1)

            def share(u, n, h):
                nc.vector.drain()
                dve.wait_ge(y_ready, H * n + h + 1)
                before = m.a2_b_out[:, :] if h == 0 else acc[:, :]
                nc.vector.tensor_tensor(acc[:, :], ps_y, before, ALU.add).then_inc(y_used, 1)
                if h == H - 1:
                    nc.vector.drain()
                    residual_begin(nc, m, xn, n, acc[:, :], 1.0)

            def end(u, n, h):
                if h == H - 1:
                    residual_end(nc, dve, m, xn, n)
            dve.sem_inc(v_moved, 1)
            dve.sem_inc(pos_moved, 1)
            dve.sem_inc(s_used, 1)
            dve.sem_inc(o_moved, 1)
            dve.sem_inc(y_used, 1)
            for j in range(2):
                dve.sem_inc(pos_written[j], 16)
            run(dve, [(0, maxima), (-1, transposes), (0, division), (4, projections), (-3, end), (-2, share)])

        @block.gpsimd
        def _(pool):
            def begin(u, n, h):
                if h == 0:
                    nc.gpsimd.tensor_copy(xs[:, u, :], tokens_T(m, n)).then_inc(xs_ready, 1)

            def end(u, n, h):
                if h == H - 1:
                    norm_power(nc, pool, m, xn, n)
            run(pool, [(-2, end), (5, begin)])

        @block.sync
        def _(sp):
            def write(u, n, h):
                sp.wait_ge(pos_moved, H * n + h + 2)
                sp.dma_start(scratch[h % S4].rearrange("t q r -> q t r"), pos[:, h % 2, :, :]).then_inc(pos_written[h % 2], 16)

            def read(u, n, h):
                sp.wait_ge(pos_written[h % 2], 16 * (H // 2 * n + h // 2) + 32)
                rows = scratch[h % S4].rearrange("t q r -> t (q r)")[:, P - 1:P - 1 + P * (WIN - 1)]
                skewed_rows = rows.rearrange("t (q r) -> q t r", r=WIN - 1)[:, :, 0:SEQ]
                sp.dma_start(shifted[:, h % S4, :, :], skewed_rows).then_inc(pos_shifted[h % S4], 16)
            run(sp, [(3, write), (2, read)])


def build(nc, h, out):
    with ExitStack() as ctx:
        sb = lambda name, shape: ctx.enter_context(nc.sbuf_tensor(name, shape, F32))
        m = Record()
        m.loaded, m.total = {}, {}
        m.psum = ctx.enter_context(nc.psum_tensor("psum", [P, 8, 512], F32))
        m.X = sb("X", [P, NB, PAIR * D])
        m.XN = sb("XN", [P, NB, PAIR * D])
        loads = {}

        def load(group, name, dst, src):
            loads.setdefault(group, []).append((dst, src))

        def weight(group, name, shape):
            buf = sb(name, shape)
            load(group, name, buf[:], h[name])
            return buf
        load("x", "x", m.X[:].rearrange("p n (t d) -> p (n t) d", t=PAIR), h["x"].rearrange("(t p) d -> p t d", p=P))
        m.ident = weight("const", "ident", [P, P])
        m.ones = weight("const", "ones", [P, P])
        m.neg_half = weight("const", "neg_half", [P, 80])
        m.f0_w1 = weight("f0", "f0_w1", [P, 512])
        m.f0_w2 = weight("f0", "f0_w2", [P, 512])
        m.f0_b1 = sb("f0_b1", [P, PAIR, 512])
        for t in range(PAIR):
            load("f0", "f0_b1", m.f0_b1[:, t, :], h["f0_b1"].partition_broadcast(P))
        m.f0_b2 = sb("f0_b2", [P, PAIR * D])
        for t in range(PAIR):
            load("f0", "f0_b2", m.f0_b2[:, t * D:(t + 1) * D], h["f0_b2"].partition_broadcast(P))
        m.f0_ln1_g = weight("f0", "f0_ln1_g", [P, 1])
        m.f0_ln1_b = weight("f0", "f0_ln1_b", [P, 1])
        m.f0_ln2_g = weight("f0", "f0_ln2_g", [P, 4])
        m.f0_ln2_b = weight("f0", "f0_ln2_b", [P, 4])
        m.m1_gate = weight("m1", "m1_gate", [P, 9])
        m.m1_down = weight("m1", "m1_down", [88, 10, 2, D])
        m.m2_gate = weight("m2", "m2_gate", [P, 8])
        m.m2_gate_b = sb("m2_gate_b", [P, 8])
        load("m2", "m2_gate_b", m.m2_gate_b[:, :], h["m2_gate_b"].partition_broadcast(P))
        m.m2_b1 = weight("m2", "m2_b1", [P, 32])
        m.m2_w2 = weight("m2", "m2_w2", [P, 8, 4, D])
        m.m2_b2 = sb("m2_b2", [P, D])
        for t in range(NT):
            load("m2", "m2_b2", m.m2_b2[8 * t:8 * t + 8, :], h["m2_b2"])
        m.m3_gate = weight("m3", "m3_gate", [P, 8])
        m.m3_gate_b = sb("m3_gate_b", [P, 8])
        load("m3", "m3_gate_b", m.m3_gate_b[:, :], h["m3_gate_b"].partition_broadcast(P))
        m.m3_up = weight("m3", "m3_up", [P, 512])
        m.m3_shared_out = weight("m3", "m3_shared_out", [P, D])
        m.m3_w2 = weight("m3", "m3_w2", [P, 8 * D])
        m.countdown = weight("m1", "countdown", [P, 8])
        m.tile_mask = weight("m2", "tile_mask", [P, NT])
        m.gates = sb("gates", [P, NT, 9])
        m.arena = sb("arena", [P, 4, NB * SEQ])
        m.XT = m.arena[:, 0, :]
        m.bias2_of_tile = m.arena[:, 2, :]
        m.a1_in_g = weight("a1", "a1_in_g", [P, 1])
        m.a1_in_b = weight("a1", "a1_in_b", [P, 1])
        m.a1_in = weight("a1", "a1_in", [P, 384])
        m.a1_out = weight("a1", "a1_out", [96, 2, D])
        m.a1_alog = weight("a1", "a1_alog", [96, 16])
        m.a1_b = weight("a1", "a1_b", [96, 16])
        m.a1_c = weight("a1", "a1_c", [96, 16])
        for part in ("out_g", "out_b"):
            buf = sb("a1_" + part, [P, D])
            load("a1", "a1_" + part, buf[:, :], h["a1_" + part].partition_broadcast(P))
            if part == "out_g":
                m.a1_out_g = buf
            else:
                m.a1_out_b = buf
        m.H1 = m.arena[:, 3, :].rearrange("p (n f) -> p n f", n=NB)
        m.a0g, m.a0l = Record(), Record()
        m.a0g.norm, m.a0l.norm = weight("a0", "a0g_norm", [P, 1]), weight("a0", "a0l_norm", [P, 1])
        m.a0g.q = weight("a0", "a0g_q", [P, D])
        m.a0g.down = weight("a0", "a0g_down", [P, 32])
        m.a0g.kv = weight("a0", "a0g_kv", [32, 64])
        m.a0l.qkv = weight("a0", "a0l_qkv", [P, 192])
        m.a0g.o, m.a0l.o = weight("a0", "a0g_o", [P, D]), weight("a0", "a0l_o", [P, D])
        m.a0g.cos, m.a0g.sin = weight("a0", "a0g_cos", [P, PAIR, 4]), weight("a0", "a0g_sin", [P, PAIR, 4])
        m.a0l.cos, m.a0l.sin = weight("a0", "a0l_cos", [P, PAIR, 4]), weight("a0", "a0l_sin", [P, PAIR, 4])
        m.copy_mask = weight("a0", "copy_mask", [P, 4])
        m.head_mask = weight("a0", "head_mask", [P, 4])
        m.causal_mask = weight("a0", "causal_mask", [P, P])
        m.window_mask = weight("a0", "window_mask", [P, 288])
        m.a3_ln_g, m.a3_ln_b = weight("a3", "a3_ln_g", [P, 1]), weight("a3", "a3_ln_b", [P, 1])
        m.a3_q, m.a3_k, m.a3_v = (weight("a3", "a3_" + k, [P, D]) for k in "qkv")
        m.a3_bq, m.a3_bk = weight("a3", "a3_bq", [P, 1]), weight("a3", "a3_bk", [P, 1])
        m.a3_bv = sb("a3_bv", [P, D])
        load("a3", "a3_bv", m.a3_bv[:, :], h["a3_bv"].partition_broadcast(P))
        m.a2_w = weight("a2", "a2_w", [P, 3, 8 * P])
        m.a2_out = weight("a2", "a2_out", [P, 8, D])
        m.a2_embed_bias, m.a2_pos_bias = weight("a2", "a2_embed_bias", [P, 8]), weight("a2", "a2_pos_bias", [P, 8])
        m.a2_b_out = sb("a2_b_out", [P, PAIR * D])
        for t in range(PAIR):
            load("a2", "a2_b_out", m.a2_b_out[:, t * D:(t + 1) * D], h["a2_b_out"].partition_broadcast(P))
        m.a2_w_rel, m.a2_positions = h["a2_w_rel"], h["a2_positions"]
        raw_up = m.arena[:, :, :].rearrange("p a f -> p (a f)")[:, 0:10 * 352].rearrange("p (e f) -> p e f", e=10)
        raw_w1 = m.arena[:, :, :].rearrange("p a f -> p (a f)")[:, 0:8 * 512].rearrange("p (e f) -> p e f", e=8)
        load("m1_raw", "m1_up", raw_up, h["m1_up"])
        load("m2_raw", "m2_w1", raw_w1, h["m2_w1"])
        for group in loads:
            m.loaded[group] = ctx.enter_context(nc.semaphore("loaded_" + group))
            m.total[group] = 16 * len(loads[group])
        stored = ctx.enter_context(nc.semaphore("stored"))

        issued = []

        def issue(sp, groups):
            for group in groups:
                issued.append(group)
                for dst, src in loads[group]:
                    sp.dma_start(dst, src).then_inc(m.loaded[group], 16)
        early = ("x", "const", "f0")
        m.issue_early = lambda sp: issue(sp, early)
        m.issue_late = lambda sp: issue(sp, [group for group in loads if group not in early + ("m1_raw", "m2_raw")])
        issue_m1 = lambda sp: issue(sp, ["m1_raw"])
        issue_m2 = lambda sp: issue(sp, ["m2_raw"])
        input_norm(nc, m)
        clear_signals(nc)
        stages = [
            lambda: (ternary_weights(nc, m), ffn_ternary(nc, m, "f0a", m.issue_late)),
            lambda: latent_and_local_attention(nc, m),
            lambda: ffn_ternary(nc, m, "f0b", issue_m1),
            lambda: moe_gated(nc, m, "m1a"),
            lambda: state_space(nc, m, "a1"),
            lambda: moe_gated(nc, m, "m1b", issue_m2),
            lambda: moe_gelu(nc, m, "m2a"),
            lambda: relative_attention(nc, m, "a2"),
            lambda: moe_gelu(nc, m, "m2b"),
            lambda: moe_common(nc, m, "m3a"),
            lambda: full_attention(nc, m, "a3"),
            lambda: moe_common(nc, m, "m3b"),
        ]
        GATED, GELU = (3, 5), (6, 8)
        split = ctx.enter_context(ExitStack())
        for i, stage in enumerate(stages):
            if i == GATED[0]:
                m.m1_up = split_weights(nc, m, split, "m1_raw", raw_up)
            if i == GELU[0]:
                split.close()
                m.m2_w1 = split_weights(nc, m, split, "m2_raw", raw_w1)
            stage()
            clear_signals(nc)
            if i == GELU[1]:
                split.close()
        with nc.Block() as block:
            @block.sync
            def _(sp):
                for group in issued:
                    sp.wait_ge(m.loaded[group], m.total[group])
                sp.dma_start(out.rearrange("(t p) d -> p t d", p=P),
                             m.X[:].rearrange("p n (t d) -> p (n t) d", t=PAIR)).then_inc(stored, 16)
                sp.wait_ge(stored, 16)


def position_features(length, size):
    f = np.float32
    n = size // 6
    distances = np.arange(-length + 1, length, dtype=f)
    far = np.abs(distances)[:, None]
    half_life = f(2.0) ** np.linspace(3.0, math.log(length) / math.log(2.0), n, dtype=f)
    decaying = np.exp(f(-math.log(2.0)) / half_life[None] * far)
    central = (f(2.0) ** np.arange(1, n + 1, dtype=f) - f(1.0) > far).astype(f)
    stddev = length / (2.0 * n)
    mean = np.linspace(length / n, float(length), n, dtype=f)[None]
    shape = (mean / f(stddev)) ** f(2.0)
    rate = mean / f(stddev ** 2)
    log_far = np.log(np.where(far > 0, far, f(1.0)))
    log_unnormed = np.where(far > 0, (shape - f(1.0)) * log_far, f(-np.inf)) - rate * far
    log_norm = np.array([[math.lgamma(float(v)) for v in shape[0]]], dtype=f) - shape * np.log(rate)
    gamma = np.exp(log_unnormed - log_norm).astype(f) + f(1e-8)
    gamma = gamma / np.max(gamma, axis=-1, keepdims=True)
    out = np.concatenate([decaying, central, gamma], -1)
    return np.concatenate([out, np.sign(distances)[:, None] * out], -1).astype(f)


def kernel(**a):
    import concourse.bacc as bacc
    from concourse.bass_utils import run_bass_kernel_spmd as run
    c = lambda v: np.ascontiguousarray(v)
    a = {k: np.asarray(v) for k, v in a.items()}
    arrays = {
        "x": c(a["L0_attn_hidden"].reshape(NB * SEQ, D)),
        "ident": np.eye(P, dtype=np.float32),
        "ones": np.ones((P, P), np.float32),
        "neg_half": np.full((P, 80), -0.5, np.float32),
        "f0_w1": c(a["L0_ffn_w1"].T),
        "f0_w2": c(a["L0_ffn_w2"].reshape(D, 4, P).transpose(2, 1, 0).reshape(P, 512)),
        "f0_b1": a["L0_ffn_b1"], "f0_b2": a["L0_ffn_b2"],
        "f0_ln1_g": c(a["L0_ffn_ln1_g"].reshape(P, 1)), "f0_ln1_b": c(a["L0_ffn_ln1_b"].reshape(P, 1)),
        "f0_ln2_g": c(a["L0_ffn_ln2_g"].reshape(4, P).T), "f0_ln2_b": c(a["L0_ffn_ln2_b"].reshape(4, P).T),
    }
    eu = a["L1_ffn_experts_gate_up"].transpose(2, 0, 1)
    sg, su = (a[f"L1_ffn_shared_{k}_w"].reshape(2, 176, D).transpose(2, 0, 1) for k in ("gate", "up"))
    arrays["m1_up"] = c(np.concatenate([eu, np.concatenate([sg, su], 2)], 1))
    ed = a["L1_ffn_experts_down"].reshape(8, D, 2, 88).transpose(3, 0, 2, 1)
    sd = a["L1_ffn_shared_down_w"].reshape(D, 2, 2, 88).transpose(3, 1, 2, 0)
    arrays["m1_down"] = c(np.concatenate([ed, sd], 1))
    arrays["m1_gate"] = c(np.concatenate([a["L1_ffn_gate_w"], a["L1_ffn_shared_expert_gate_w"]], 0).T)
    arrays["m2_gate"], arrays["m2_gate_b"] = a["L2_ffn_Wg"], a["L2_ffn_bg"]
    arrays["m2_b1"] = c(a["L2_ffn_b1"].reshape(32, P).T)
    arrays["m2_w1"] = c(a["L2_ffn_W1"].transpose(1, 0, 2))
    arrays["m2_w2"] = c(a["L2_ffn_W2"].reshape(8, 4, P, D).transpose(2, 0, 1, 3))
    arrays["m2_b2"] = a["L2_ffn_b2"]
    arrays["m3_gate"], arrays["m3_gate_b"] = a["L3_ffn_w_gate"], a["L3_ffn_gate_bias"]
    arrays["a1_in_g"], arrays["a1_in_b"] = a["L1_attn_ln_in_g"].reshape(P, 1), a["L1_attn_ln_in_b"].reshape(P, 1)
    arrays["a1_in"] = c(a["L1_attn_W_in"].T)
    arrays["a1_out"] = c(a["L1_attn_W_out"].T.reshape(2, 96, D).transpose(1, 0, 2))
    for k, v in (("alog", "A_log"), ("b", "B"), ("c", "C")):
        arrays["a1_" + k] = c(a["L1_attn_" + v].reshape(2, 96, 8).transpose(1, 0, 2).reshape(96, 16))
    arrays["a1_out_g"], arrays["a1_out_b"] = a["L1_attn_ln_out_g"], a["L1_attn_ln_out_b"]
    arrays["a0g_norm"], arrays["a0l_norm"] = a["L0_attn_norm1_w"].reshape(P, 1), a["L0_attn_norm2_w"].reshape(P, 1)
    arrays["a0g_q"], arrays["a0g_down"] = a["L0_attn_g_wq"], a["L0_attn_g_kv_down"]
    arrays["a0g_kv"] = c(np.concatenate([a["L0_attn_g_k_up"], a["L0_attn_g_v_up"]], 1))
    arrays["a0l_qkv"] = c(np.concatenate([a["L0_attn_l_wq"], a["L0_attn_l_wk"], a["L0_attn_l_wv"]], 1))
    arrays["a0g_o"], arrays["a0l_o"] = a["L0_attn_g_wo"], a["L0_attn_l_wo"]
    for k, base in (("g", 1000000.0), ("l", 10000.0)):
        inv_freq = (np.float32(1.0) / np.float32(base) ** (np.arange(0, 8, 2, dtype=np.float32) / np.float32(8))).astype(np.float32)
        angle = np.arange(SEQ, dtype=np.float32)[:, None] * inv_freq[None]
        for name, fn in (("cos", np.cos), ("sin", np.sin)):
            arrays[f"a0{k}_{name}"] = c(fn(angle).astype(np.float32).reshape(PAIR, P, 4).transpose(1, 0, 2))
    row = np.arange(P)
    arrays["head_mask"] = (row[:, None] // 32 == np.arange(4)[None]).astype(np.float32)
    arrays["copy_mask"] = (row[:, None] % 32 // 8 == np.arange(4)[None]).astype(np.float32)
    arrays["causal_mask"] = (row[:, None] <= row[None]).astype(np.float32)
    gap = np.arange(160)[None] - row[:, None]
    window = ((gap >= 0) & (gap < 32)).astype(np.float32)
    arrays["window_mask"] = c(np.concatenate([window, window[:, :P]], 1))
    arrays["a3_ln_g"], arrays["a3_ln_b"] = a["L3_attn_ln_g"].reshape(P, 1), a["L3_attn_ln_b"].reshape(P, 1)
    arrays["a3_q"], arrays["a3_k"], arrays["a3_v"] = (a["L3_attn_W" + k] for k in "qkv")
    arrays["a3_bq"], arrays["a3_bk"], arrays["a3_bv"] = a["L3_attn_bq"].reshape(P, 1), a["L3_attn_bk"].reshape(P, 1), a["L3_attn_bv"]
    arrays["a2_w"] = c(np.stack([a["L2_attn_w_qs"], a["L2_attn_w_ks"], a["L2_attn_w_vs"]], 1))
    arrays["a2_out"] = c(a["L2_attn_w_out"].reshape(8, P, D).transpose(1, 0, 2))
    arrays["a2_embed_bias"], arrays["a2_pos_bias"] = c(a["L2_attn_rel_embed_bias"].reshape(8, P).T), c(a["L2_attn_rel_pos_bias"].reshape(8, P).T)
    arrays["a2_b_out"] = a["L2_attn_b_out"]
    arrays["a2_w_rel"] = c(a["L2_attn_w_rel_pos_k"].reshape(2, 96, 1024).transpose(1, 0, 2))
    arrays["a2_positions"] = c(np.pad(position_features(SEQ, 192), ((0, 1), (0, 0))).T.reshape(2, 96, 512).transpose(1, 0, 2))
    w1, ws = a["L3_ffn_w1_shared"], a["L3_ffn_w_shared_in"]
    arrays["m3_up"] = c(np.concatenate([w1[:, :P], ws[:, :P], w1[:, P:], ws[:, P:]], 1))
    arrays["m3_shared_out"] = a["L3_ffn_w_shared_out"]
    arrays["m3_w2"] = c(a["L3_ffn_w2"].transpose(1, 0, 2).reshape(P, 8 * D))
    arrays["countdown"] = np.tile(np.arange(8, 0, -1, dtype=np.float32), (P, 1))
    arrays["tile_mask"] = np.repeat(np.eye(NT, dtype=np.float32), 8, 0)
    nc = bacc.Bacc("TRN2", target_bir_lowering=False, num_devices=1)
    ins, h = {}, {}
    for name, v in arrays.items():
        ins["in_" + name] = v
        h[name] = nc.dram_tensor("in_" + name, v.shape, F32, kind="ExternalInput").ap()
    out = nc.dram_tensor("out", (NB * SEQ, D), F32, kind="ExternalOutput").ap()
    build(nc, h, out)
    r = run(nc, [ins], core_ids=[0])
    return np.asarray(r.results[0]["out"]).reshape(NB, SEQ, D)
```
